# Optimizing a Trainium2 kernel written in Bass

```python
import numpy as np
import jax
import jax.numpy as jnp

def _softmax(x, axis=-1):
    return jax.nn.softmax(x, axis=axis)

def _gelu(x):
    return jax.nn.gelu(x, approximate=True)

def _silu(x):
    return jax.nn.silu(x)

def _sigmoid(x):
    return jax.nn.sigmoid(x)

def _layernorm(x, axis=-1, eps=1e-05):
    m = jnp.mean(x, axis=axis, keepdims=True)
    v = jnp.var(x, axis=axis, keepdims=True)
    return (x - m) / jnp.sqrt(v + eps)

def _scatter_add(tgt, idx, src, axis=0):
    return tgt.at[idx].add(src)

def _segment_sum(src, seg, n):
    return jax.ops.segment_sum(src, seg, n)
kernel_name = 'mk_gnn_preln_d2_gnn_r64_e14530'

def setup_inputs(seed: int=0):
    np.random.seed(seed)
    _w = jnp.asarray

    def _rec_inputs():
        import jax
        import jax.numpy as jnp
        _gk = jax.random.key(seed)
        x = -0.0005121 + 1.001 * jax.random.normal(jax.random.fold_in(_gk, 1), (50000, 160), jnp.float32)
        src = jax.random.randint(jax.random.fold_in(_gk, 2), (25000,), 0, 50000, jnp.int32)
        dst = jax.random.randint(jax.random.fold_in(_gk, 3), (25000,), 0, 50000, jnp.int32)
        _o = jnp.argsort(dst, stable=True)
        src = src[_o]
        dst = dst[_o]
        edge_attr_4 = 0.000735704 + 1.0001 * jax.random.normal(jax.random.fold_in(_gk, 12), (25000, 4), jnp.float32)
        edge_attr_64 = 0.000127647 + 1.00004 * jax.random.normal(jax.random.fold_in(_gk, 13), (25000, 64), jnp.float32)
        node_vec1 = -0.00719938 + 0.999885 * jax.random.normal(jax.random.fold_in(_gk, 15), (50000, 1), jnp.float32)
        return (x, src, dst, edge_attr_4, edge_attr_64, node_vec1)
    x, src, dst, edge_attr_4, edge_attr_64, node_vec1 = _rec_inputs()

    def _L0_gnn_setup():
        import jax, jax.numpy as jnp
        import numpy as np
        N = 20000
        E = 10000
        INV_SQRT3 = 0.5773502691896258
        INV8 = 0.125
        INV_SQRT32 = 0.17677669529663687
        INV64 = 0.015625
        INV32 = 0.03125
        INV_SQRT2048 = 0.022097086912079608
        key = jax.random.key(seed)
        ks = jax.random.split(key, 16)
        f32 = jnp.float32
        return {'node_features': jax.random.normal(ks[0], (N, 160), f32), 'edge_index': jax.random.randint(ks[1], (2, E), 0, N), 'edge_attr_tensor': jax.random.normal(ks[2], (E, 4), f32), 'node_attr_scalar_raw': jax.random.normal(ks[3], (N, 1), f32), 'Wm_ss': jax.random.normal(ks[4], (64, 64), f32), 'Wm_vv': jax.random.normal(ks[5], (32, 64), f32), 'Wm_sv': jax.random.normal(ks[6], (64, 32), f32), 'Wm_vs': jax.random.normal(ks[7], (32, 32), f32), 'Lm_s': jax.random.normal(ks[8], (64, 64), f32), 'Lm_v': jax.random.normal(ks[9], (32, 32), f32), 'Wu_ss': jax.random.normal(ks[10], (64, 64, 64), f32), 'Wu_vv': jax.random.normal(ks[11], (32, 32, 64), f32), 'Wu_sv': jax.random.normal(ks[12], (64, 32, 32), f32), 'Wu_vs': jax.random.normal(ks[13], (32, 64, 32), f32), 'Lu_s': jax.random.normal(ks[14], (64, 64), f32), 'Lu_v': jax.random.normal(ks[15], (32, 32), f32)}
    _L0_gnn_all = _L0_gnn_setup()
    _L0_gnn_in = {k: v for k, v in _L0_gnn_all.items() if k in ('Wm_ss', 'Wm_vv', 'Wm_sv', 'Wm_vs', 'Lm_s', 'Lm_v', 'Wu_ss', 'Wu_vv', 'Wu_sv', 'Wu_vs', 'Lu_s', 'Lu_v')}
    del _L0_gnn_all

    def _L1_gnn_setup():
        import jax, jax.numpy as jnp
        import numpy as np
        N, E = (625, 10000)
        S_IN, V_IN = (64, 32)
        S_MID, V_MID = (96, 128)
        S_OUT, V_OUT = (96, 32)
        R = 64
        FC_HID = 64
        W_NUMEL = 64 + 64 + 32 + 32 + 32
        NUM_NEIGHBORS = 16.0

        def _inv(d):
            return 1.0 / jnp.sqrt(jnp.float32(d))

        def _forward(node_features, node_attr, edge_attr, edge_scalars, lin1_ws, lin1_wv, fc_w1, fc_w2, sc_ws, sc_wv, lin2_ws, lin2_wv, edge_src, edge_dst):
            n = node_features.shape[0]
            s = node_features[:, :S_IN]
            v = node_features[:, S_IN:].reshape(n, V_IN, 3)
            a = node_attr
            sc_s = s @ sc_ws * a * _inv(S_IN)
            sc_v = jnp.einsum('nci,cd->ndi', v, sc_wv) * a[:, :, None] * _inv(V_IN)
            h_s = s @ lin1_ws * a * _inv(S_IN)
            h_v = jnp.einsum('nci,cd->ndi', v, lin1_wv) * a[:, :, None] * _inv(V_IN)
            hid = jax.nn.silu(edge_scalars @ fc_w1 * _inv(R))
            w = hid @ fc_w2 * _inv(FC_HID)
            w1, w2, w3, w4, w5 = jnp.split(w, [64, 128, 160, 192], axis=-1)
            es = h_s[edge_src]
            ev = h_v[edge_src]
            e0 = edge_attr[:, :1]
            e1 = edge_attr[:, 1:4]
            m_s1 = w1 * es * e0
            m_s2 = w4 * jnp.einsum('eci,ei->ec', ev, e1) * _inv(3)
            m_v1 = (w2 * es)[:, :, None] * e1[:, None, :]
            m_v2 = w3[:, :, None] * ev * e0[:, :, None]
            m_v3 = w5[:, :, None] * jnp.cross(ev, e1[:, None, :]) * _inv(2)
            mid_s = jnp.concatenate([m_s1, m_s2], axis=-1)
            mid_v = jnp.concatenate([m_v1, m_v2, m_v3], axis=1)
            inv_nn = 1.0 / jnp.sqrt(jnp.float32(NUM_NEIGHBORS))
            agg_s = jax.ops.segment_sum(mid_s, edge_dst, num_segments=n) * inv_nn
            agg_v = jax.ops.segment_sum(mid_v, edge_dst, num_segments=n) * inv_nn
            o_s = agg_s @ lin2_ws * a * _inv(S_MID)
            o_v = jnp.einsum('nci,cd->ndi', agg_v, lin2_wv) * a[:, :, None] * _inv(V_MID)
            pre_s = sc_s + o_s
            pre_v = sc_v + o_v
            scalars = jax.nn.silu(pre_s[:, :64])
            gates = jax.nn.sigmoid(pre_s[:, 64:96])
            gated = gates[:, :, None] * pre_v
            return jnp.concatenate([scalars, gated.reshape(n, 3 * V_OUT)], axis=-1)
        key = jax.random.key(seed)
        ks = jax.random.split(key, 13)
        return {'node_features': jax.random.normal(ks[0], (N, S_IN + 3 * V_IN), jnp.float32), 'node_attr': jnp.ones((N, 1), jnp.float32), 'edge_src': jax.random.randint(ks[1], (E,), 0, N), 'edge_dst': jax.random.randint(ks[2], (E,), 0, N), 'edge_attr': jax.random.normal(ks[3], (E, 4), jnp.float32), 'edge_scalars': jax.random.normal(ks[4], (E, R), jnp.float32), 'lin1_ws': jax.random.normal(ks[5], (S_IN, S_IN), jnp.float32), 'lin1_wv': jax.random.normal(ks[6], (V_IN, V_IN), jnp.float32), 'fc_w1': jax.random.normal(ks[7], (R, FC_HID), jnp.float32), 'fc_w2': jax.random.normal(ks[8], (FC_HID, W_NUMEL), jnp.float32), 'sc_ws': jax.random.normal(ks[9], (S_IN, S_OUT), jnp.float32), 'sc_wv': jax.random.normal(ks[10], (V_IN, V_OUT), jnp.float32), 'lin2_ws': jax.random.normal(ks[11], (S_MID, S_OUT), jnp.float32), 'lin2_wv': jax.random.normal(ks[12], (V_MID, V_OUT), jnp.float32)}
    _L1_gnn_all = _L1_gnn_setup()
    _L1_gnn_in = {k: v for k, v in _L1_gnn_all.items() if k in ('lin1_ws', 'lin1_wv', 'fc_w1', 'fc_w2', 'sc_ws', 'sc_wv', 'lin2_ws', 'lin2_wv')}
    del _L1_gnn_all
    return {'x': x, 'src': src, 'dst': dst, 'edge_attr_4': edge_attr_4, 'edge_attr_64': edge_attr_64, 'node_vec1': node_vec1, 'L0_gnn_Wm_ss': _L0_gnn_in['Wm_ss'], 'L0_gnn_Wm_vv': _L0_gnn_in['Wm_vv'], 'L0_gnn_Wm_sv': _L0_gnn_in['Wm_sv'], 'L0_gnn_Wm_vs': _L0_gnn_in['Wm_vs'], 'L0_gnn_Lm_s': _L0_gnn_in['Lm_s'], 'L0_gnn_Lm_v': _L0_gnn_in['Lm_v'], 'L0_gnn_Wu_ss': _L0_gnn_in['Wu_ss'], 'L0_gnn_Wu_vv': _L0_gnn_in['Wu_vv'], 'L0_gnn_Wu_sv': _L0_gnn_in['Wu_sv'], 'L0_gnn_Wu_vs': _L0_gnn_in['Wu_vs'], 'L0_gnn_Lu_s': _L0_gnn_in['Lu_s'], 'L0_gnn_Lu_v': _L0_gnn_in['Lu_v'], 'L1_gnn_lin1_ws': _L1_gnn_in['lin1_ws'], 'L1_gnn_lin1_wv': _L1_gnn_in['lin1_wv'], 'L1_gnn_fc_w1': _L1_gnn_in['fc_w1'], 'L1_gnn_fc_w2': _L1_gnn_in['fc_w2'], 'L1_gnn_sc_ws': _L1_gnn_in['sc_ws'], 'L1_gnn_sc_wv': _L1_gnn_in['sc_wv'], 'L1_gnn_lin2_ws': _L1_gnn_in['lin2_ws'], 'L1_gnn_lin2_wv': _L1_gnn_in['lin2_wv']}

def reference(x, src, dst, edge_attr_4, edge_attr_64, node_vec1, L0_gnn_Wm_ss, L0_gnn_Wm_vv, L0_gnn_Wm_sv, L0_gnn_Wm_vs, L0_gnn_Lm_s, L0_gnn_Lm_v, L0_gnn_Wu_ss, L0_gnn_Wu_vv, L0_gnn_Wu_sv, L0_gnn_Wu_vs, L0_gnn_Lu_s, L0_gnn_Lu_v, L1_gnn_lin1_ws, L1_gnn_lin1_wv, L1_gnn_fc_w1, L1_gnn_fc_w2, L1_gnn_sc_ws, L1_gnn_sc_wv, L1_gnn_lin2_ws, L1_gnn_lin2_wv):
    import jax
    import jax.numpy as jnp

    def _L0_gnn_ref(node_features, edge_index, edge_attr_tensor, node_attr_scalar_raw, Wm_ss, Wm_vv, Wm_sv, Wm_vs, Lm_s, Lm_v, Wu_ss, Wu_vv, Wu_sv, Wu_vs, Lu_s, Lu_v):
        import jax, jax.numpy as jnp
        import numpy as np
        N = 20000
        E = 10000
        INV_SQRT3 = 0.5773502691896258
        INV8 = 0.125
        INV_SQRT32 = 0.17677669529663687
        INV64 = 0.015625
        INV32 = 0.03125
        INV_SQRT2048 = 0.022097086912079608
        n = node_features.shape[0]
        e = edge_attr_tensor.shape[0]
        row, col = (edge_index[0], edge_index[1])
        r_vec = edge_attr_tensor[:, :3]
        dist = edge_attr_tensor[:, 3:4]
        xj = node_features[col]
        s = xj[:, :64]
        v = xj[:, 64:].reshape(e, 32, 3)
        m0 = s @ Wm_ss * dist * INV8 + jnp.einsum('eui,ei->eu', v, r_vec) @ Wm_vv * (INV_SQRT3 * INV_SQRT32)
        m1 = (s @ Wm_sv)[:, :, None] * r_vec[:, None, :] * INV8 + jnp.einsum('eui,uw->ewi', v, Wm_vs) * dist[:, :, None] * INV_SQRT32
        m0 = m0 + s @ Lm_s * INV8
        m1 = m1 + jnp.einsum('eui,uw->ewi', v, Lm_v) * INV_SQRT32
        msg = jnp.concatenate([m0, m1.reshape(e, 96)], axis=-1)
        agg = jax.ops.segment_sum(msg, row, num_segments=n)
        a0 = agg[:, :64]
        a1 = agg[:, 64:].reshape(n, 32, 3)
        xs = node_features[:, :64]
        xv = node_features[:, 64:].reshape(n, 32, 3)
        u0 = jnp.einsum('nu,nv,uvw->nw', xs, a0, Wu_ss) * INV64 + jnp.einsum('nui,nvi,uvw->nw', xv, a1, Wu_vv) * (INV_SQRT3 * INV32)
        u1 = jnp.einsum('nu,nvi,uvw->nwi', xs, a1, Wu_sv) * INV_SQRT2048 + jnp.einsum('nui,nv,uvw->nwi', xv, a0, Wu_vs) * INV_SQRT2048
        u0 = u0 + xs @ Lu_s * INV8
        u1 = u1 + jnp.einsum('nui,uw->nwi', xv, Lu_v) * INV_SQRT32
        upd = jnp.concatenate([u0, u1.reshape(n, 96)], axis=-1)
        return node_features + upd

    def _L1_gnn_ref(node_features, node_attr, edge_src, edge_dst, edge_attr, edge_scalars, lin1_ws, lin1_wv, fc_w1, fc_w2, sc_ws, sc_wv, lin2_ws, lin2_wv):
        import jax, jax.numpy as jnp
        import numpy as np
        N, E = (625, 10000)
        S_IN, V_IN = (64, 32)
        S_MID, V_MID = (96, 128)
        S_OUT, V_OUT = (96, 32)
        R = 64
        FC_HID = 64
        W_NUMEL = 64 + 64 + 32 + 32 + 32
        NUM_NEIGHBORS = 16.0

        def _inv(d):
            return 1.0 / jnp.sqrt(jnp.float32(d))

        def _forward(node_features, node_attr, edge_attr, edge_scalars, lin1_ws, lin1_wv, fc_w1, fc_w2, sc_ws, sc_wv, lin2_ws, lin2_wv, edge_src, edge_dst):
            n = node_features.shape[0]
            s = node_features[:, :S_IN]
            v = node_features[:, S_IN:].reshape(n, V_IN, 3)
            a = node_attr
            sc_s = s @ sc_ws * a * _inv(S_IN)
            sc_v = jnp.einsum('nci,cd->ndi', v, sc_wv) * a[:, :, None] * _inv(V_IN)
            h_s = s @ lin1_ws * a * _inv(S_IN)
            h_v = jnp.einsum('nci,cd->ndi', v, lin1_wv) * a[:, :, None] * _inv(V_IN)
            hid = jax.nn.silu(edge_scalars @ fc_w1 * _inv(R))
            w = hid @ fc_w2 * _inv(FC_HID)
            w1, w2, w3, w4, w5 = jnp.split(w, [64, 128, 160, 192], axis=-1)
            es = h_s[edge_src]
            ev = h_v[edge_src]
            e0 = edge_attr[:, :1]
            e1 = edge_attr[:, 1:4]
            m_s1 = w1 * es * e0
            m_s2 = w4 * jnp.einsum('eci,ei->ec', ev, e1) * _inv(3)
            m_v1 = (w2 * es)[:, :, None] * e1[:, None, :]
            m_v2 = w3[:, :, None] * ev * e0[:, :, None]
            m_v3 = w5[:, :, None] * jnp.cross(ev, e1[:, None, :]) * _inv(2)
            mid_s = jnp.concatenate([m_s1, m_s2], axis=-1)
            mid_v = jnp.concatenate([m_v1, m_v2, m_v3], axis=1)
            inv_nn = 1.0 / jnp.sqrt(jnp.float32(NUM_NEIGHBORS))
            agg_s = jax.ops.segment_sum(mid_s, edge_dst, num_segments=n) * inv_nn
            agg_v = jax.ops.segment_sum(mid_v, edge_dst, num_segments=n) * inv_nn
            o_s = agg_s @ lin2_ws * a * _inv(S_MID)
            o_v = jnp.einsum('nci,cd->ndi', agg_v, lin2_wv) * a[:, :, None] * _inv(V_MID)
            pre_s = sc_s + o_s
            pre_v = sc_v + o_v
            scalars = jax.nn.silu(pre_s[:, :64])
            gates = jax.nn.sigmoid(pre_s[:, 64:96])
            gated = gates[:, :, None] * pre_v
            return jnp.concatenate([scalars, gated.reshape(n, 3 * V_OUT)], axis=-1)
        return _forward(node_features, node_attr, edge_attr, edge_scalars, lin1_ws, lin1_wv, fc_w1, fc_w2, sc_ws, sc_wv, lin2_ws, lin2_wv, edge_src, edge_dst)
    edge_index = jnp.stack([src, dst])
    h = jnp.maximum(_layernorm(x, axis=-1), 0.0)
    x = x + _L0_gnn_ref(h, edge_index, edge_attr_4, node_vec1, L0_gnn_Wm_ss, L0_gnn_Wm_vv, L0_gnn_Wm_sv, L0_gnn_Wm_vs, L0_gnn_Lm_s, L0_gnn_Lm_v, L0_gnn_Wu_ss, L0_gnn_Wu_vv, L0_gnn_Wu_sv, L0_gnn_Wu_vs, L0_gnn_Lu_s, L0_gnn_Lu_v)
    h = jnp.maximum(_layernorm(x, axis=-1), 0.0)
    x = x + _L1_gnn_ref(h, node_vec1, src, dst, edge_attr_4, edge_attr_64, L1_gnn_lin1_ws, L1_gnn_lin1_wv, L1_gnn_fc_w1, L1_gnn_fc_w2, L1_gnn_sc_ws, L1_gnn_sc_wv, L1_gnn_lin2_ws, L1_gnn_lin2_wv)
    return x

_drawn_inputs = setup_inputs


def setup_inputs(seed=0):
    import zlib

    import numpy as np

    out = dict(_drawn_inputs(seed))
    spreads = {}
    factors = {'L1_gnn_lin1_ws': 3.126,
     'L1_gnn_lin1_wv': 3.644,
     'L1_gnn_lin2_ws': 3.396,
     'L1_gnn_lin2_wv': 3.405}
    for name, (base, spread) in spreads.items():
        noise = np.random.default_rng([zlib.crc32(name.encode()), seed]).standard_normal(out[name].shape)
        drawn = base * np.exp(spread * noise) if base else spread * noise
        out[name] = jnp.asarray(drawn.astype(out[name].dtype))
    for name, factor in factors.items():
        out[name] = (out[name] * factor).astype(out[name].dtype)
    return out
```

```python
from contextlib import ExitStack

import concourse.bass as bass
from concourse import mybir
import math

P = 125
F32 = mybir.dt.float32
I32 = mybir.dt.int32
ALU = mybir.AluOpType
ACT = mybir.ActivationFunctionType
AX = mybir.AxisListType
S0, V0, D = 64, 32, 160
VD = 3 * V0
X1W = D + 1
AGW = 96 + VD
RPC = 8
TPG = 4
EPS = 1e-5


def waits_alone(eng, T):
    eng.sem_inc(T["passed"], 1)


def bcast(ap, axis, n):
    ap = ap.unsqueeze(axis)
    shape = list(ap.shape)
    shape[axis] = n
    return ap.broadcast_to(shape)


def reused(pair):
    return not (isinstance(pair, int) and pair == 0)


def by_two(eng, n, first, second):
    half = n // 2
    first(0, 0)

    def turn(pair):
        first(pair, 1)
        second(pair, 0)
        first(pair + 1, 0)
        second(pair, 1)

    if half > 1:
        turn(0)
    if half > 2:
        with eng.Fori(1, half - 1) as pair:
            turn(pair)
    first(half - 1, 1)
    second(half - 1, 0)
    second(half - 1, 1)


def stage_weights(nc, T, W, sem):
    names = sorted(W)

    with nc.Block() as block:
        loaded, cleared, scaled, eye_added = (sem(n) for n in ("w_loaded", "w_cleared", "w_scaled", "w_eye"))
        loads = []

        def load(dst, src):
            loads.append((dst, src))

        load(T["ident"][:, :], W["ident"])
        load(T["earlier"][:, :], W["earlier"])
        load(T["spare"][:, 0:1], W["spare_x"])
        load(T["a_all"][:, :], W["node_vec1"].rearrange("(p n) o -> p (n o)", p=P))
        load(T["ea"][:, :, :], W["edge_attr_4"].rearrange("(p t) c -> p t c", p=P))
        load(T["idx"][:, 0, :], W["src"].rearrange("(p t) -> p t", p=P))
        load(T["idx"][:, 1, :], W["dst"].rearrange("(p t) -> p t", p=P))
        load(T["w_pair"][:, 0:32, :], W["Wu_ss"].rearrange("(c a) v w -> (a v) c w", a=2))
        load(T["w_pair"][:, 32:40, :], W["Wu_vv"].rearrange("(c a) v w -> (a v) c w", a=4))
        load(T["w_vec"][S0:2 * S0, :, 0:V0], W["Wu_sv"])
        load(T["w_vec"][0:S0, :, V0:2 * V0], W["Wu_vs"])
        load(T["w_msg_s"][:, 0:64], W["Wm_ss"])
        load(T["w_msg_s"][:, 64:128], W["Lm_s"])
        load(T["w_msg_s"][:, 128:160], W["Wm_sv"])
        load(T["w_lin_s"][:, :], W["Lu_s"])
        load(T["w_in_s"][:, :], W["lin1_ws"])
        load(T["w_fc1"][:, :], W["fc_w1"])
        load(T["w_fc2"][:, :], W["fc_w2"])
        load(T["w_sc_s"][:, :], W["sc_ws"])
        load(T["w_out_s"][:, :], W["lin2_ws"])
        load(T["w_out_v"][:, :], W["lin2_wv"])
        for dst, src, n in (("w_msg_v", "Wm_vs", 32), ("w_lin_v", "Lu_v", 32), ("w_in_v", "lin1_wv", 32),
                            ("w_sc_v", "sc_wv", 32)):
            for i in range(3):
                load(T[dst][i:VD:3, i * n:(i + 1) * n], W[src])
        for i in range(3):
            load(T["w_msg_v"][i:VD:3, VD + i * 32:VD + (i + 1) * 32], W["Lm_v"])
            load(T["w_msg_v"][i:VD:3, 2 * VD + i * 64:2 * VD + (i + 1) * 64], W["Wm_vv"])
            load(T["eye_v"][i:VD:3, i * 32:(i + 1) * 32], W["ident"][0:32, 0:32])

        clears = [T[n] for n in ("w_msg_v", "w_lin_v", "w_in_v", "w_sc_v", "eye_v")]
        r32 = 1 / math.sqrt(32)
        scales = [
            (T["w_pair"][:, 0:32, :], 1 / 64),
            (T["w_pair"][:, 32:40, :], 1 / math.sqrt(3) / 32),
            (T["w_vec"][:, :, :], 1 / math.sqrt(2048)),
            (T["w_msg_s"][:, :], 1 / 8),
            (T["w_msg_v"][:, 0:2 * VD], r32),
            (T["w_msg_v"][:, 2 * VD:2 * VD + 192], r32 / math.sqrt(3)),
            (T["w_lin_s"][:, :], 1 / 8),
            (T["w_lin_v"][:, :], r32),
            (T["w_in_s"][:, :], 1 / 8),
            (T["w_in_v"][:, :], r32),
            (T["w_fc1"][:, :], 1 / 8),
            (T["w_fc2"][:, :], 1 / 8),
            (T["w_sc_s"][:, :], 1 / 8),
            (T["w_sc_v"][:, :], r32),
            (T["w_out_s"][0:64, :], 1 / 4 / math.sqrt(96)),
            (T["w_out_s"][64:96, :], 1 / 4 / math.sqrt(96) / math.sqrt(3)),
            (T["w_out_v"][0:96, :], 1 / 4 / math.sqrt(128)),
            (T["w_out_v"][96:128, :], 1 / 4 / math.sqrt(128) / math.sqrt(2)),
        ]

        @block.sync
        def _(sp):
            sp.wait_ge(cleared, len(clears) + 2)
            for dst, src in loads:
                sp.dma_start(dst, src, allow_slow_non_contiguous=True).then_inc(loaded, 16)
            sp.wait_ge(loaded, 16 * len(loads))

        @block.vector
        def _(dve):
            for t in clears:
                nc.vector.memset(t[:, :], 0.0).then_inc(cleared, 1)
            nc.vector.memset(T["w_vec"][:, :, :], 0.0).then_inc(cleared, 1)
            nc.vector.memset(T["eps"][:, :], EPS).then_inc(cleared, 1)
            dve.wait_ge(scaled, len(scales))
            nc.vector.tensor_tensor(T["w_lin_s"][:, :], T["w_lin_s"][:, :], T["ident"][0:S0, 0:S0],
                                    ALU.add).then_inc(eye_added, 1)
            nc.vector.tensor_tensor(T["w_lin_v"][:, :], T["w_lin_v"][:, :], T["eye_v"][:, :],
                                    ALU.add).then_inc(eye_added, 1)
            dve.wait_ge(eye_added, 2)

        @block.scalar
        def _(act):
            act.wait_ge(loaded, 16 * len(loads))
            for ap, c in scales:
                nc.scalar.mul(ap, ap, c).then_inc(scaled, 1)
            act.wait_ge(scaled, len(scales))


def stage_nodes0(nc, T, W, sem, N, NT, DR):
    NPP = N // P
    NCH = NPP // RPC
    TPC = NT // NCH
    x_v = W["x"].rearrange("(p n) d -> p (n d)", p=P)
    h_v = DR["h0"].rearrange("(p n) d -> p (n d)", p=P)
    x1_v = DR["x1"][0:N, :].rearrange("(p n) d -> p (n d)", p=P)
    ag_v = DR["agg"][0:N, :].rearrange("(p n) d -> p (n d)", p=P)

    with ExitStack() as ctx:
        def sb(name, shape, dt=F32):
            return ctx.enter_context(nc.sbuf_tensor(name, shape, dt))

        def pb(name):
            return ctx.enter_context(nc.psum_tensor(name, [128, 512], F32))

        xt = [sb(f"n0_x{b}", [P, RPC, D]) for b in range(2)]
        ht = [sb(f"n0_h{b}", [P, RPC, D]) for b in range(2)]
        base = [sb(f"n0_base{b}", [P, RPC, X1W]) for b in range(2)]
        stat = sb("n0_stat", [P, RPC, 6])
        mv = sb("n0_mv", [P, RPC, 2])
        std = sb("n0_std", [P, RPC])
        rstd = [sb(f"n0_rstd{b}", [P, RPC]) for b in range(2)]
        shift = [sb(f"n0_shift{b}", [P, RPC]) for b in range(2)]
        hT_s = [sb(f"n0_hTs{h}", [S0, 4 * P]) for h in range(2)]
        hT_v = [sb(f"n0_hTv{h}", [VD, 4 * P]) for h in range(2)]
        zero = sb("n0_zero", [P, RPC * AGW])
        rows = [sb(f"n0_rows{b}", [P, 2, TPC, P], I32) for b in range(2)]
        same = sb("n0_same", [P, 2 * TPC, P])
        hit = sb("n0_hit", [P, 2 * TPC, P])
        rep = sb("n0_rep", [P, 2, NT])
        target = sb("n0_target", [P, 2, NT])
        toward = sb("n0_toward", [P, 2, NT])
        ps_s = [pb(f"n0_ps_s{h}") for h in range(2)]
        ps_v = [pb(f"n0_ps_v{h}") for h in range(2)]
        ps_o = [pb(f"n0_ps_o{q}") for q in range(4)]

        x_loaded = [sem(f"n0_x_loaded{b}") for b in range(2)]
        rows_loaded = [sem(f"n0_rows_loaded{b}") for b in range(2)]
        rows_used = [sem(f"n0_rows_used{b}") for b in range(2)]
        zeroed = sem("n0_zeroed")
        spare_stored = sem("n0_spare_stored")
        agg_cleared = sem("n0_agg_cleared")
        stats_done = sem("n0_stats_done")
        var_done = sem("n0_var_done")
        std_done = sem("n0_std_done")
        rstd_done = sem("n0_rstd_done")
        shift_done = sem("n0_shift_done")
        h_done = [sem(f"n0_h_done{b}") for b in range(2)]
        hT_made = sem("n0_hT_made")
        hT_copied = sem("n0_hT_copied")
        lin_made = sem("n0_lin_made")
        base_added = sem("n0_base_added")
        base_done = [sem(f"n0_base_done{b}") for b in range(2)]
        h_stored = [sem(f"n0_h_stored{b}") for b in range(2)]
        x1_stored = [sem(f"n0_x1_stored{b}") for b in range(2)]
        compared = sem("n0_compared")
        masked = sem("n0_masked")
        rep_done = sem("n0_rep_done")
        target_done = sem("n0_target_done")

        with nc.Block() as block:
            @block.sync
            def _(sp):
                sp.wait_ge(zeroed, 1)
                sp.dma_start(DR["x1"][N:N + P, :], zero[:, 0:X1W]).then_inc(spare_stored, 16)
                sp.dma_start(DR["agg"][N:N + P, :], zero[:, 0:AGW]).then_inc(spare_stored, 16)

                def load(pair, b):
                    c = 2 * pair + b
                    sp.wait_ge(base_done[b], pair)
                    sp.wait_ge(h_done[b], pair)
                    sp.dma_start(xt[b][:, :, :].rearrange("p r d -> p (r d)"),
                                 x_v[:, bass.ds(c * (RPC * D), RPC * D)]).then_inc(x_loaded[b], 16)
                    sp.wait_ge(rows_used[b], pair)
                    for k, name in enumerate(("src_rows", "dst_rows")):
                        row = W[name][bass.ds(c * (TPC * P), TPC * P)].partition_broadcast(P)
                        sp.dma_start(rows[b][:, k, :, :].rearrange("p t q -> p (t q)"), row).then_inc(rows_loaded[b], 16)

                def store(pair, b):
                    c = 2 * pair + b
                    sp.dma_start(ag_v[:, bass.ds(c * (RPC * AGW), RPC * AGW)], zero[:, :]).then_inc(agg_cleared, 16)
                    sp.wait_ge(h_done[b], pair + 1)
                    sp.dma_start(h_v[:, bass.ds(c * (RPC * D), RPC * D)],
                                 ht[b][:, :, :].rearrange("p r d -> p (r d)")).then_inc(h_stored[b], 16)
                    sp.wait_ge(base_done[b], pair + 1)
                    sp.dma_start(x1_v[:, bass.ds(c * (RPC * X1W), RPC * X1W)],
                                 base[b][:, :, :].rearrange("p r d -> p (r d)")).then_inc(x1_stored[b], 16)

                by_two(sp, NCH, load, store)
                sp.wait_ge(spare_stored, 32)
                sp.wait_ge(agg_cleared, 16 * NCH)
                for b in range(2):
                    sp.wait_ge(h_stored[b], 16 * (NCH // 2))
                    sp.wait_ge(x1_stored[b], 16 * (NCH // 2))

            @block.vector
            def _(dve):
                nc.vector.memset(zero[:, :], 0.0).then_inc(zeroed, 1)

                def normalise(pair, b):
                    c = 2 * pair + b
                    dve.wait_ge(x_loaded[b], 16 * (pair + 1))
                    for r in range(RPC):
                        ins = nc.vector.bn_stats(stat[:, r, :], xt[b][:, r, :])
                    ins.then_inc(stats_done, 1)
                    dve.wait_ge(stats_done, c + 1)
                    dve.wait_ge(std_done, c)
                    waits_alone(dve, T)
                    for r in range(RPC):
                        ins = nc.vector.bn_aggr(mv[:, r, :], stat[:, r, :])
                    ins.then_inc(var_done, 1)
                    repeats(pair, b)
                    dve.wait_ge(std_done, c + 1)
                    dve.wait_ge(h_done[b], pair)
                    nc.vector.reciprocal(rstd[b][:, :], std[:, :]).then_inc(rstd_done, 1)
                    dve.wait_ge(rstd_done, c + 1)
                    nc.vector.scalar_tensor_tensor(shift[b][:, :], mv[:, :, 0], -1.0, rstd[b][:, :], ALU.mult,
                                                   ALU.mult).then_inc(shift_done, 1)

                def repeats(pair, b):
                    c = 2 * pair + b
                    dve.wait_ge(rows_loaded[b], 32 * (pair + 1))
                    for k in range(2):
                        mine = T["idx"][:, k, bass.ds(c * TPC, TPC)]
                        ins = nc.vector.tensor_tensor(same[:, k * TPC:(k + 1) * TPC, :], rows[b][:, k, :, :],
                                                      bcast(mine, 2, P), ALU.is_equal)
                        if k == 1:
                            ins.then_inc(compared, 1)
                    dve.wait_ge(compared, c + 1)
                    nc.vector.tensor_tensor(hit[:, :, :], same[:, :, :], bcast(T["earlier"][:, :], 1, 2 * TPC),
                                            ALU.mult).then_inc(masked, 1)
                    dve.wait_ge(masked, c + 1)
                    nc.vector.tensor_reduce(rep[:, :, bass.ds(c * TPC, TPC)],
                                            hit[:, :, :].rearrange("p (k t) q -> p k t q", k=2), AX.X,
                                            ALU.max).then_inc(rows_used[b], 1)

                def add(pair, b):
                    c = 2 * pair + b
                    dve.wait_ge(x1_stored[b], 16 * pair)
                    for q in range(4):
                        dve.wait_ge(lin_made, 4 * c + q + 1)
                        o = ps_o[q][0:P, 0:2 * D].rearrange("p (r d) -> p r d", r=2)
                        r = slice(2 * q, 2 * q + 2)
                        nc.vector.tensor_tensor(base[b][:, r, 0:S0], xt[b][:, r, 0:S0], o[:, :, 0:S0], ALU.add)
                        ins = nc.vector.tensor_tensor(
                            base[b][:, r, S0:D].rearrange("p r (w i) -> p r w i", i=3),
                            xt[b][:, r, S0:D].rearrange("p r (w i) -> p r w i", i=3),
                            o[:, :, S0:D].rearrange("p r (i w) -> p r w i", i=3), ALU.add)
                        ins.then_inc(base_added, 1)
                    nc.vector.tensor_copy(base[b][:, :, D], T["a_all"][:, bass.ds(c * RPC, RPC)]).then_inc(base_done[b], 1)

                by_two(dve, NCH, normalise, add)
                nc.vector.tensor_copy(target[:, :, :], T["idx"][:, :, 0:NT]).then_inc(target_done, 1)
                dve.wait_ge(target_done, 1)
                flat = "p k t -> p (k t)"
                nc.vector.tensor_scalar(toward[:, :, :].rearrange(flat), target[:, :, :].rearrange(flat), -1.0,
                                        T["spare"][:, 0:1], ALU.mult, ALU.add).then_inc(target_done, 1)
                for b in range(2):
                    dve.wait_ge(rows_used[b], NCH // 2)
                dve.wait_ge(target_done, 2)
                nc.vector.tensor_tensor(toward[:, :, :].rearrange(flat), toward[:, :, :].rearrange(flat),
                                        rep[:, :, :].rearrange(flat), ALU.mult).then_inc(target_done, 1)
                dve.wait_ge(target_done, 3)
                nc.vector.tensor_tensor(T["put"][:, :, :].rearrange(flat), toward[:, :, :].rearrange(flat),
                                        target[:, :, :].rearrange(flat), ALU.add).then_inc(target_done, 1)
                dve.wait_ge(target_done, 4)

            @block.scalar
            def _(act):
                def relu(pair, b):
                    c = 2 * pair + b
                    act.wait_ge(var_done, c + 1)
                    act.wait_ge(shift_done, c)
                    nc.scalar.activation(std[:, :], mv[:, :, 1], ACT.Sqrt, bias=T["eps"][:, 0:1]).then_inc(std_done, 1)
                    act.wait_ge(shift_done, c + 1)
                    act.wait_ge(h_stored[b], 16 * pair)
                    for r in range(RPC):
                        ins = nc.scalar.activation(ht[b][:, r, :], xt[b][:, r, :], ACT.Relu,
                                                   bias=shift[b][:, r:r + 1], scale=rstd[b][:, r:r + 1])
                    ins.then_inc(h_done[b], 1)

                def copy(pair, b):
                    c = 2 * pair + b
                    for h in range(2):
                        act.wait_ge(hT_made, 2 * c + h + 1)
                        act.wait_ge(lin_made, 4 * c)
                        nc.scalar.copy(hT_s[h][:, :], ps_s[h][0:S0, 0:4 * P])
                        nc.scalar.copy(hT_v[h][:, :], ps_v[h][0:VD, 0:4 * P]).then_inc(hT_copied, 1)

                by_two(act, NCH, relu, copy)

            @block.tensor
            def _(pe):
                def turn(pair, b):
                    c = 2 * pair + b
                    pe.wait_ge(h_done[b], pair + 1)
                    for h in range(2):
                        pe.wait_ge(hT_copied, 2 * c)
                        for r in range(4):
                            nc.tensor.transpose(ps_v[h][0:VD, r * P:(r + 1) * P], ht[b][:, 4 * h + r, S0:D],
                                                T["ident"][0:P, 0:P])
                            ins = nc.tensor.transpose(ps_s[h][0:S0, r * P:(r + 1) * P], ht[b][:, 4 * h + r, 0:S0],
                                                      T["ident"][0:P, 0:P])
                        ins.then_inc(hT_made, 1)

                def linear(pair, b):
                    c = 2 * pair + b
                    for q in range(4):
                        pe.wait_ge(hT_copied, 2 * c + q // 2 + 1)
                        pe.wait_ge(base_added, 4 * c)
                        for r in range(2):
                            m = (2 * q + r) % 4 * P
                            nc.tensor.matmul(ps_o[q][0:P, r * D:r * D + S0], hT_s[q // 2][:, m:m + P],
                                             T["w_lin_s"][:, :], start=True, stop=True)
                            ins = nc.tensor.matmul(ps_o[q][0:P, r * D + S0:(r + 1) * D], hT_v[q // 2][:, m:m + P],
                                                   T["w_lin_v"][:, :], start=True, stop=True)
                        ins.then_inc(lin_made, 1)

                by_two(pe, NCH, turn, linear)


def stage_edges0(nc, T, W, sem, NT, DR):
    src_rows = W["src_rows"]
    G_AD, G_BE, G_C, G_F = 0, D, 2 * D, 2 * D + V0
    NG = 14
    CH = [list(range(4 * g, 4 * g + 4)) for g in range(NG)]

    with ExitStack() as ctx:
        def sb(name, shape, dt=F32):
            return ctx.enter_context(nc.sbuf_tensor(name, shape, dt))

        def pb(name):
            return ctx.enter_context(nc.psum_tensor(name, [128, 512], F32))

        h_dst = [sb(f"e0_h_dst{b}", [P, D]) for b in range(2)]
        own = [sb(f"e0_own{b}", [P, S0 + D]) for b in range(2)]
        vec = [sb(f"e0_vec{b}", [P, 3, 2 * V0]) for b in range(2)]
        hd_s = sb("e0_hd_s", [S0, P])
        hd_v = sb("e0_hd_v", [VD, P])
        gm = sb("e0_gm", [P, 2 * D + V0 + 3 * S0])
        sm = sb("e0_sm", [128, P])
        pair_s = sb("e0_pair_s", [P, 4, 16, S0])
        pair_v = sb("e0_pair_v", [P, 3, V0, V0])
        pairT = [sb(f"e0_pairT{k}", [128, 4 * P]) for k in range(3)]
        prod = [sb(f"e0_prod{k}", [P, 3, 8, 2 * V0]) for k in range(2)]
        upd = sb("e0_upd", [P, X1W])
        total = [sb(f"e0_total{b}", [P, X1W]) for b in range(2)]
        rows = [sb(f"e0_rows{b}", [P, P], I32) for b in range(2)]
        same = [sb(f"e0_same{b}", [P, P]) for b in range(2)]
        ends = [sb(f"e0_ends{b}", [P, 2], I32) for b in range(2)]
        put = sb("e0_put", [P, 1], I32)
        ps_y = [pb(f"e0_ps_y{k}") for k in range(2)]
        ps_t = [pb(f"e0_ps_t{k}") for k in range(2)]
        ps_m, ps_u, ps_g, ps_f = pb("e0_ps_m"), pb("e0_ps_u"), pb("e0_ps_g"), pb("e0_ps_f")

        gathered = [sem(f"e0_gathered{b}") for b in range(2)]
        rows_loaded = [sem(f"e0_rows_loaded{b}") for b in range(2)]
        same_made = sem("e0_same_made")
        hd_turned = sem("e0_hd_turned")
        hd_copied = sem("e0_hd_copied")
        gm_made = sem("e0_gm_made")
        gm_copied = sem("e0_gm_copied")
        msg_step = sem("e0_msg_step")
        vec_copied = sem("e0_vec_copied")
        sm_turned = sem("e0_sm_turned")
        sm_copied = sem("e0_sm_copied")
        pair_s_made = sem("e0_pair_s_made")
        pair_v_made = sem("e0_pair_v_made")
        pairs_turned = sem("e0_pairs_turned")
        pairs_copied = sem("e0_pairs_copied")
        pairs_summed = sem("e0_pairs_summed")
        y_made = sem("e0_y_made")
        y_used = sem("e0_y_used")
        vec_summed = sem("e0_vec_summed")
        upd_cleared = sem("e0_upd_cleared")
        upd_s_copied = sem("e0_upd_s_copied")
        total_made = sem("e0_total_made")
        total_copied = sem("e0_total_copied")
        added = sem("e0_added")
        ends_copied = sem("e0_ends_copied")
        put_copied = sem("e0_put_copied")
        MSG = 8

        def tiles(eng, step):
            step(0, 0, 2)
            step(0, 1, 2)
            with eng.Fori(1, NT // 2 - 1) as pair:
                step(pair, 0, 2)
                step(pair, 1, 2)
            step(NT // 2 - 1, 0, 1)
            step(NT // 2 - 1, 1, 0)

        with nc.Block() as block:
            @block.sync
            def _(sp):
                def rows_of(pair, b):
                    t = 2 * pair + b
                    sp.dma_start(rows[b][:, :], src_rows[bass.ds(t * P, P)].partition_broadcast(P)).then_inc(rows_loaded[b], 16)

                rows_of(0, 0)
                rows_of(0, 1)

                def step(pair, b, follow):
                    if follow == 2:
                        sp.wait_ge(same_made, 2 * pair + b + 1)
                        rows_of(pair + 1, b)

                tiles(sp, step)

            @block.gpsimd
            def _(pool):
                def gather(pair, b):
                    t = 2 * pair + b
                    waits_alone(pool, T)
                    nc.gpsimd.tensor_copy(ends[b][:, :], T["idx"][:, :, bass.ds(t, 1)].squeeze(2)).then_inc(ends_copied, 1)
                    pool.wait_ge(ends_copied, t + 1)
                    waits_alone(pool, T)
                    pool.indirect_dma_start(own[b][:, S0:S0 + D], None, DR["h0"],
                                            bass.IndirectOffsetOnAxis(ends[b][:, 0:1], 0)).then_inc(gathered[b], 16)
                    pool.indirect_dma_start(h_dst[b][:, :], None, DR["h0"],
                                            bass.IndirectOffsetOnAxis(ends[b][:, 1:2], 0)).then_inc(gathered[b], 16)

                def copy_vec(pair, b):
                    pool.wait_ge(gathered[b], 32 * (pair + 1))
                    waits_alone(pool, T)
                    nc.gpsimd.tensor_copy(vec[b][:, :, V0:2 * V0],
                                          own[b][:, 2 * S0:S0 + D].rearrange("p (u i) -> p i u", i=3)).then_inc(vec_copied, 1)

                gather(0, 0)
                gather(0, 1)
                copy_vec(0, 0)

                def step(pair, b, follow):
                    t = 2 * pair + b
                    pool.wait_ge(msg_step, MSG * (t + 1))
                    pool.wait_ge(pairs_turned, NG * t)
                    nc.gpsimd.tensor_tensor(pair_v[:, :, :, :], bcast(vec[b][:, :, V0:2 * V0], 3, V0),
                                            bcast(vec[b][:, :, 0:V0], 2, V0), ALU.mult).then_inc(pair_v_made, 1)
                    if follow:
                        pool.wait_ge(vec_summed, 4 * t)
                        copy_vec(pair + b, 1 - b)
                    if follow == 2:
                        pool.wait_ge(hd_turned, t + 1)
                        pool.wait_ge(sm_turned, t + 1)
                        pool.wait_ge(pair_s_made, 4 * (t + 1))
                        pool.wait_ge(vec_copied, t + 1)
                        gather(pair + 1, b)
                    pool.wait_ge(added, 16 * t)
                    waits_alone(pool, T)
                    nc.gpsimd.tensor_copy(put[:, :], T["put"][:, 0, bass.ds(t, 1)]).then_inc(put_copied, 1)
                    pool.wait_ge(put_copied, t + 1)
                    pool.wait_ge(total_copied, t + 1)
                    waits_alone(pool, T)
                    pool.indirect_dma_start(DR["x1"], bass.IndirectOffsetOnAxis(put[:, 0:1], 0),
                                            total[b][:, :], None, compute_op=ALU.add).then_inc(added, 16)

                tiles(pool, step)
                pool.wait_ge(added, 16 * NT)

            @block.vector
            def _(dve):
                nc.vector.memset(upd[:, :], 0.0).then_inc(upd_cleared, 1)

                def message(pair, b):
                    t = 2 * pair + b
                    dve.wait_ge(rows_loaded[b], 16 * (pair + 1))
                    nc.vector.tensor_tensor(same[b][:, :], rows[b][:, :],
                                            T["idx"][:, 0, bass.ds(t, 1)].broadcast_to([P, P]),
                                            ALU.is_equal).then_inc(same_made, 1)
                    dve.wait_ge(gm_copied, t + 1)
                    dve.wait_ge(vec_copied, t + 1)
                    m0 = own[b][:, 0:S0]
                    m1 = vec[b][:, :, 0:V0]
                    dist = T["ea"][:, bass.ds(t, 1), 3]
                    nc.vector.scalar_tensor_tensor(m0, gm[:, G_AD:G_AD + S0], dist, gm[:, G_BE:G_BE + S0], ALU.mult,
                                                   ALU.add).then_inc(msg_step, 1)
                    nc.vector.scalar_tensor_tensor(
                        m1, gm[:, G_AD + S0:G_AD + D].rearrange("p (i w) -> p i w", i=3), dist,
                        gm[:, G_BE + S0:G_BE + D].rearrange("p (i w) -> p i w", i=3), ALU.mult,
                        ALU.add).then_inc(msg_step, 1)
                    for i in range(3):
                        r = T["ea"][:, bass.ds(t, 1), i]
                        dve.wait_ge(msg_step, MSG * t + 2 * i + 1)
                        nc.vector.scalar_tensor_tensor(m0, gm[:, G_F + i * S0:G_F + (i + 1) * S0], r, m0, ALU.mult,
                                                       ALU.add).then_inc(msg_step, 1)
                        dve.wait_ge(msg_step, MSG * t + 2)
                        nc.vector.scalar_tensor_tensor(m1[:, i, :], gm[:, G_C:G_C + V0], r, m1[:, i, :], ALU.mult,
                                                       ALU.add).then_inc(msg_step, 1)

                def step(pair, b, follow):
                    t = 2 * pair + b
                    dve.wait_ge(msg_step, MSG * (t + 1))
                    dve.wait_ge(pairs_turned, NG * t)
                    for k in range(4):
                        nc.vector.tensor_tensor(pair_s[:, k, :, :], bcast(own[b][:, S0 + 16 * k:S0 + 16 * (k + 1)], 2, S0),
                                                bcast(own[b][:, 0:S0], 1, 16), ALU.mult).then_inc(pair_s_made, 1)

                    def multiply(q):
                        dve.wait_ge(y_made, 4 * t + q + 1)
                        if q >= 2:
                            dve.wait_ge(vec_summed, 4 * t + q - 1)
                        else:
                            dve.wait_ge(vec_summed, 4 * t)
                        y = ps_y[q % 2][0:P, :].rearrange("p (w c) -> p w c", c=2 * V0)
                        nc.vector.tensor_tensor(prod[q % 2][:, :, :, :], bcast(y, 1, 3), bcast(vec[b][:, :, :], 2, 8),
                                                ALU.mult).then_inc(y_used, 1)

                    def reduce(q):
                        dve.wait_ge(y_used, 4 * t + q + 1)
                        if q == 0:
                            dve.wait_ge(total_made, t)
                            dve.wait_ge(upd_cleared, 1)
                        out = upd[:, S0 + 24 * q:S0 + 24 * (q + 1)].rearrange("p (w i) -> p i w", i=3)
                        nc.vector.tensor_reduce(out, prod[q % 2][:, :, :, :], AX.X, ALU.add).then_inc(vec_summed, 1)

                    multiply(0)
                    multiply(1)
                    reduce(0)
                    multiply(2)
                    reduce(1)
                    multiply(3)
                    reduce(2)
                    reduce(3)
                    if follow:
                        dve.wait_ge(total_made, t)
                        message(pair + b, 1 - b)

                message(0, 0)
                tiles(dve, step)

            @block.scalar
            def _(act):
                def copy_hd(t):
                    act.wait_ge(hd_turned, t + 1)
                    act.wait_ge(gm_made, t)
                    nc.scalar.copy(hd_s[:, :], ps_f[0:S0, 2 * P:3 * P])
                    nc.scalar.copy(hd_v[:, :], ps_f[0:VD, 3 * P:4 * P]).then_inc(hd_copied, 1)

                def copy_gm(t):
                    act.wait_ge(gm_made, t + 1)
                    act.wait_ge(msg_step, MSG * t)
                    nc.scalar.copy(gm[:, 0:2 * D], ps_g[0:P, 0:2 * D])
                    nc.scalar.copy(gm[:, 2 * D:], ps_f[0:P, 0:V0 + 3 * S0]).then_inc(gm_copied, 1)

                def step(pair, b, follow):
                    t = 2 * pair + b
                    act.wait_ge(sm_turned, t + 1)
                    act.wait_ge(y_made, 4 * t)
                    nc.scalar.copy(sm[:, :], ps_m[:, 0:P]).then_inc(sm_copied, 1)
                    if follow:
                        copy_hd(t + 1)
                        copy_gm(t + 1)
                    for g in range(NG):
                        act.wait_ge(pairs_turned, NG * t + g + 1)
                        if g >= 3:
                            act.wait_ge(pairs_summed, NG * t + g - 2)
                        else:
                            act.wait_ge(pairs_summed, NG * t)
                        nc.scalar.copy(pairT[g % 3][:, :], ps_t[g % 2][:, 0:4 * P]).then_inc(pairs_copied, 1)
                    act.wait_ge(pairs_summed, NG * (t + 1))
                    act.wait_ge(upd_cleared, 1)
                    act.wait_ge(total_made, t)
                    nc.scalar.copy(upd[:, 0:S0], ps_u[0:P, 0:S0]).then_inc(upd_s_copied, 1)
                    act.wait_ge(total_made, t + 1)
                    if reused(pair):
                        act.wait_ge(added, 16 * (t - 1))
                    nc.scalar.copy(total[b][:, :], ps_g[0:P, 0:X1W]).then_inc(total_copied, 1)

                copy_hd(0)
                copy_gm(0)
                tiles(act, step)

            @block.tensor
            def _(pe):
                def turn_hd(pair, b):
                    t = 2 * pair + b
                    pe.wait_ge(gathered[b], 32 * (pair + 1))
                    pe.wait_ge(gm_copied, t)
                    nc.tensor.transpose(ps_f[0:VD, 3 * P:4 * P], h_dst[b][:, S0:D], T["ident"][0:P, 0:P])
                    nc.tensor.transpose(ps_f[0:S0, 2 * P:3 * P], h_dst[b][:, 0:S0], T["ident"][0:P, 0:P]).then_inc(hd_turned, 1)

                def message_products(t):
                    pe.wait_ge(hd_copied, t + 1)
                    pe.wait_ge(gm_copied, t)
                    mv = T["w_msg_v"]
                    for out, x, w in ((ps_g[0:P, 0:S0], hd_s, T["w_msg_s"][:, 0:S0]),
                                      (ps_g[0:P, S0:D], hd_v, mv[:, 0:VD]),
                                      (ps_g[0:P, D:D + S0], hd_s, T["w_msg_s"][:, S0:2 * S0]),
                                      (ps_g[0:P, D + S0:2 * D], hd_v, mv[:, VD:2 * VD]),
                                      (ps_f[0:P, 0:V0], hd_s, T["w_msg_s"][:, 2 * S0:2 * S0 + V0]),
                                      (ps_f[0:P, V0:V0 + 3 * S0], hd_v, mv[:, 2 * VD:])):
                        ins = nc.tensor.matmul(out, x[:, :], w, start=True, stop=True)
                    ins.then_inc(gm_made, 1)

                def step(pair, b, follow):
                    t = 2 * pair + b
                    pe.wait_ge(msg_step, MSG * (t + 1))
                    pe.wait_ge(sm_copied, t)
                    nc.tensor.transpose(ps_m[:, 0:P], own[b][:, 0:2 * S0],
                                        T["ident"][0:P, 0:P]).then_inc(sm_turned, 1)
                    if follow:
                        turn_hd(pair + b, 1 - b)

                    def vector_weights(q):
                        if q == 0:
                            pe.wait_ge(sm_copied, t + 1)
                        if q >= 2:
                            pe.wait_ge(y_used, 4 * t + q - 1)
                        else:
                            pe.wait_ge(y_used, 4 * t)
                        nc.tensor.matmul(ps_y[q % 2][0:P, :], sm[:, 0:P],
                                         T["w_vec"][:, 8 * q:8 * (q + 1), :].rearrange("p w c -> p (w c)"),
                                         start=True, stop=True).then_inc(y_made, 1)

                    def turn(g):
                        if g % 2 == 0 and g < 8:
                            pe.wait_ge(pair_s_made, 4 * t + g // 2 + 1)
                        if g == 8:
                            pe.wait_ge(pair_v_made, t + 1)
                        if g >= 2:
                            pe.wait_ge(pairs_copied, NG * t + g - 1)
                        for n, c in enumerate(CH[g]):
                            if c < 32:
                                x = pair_s[:, c // 8, 2 * (c % 8):2 * (c % 8) + 2, :].rearrange("p u v -> p (u v)")
                            else:
                                i, c8 = divmod(c - 32, 8)
                                x = pair_v[:, i, 4 * c8:4 * c8 + 4, :].rearrange("p u v -> p (u v)")
                            ins = nc.tensor.transpose(ps_t[g % 2][:, n * P:(n + 1) * P], x, T["ident"][0:P, 0:P])
                        ins.then_inc(pairs_turned, 1)

                    def sum_pairs(g):
                        pe.wait_ge(pairs_copied, NG * t + g + 1)
                        if g == 0:
                            pe.wait_ge(upd_s_copied, t)
                        for n, c in enumerate(CH[g]):
                            w = T["w_pair"][:, c if c < 32 else 32 + (c - 32) % 8, :]
                            ins = nc.tensor.matmul(ps_u[0:P, 0:S0], pairT[g % 3][:, n * P:(n + 1) * P], w,
                                                   start=(c == 0), stop=(c == 55))
                        ins.then_inc(pairs_summed, 1)

                    vector_weights(0)
                    vector_weights(1)
                    turn(0)
                    if follow:
                        pe.wait_ge(total_copied, t)
                        message_products(t + 1)
                    for g in range(1, NG):
                        turn(g)
                        sum_pairs(g - 1)
                        if g == 8:
                            vector_weights(2)
                        if g == 11:
                            vector_weights(3)
                    sum_pairs(NG - 1)
                    pe.wait_ge(upd_s_copied, t + 1)
                    pe.wait_ge(vec_summed, 4 * (t + 1))
                    pe.wait_ge(same_made, t + 1)
                    if follow:
                        pe.wait_ge(gm_copied, t + 2)
                    nc.tensor.matmul(ps_g[0:P, 0:X1W], same[b][:, :], upd[:, :], start=True, stop=True).then_inc(total_made, 1)

                turn_hd(0, 0)
                message_products(0)
                tiles(pe, step)


def stage_edges1(nc, T, W, sem, NT, DR):
    NGR = NT // TPG
    es_v = W["edge_attr_64"].rearrange("(p t) c -> p (t c)", p=P)

    with ExitStack() as ctx:
        def sb(name, shape, dt=F32):
            return ctx.enter_context(nc.sbuf_tensor(name, shape, dt))

        ps = [ctx.enter_context(nc.psum_tensor(f"e1_ps{k}", [128, 512], F32)) for k in range(8)]
        es = [sb(f"e1_es{b}", [P, TPG, 64]) for b in range(2)]
        rows = [sb(f"e1_rows{b}", [P, TPG, P], I32) for b in range(2)]
        x1r = [sb(f"e1_x1r{b}", [P, TPG, X1W]) for b in range(2)]
        stat = sb("e1_stat", [P, TPG, 6])
        mv = sb("e1_mv", [P, TPG, 2])
        std = sb("e1_std", [P, TPG])
        rstd = sb("e1_rstd", [P, TPG])
        shift = sb("e1_shift", [P, TPG])
        h1 = sb("e1_h1", [P, TPG, D])
        esT = sb("e1_esT", [64, TPG * P])
        sig = sb("e1_sig", [64, TPG * P])
        hid = sb("e1_hid", [64, TPG * P])
        hT_s = sb("e1_hT_s", [S0, TPG * P])
        hT_v = sb("e1_hT_v", [VD, TPG * P])
        fc = [sb(f"e1_fc{b}", [P, TPG, 224]) for b in range(2)]
        hs = [sb(f"e1_hs{b}", [P, TPG, S0]) for b in range(2)]
        hv = [sb(f"e1_hv{b}", [P, TPG, 5, V0]) for b in range(2)]
        ea = [sb(f"e1_ea{b}", [P, TPG, 6]) for b in range(2)]
        ws = sb("e1_ws", [P, TPG, 2, 64])
        w3e = sb("e1_w3e", [P, TPG, V0])
        dots = sb("e1_dots", [P, TPG, 3, V0])
        dot = sb("e1_dot", [P, TPG, V0])
        cr1 = sb("e1_cr1", [P, TPG, 3, V0])
        cr2 = sb("e1_cr2", [P, TPG, 3, V0])
        mid_s = sb("e1_mid_s", [P, TPG, 96])
        mid_v = sb("e1_mid_v", [P, TPG, 3, 128])
        mT_s = sb("e1_mT_s", [96, TPG * P])
        mT_v = sb("e1_mT_v", [128, 3, TPG * P])
        out = sb("e1_out", [P, TPG, AGW])
        total = [sb(f"e1_total{b}", [P, TPG, AGW]) for b in range(2)]
        same = [sb(f"e1_same{b}", [P, TPG, P]) for b in range(2)]

        starts = [sb(f"e1_starts{b}", [P, TPG], I32) for b in range(2)]
        put = sb("e1_put", [P, TPG], I32)
        starts_copied, put_copied = sem("e1_starts_copied"), sem("e1_put_copied")
        es_loaded = [sem(f"e1_es_loaded{b}") for b in range(2)]
        rows_loaded = [sem(f"e1_rows_loaded{b}") for b in range(2)]
        gathered = [sem(f"e1_gathered{b}") for b in range(2)]
        (stats_done, var_done, std_done, rstd_done, shift_done, h1_done, ea_done, same_made, es_turned, es_copied,
         h1_turned, h1_copied, hid_made, sig_done, silu_done, fc_made, fc_copied, lin_made, lin_copied, ext_done,
         mid_step, mid_done, mid_turned, mid_copied, out_made, out_copied, total_made, total_copied, added) = (
            sem("e1_" + n) for n in (
                "stats_done", "var_done", "std_done", "rstd_done", "shift_done", "h1_done", "ea_done", "same_made",
                "es_turned", "es_copied", "h1_turned", "h1_copied", "hid_made", "sig_done", "silu_done", "fc_made",
                "fc_copied", "lin_made", "lin_copied", "ext_done", "mid_step", "mid_done", "mid_turned", "mid_copied",
                "out_made", "out_copied", "total_made", "total_copied", "added"))
        MID = 12

        with nc.Block() as block:
            @block.sync
            def _(sp):
                def load(pair, b):
                    g = 2 * pair + b
                    sp.dma_start(es[b][:, :, :].rearrange("p t c -> p (t c)"),
                                 es_v[:, bass.ds(g * (TPG * 64), TPG * 64)]).then_inc(es_loaded[b], 16)
                    sp.dma_start(rows[b][:, :, :].rearrange("p t q -> p (t q)"),
                                 W["dst_rows"][bass.ds(g * (TPG * P), TPG * P)].partition_broadcast(P)).then_inc(rows_loaded[b], 16)

                def freed(pair, b):
                    g = 2 * pair + b
                    sp.wait_ge(es_turned, g + 1)
                    sp.wait_ge(same_made, g + 1)

                load(0, 0)
                load(0, 1)
                with sp.Fori(0, NGR // 2 - 1) as pair:
                    for b in range(2):
                        freed(pair, b)
                        load(pair + 1, b)

            @block.gpsimd
            def _(pool):
                def gather(pair, b):
                    g = 2 * pair + b
                    waits_alone(pool, T)
                    nc.gpsimd.tensor_copy(starts[b][:, :], T["idx"][:, 0, bass.ds(g * TPG, TPG)]).then_inc(starts_copied, 1)
                    pool.wait_ge(starts_copied, g + 1)
                    for j in range(TPG):
                        waits_alone(pool, T)
                        pool.indirect_dma_start(x1r[b][:, j, :], None, DR["x1"],
                                                bass.IndirectOffsetOnAxis(starts[b][:, j:j + 1], 0)).then_inc(gathered[b], 16)

                def scatter(pair, b):
                    g = 2 * pair + b
                    pool.wait_ge(added, 16 * TPG * g)
                    waits_alone(pool, T)
                    nc.gpsimd.tensor_copy(put[:, :], T["put"][:, 1, bass.ds(g * TPG, TPG)]).then_inc(put_copied, 1)
                    pool.wait_ge(put_copied, g + 1)
                    pool.wait_ge(total_copied, g + 1)
                    for j in range(TPG):
                        pool.wait_ge(added, 16 * (g * TPG + j))
                        waits_alone(pool, T)
                        pool.indirect_dma_start(DR["agg"],
                                                bass.IndirectOffsetOnAxis(put[:, j:j + 1], 0),
                                                total[b][:, j, :], None, compute_op=ALU.add).then_inc(added, 16)

                gather(0, 0)
                gather(0, 1)

                def turn(pair):
                    for b in range(2):
                        g = 2 * pair + b
                        pool.wait_ge(h1_done, g + 1)
                        pool.wait_ge(ea_done, g + 1)
                        gather(pair + 1, b)
                        scatter(pair, b)

                turn(0)
                with pool.Fori(1, NGR // 2 - 1) as pair:
                    turn(pair)
                scatter(NGR // 2 - 1, 0)
                scatter(NGR // 2 - 1, 1)
                pool.wait_ge(added, 16 * NT)

            @block.vector
            def _(dve):
                def front(pair, b):
                    g = 2 * pair + b
                    dve.wait_ge(gathered[b], 16 * TPG * (pair + 1))
                    for j in range(TPG):
                        ins = nc.vector.bn_stats(stat[:, j, :], x1r[b][:, j, 0:D])
                    ins.then_inc(stats_done, 1)
                    dve.wait_ge(stats_done, g + 1)
                    waits_alone(dve, T)
                    for j in range(TPG):
                        ins = nc.vector.bn_aggr(mv[:, j, :], stat[:, j, :])
                    ins.then_inc(var_done, 1)
                    att = T["ea"][:, bass.ds(g * TPG, TPG), :]
                    a = x1r[b][:, :, D:D + 1]
                    nc.vector.tensor_tensor(ea[b][:, :, 0:4], att, a.broadcast_to([P, TPG, 4]), ALU.mult)
                    nc.vector.tensor_tensor(ea[b][:, :, 4:6], att[:, :, 1:3], a.broadcast_to([P, TPG, 2]),
                                            ALU.mult).then_inc(ea_done, 1)
                    dve.wait_ge(rows_loaded[b], 16 * (pair + 1))
                    if reused(pair):
                        dve.wait_ge(total_made, g - 1)
                    nc.vector.tensor_tensor(same[b][:, :, :], rows[b][:, :, :],
                                            bcast(T["idx"][:, 1, bass.ds(g * TPG, TPG)], 2, P),
                                            ALU.is_equal).then_inc(same_made, 1)
                    dve.wait_ge(std_done, g + 1)
                    dve.wait_ge(h1_done, g)
                    nc.vector.reciprocal(rstd[:, :], std[:, :]).then_inc(rstd_done, 1)
                    dve.wait_ge(rstd_done, g + 1)
                    nc.vector.scalar_tensor_tensor(shift[:, :], mv[:, :, 0], -1.0, rstd[:, :], ALU.mult,
                                                   ALU.mult).then_inc(shift_done, 1)
                    dve.wait_ge(sig_done, g + 1)
                    dve.wait_ge(fc_made, g)
                    nc.vector.tensor_tensor(hid[:, :], ps[3][0:64, 0:TPG * P], sig[:, :], ALU.mult).then_inc(silu_done, 1)

                def back(pair, b):
                    g = 2 * pair + b
                    e0 = ea[b][:, :, 0:1]
                    e1 = ea[b][:, :, 1:4]
                    f = fc[b]
                    v = hv[b]
                    comp = [P, TPG, 3, V0]
                    dve.wait_ge(fc_copied, g + 1)
                    dve.wait_ge(ext_done, g + 1)
                    dve.wait_ge(ea_done, g + 1)
                    dve.wait_ge(mid_turned, g)
                    tt = nc.vector.tensor_tensor
                    tt(ws[:, :, :, :], f[:, :, 0:128].rearrange("p t (k c) -> p t k c", k=2),
                       bcast(hs[b][:, :, :], 2, 2), ALU.mult).then_inc(mid_step, 1)
                    tt(w3e[:, :, :], f[:, :, 128:160], e0.broadcast_to([P, TPG, V0]), ALU.mult).then_inc(mid_step, 1)
                    tt(dots[:, :, :, :], v[:, :, 0:3, :], bcast(e1, 3, V0), ALU.mult).then_inc(mid_step, 1)
                    tt(cr1[:, :, :, :], v[:, :, 1:4, :], bcast(ea[b][:, :, 3:6], 3, V0), ALU.mult).then_inc(mid_step, 1)
                    tt(cr2[:, :, :, :], v[:, :, 2:5, :], bcast(ea[b][:, :, 2:5], 3, V0), ALU.mult).then_inc(mid_step, 1)
                    dve.wait_ge(mid_step, MID * g + 1)
                    tt(mid_s[:, :, 0:64], ws[:, :, 0, :], e0.broadcast_to([P, TPG, 64]), ALU.mult).then_inc(mid_step, 1)
                    tt(mid_v[:, :, :, 0:64], bcast(ws[:, :, 1, :], 2, 3), bcast(e1, 3, 64), ALU.mult).then_inc(mid_step, 1)
                    dve.wait_ge(mid_step, MID * g + 5)
                    tt(mid_v[:, :, :, 64:96], v[:, :, 0:3, :], bcast(w3e[:, :, :], 2, 3), ALU.mult).then_inc(mid_step, 1)
                    tt(dot[:, :, :], dots[:, :, 0, :], dots[:, :, 1, :], ALU.add).then_inc(mid_step, 1)
                    tt(cr1[:, :, :, :], cr1[:, :, :, :], cr2[:, :, :, :], ALU.subtract).then_inc(mid_step, 1)
                    dve.wait_ge(mid_step, MID * g + 9)
                    tt(dot[:, :, :], dot[:, :, :], dots[:, :, 2, :], ALU.add).then_inc(mid_step, 1)
                    dve.wait_ge(mid_step, MID * g + 11)
                    tt(mid_v[:, :, :, 96:128], cr1[:, :, :, :], bcast(f[:, :, 192:224], 2, 3), ALU.mult).then_inc(mid_step, 1)
                    tt(mid_s[:, :, 64:96], dot[:, :, :], f[:, :, 160:192], ALU.mult).then_inc(mid_done, 1)

                by_two(dve, NGR, front, back)

            @block.scalar
            def _(act):
                def front(pair, b):
                    g = 2 * pair + b
                    act.wait_ge(es_turned, g + 1)
                    act.wait_ge(hid_made, g)
                    nc.scalar.copy(esT[:, :], ps[0][0:64, 0:TPG * P]).then_inc(es_copied, 1)
                    act.wait_ge(var_done, g + 1)
                    act.wait_ge(rstd_done, g)
                    nc.scalar.activation(std[:, :], mv[:, :, 1], ACT.Sqrt, bias=T["eps"][:, 0:1]).then_inc(std_done, 1)
                    act.wait_ge(shift_done, g + 1)
                    act.wait_ge(h1_turned, g)
                    for j in range(TPG):
                        ins = nc.scalar.activation(h1[:, j, :], x1r[b][:, j, 0:D], ACT.Relu,
                                                   bias=shift[:, j:j + 1], scale=rstd[:, j:j + 1])
                    ins.then_inc(h1_done, 1)
                    act.wait_ge(hid_made, g + 1)
                    act.wait_ge(silu_done, g)
                    nc.scalar.activation(sig[:, :], ps[3][0:64, 0:TPG * P], ACT.Sigmoid).then_inc(sig_done, 1)
                    act.wait_ge(h1_turned, g + 1)
                    act.wait_ge(lin_made, g)
                    nc.scalar.copy(hT_s[:, :], ps[1][0:S0, 0:TPG * P])
                    nc.scalar.copy(hT_v[:, :], ps[2][0:VD, 0:TPG * P]).then_inc(h1_copied, 1)
                    if reused(pair):
                        act.wait_ge(mid_done, g - 1)
                    act.wait_ge(fc_made, g + 1)
                    for k in range(2):
                        ins = nc.scalar.copy(fc[b][:, 2 * k:2 * k + 2, :],
                                             ps[k][0:P, 0:448].rearrange("p (t c) -> p t c", t=2))
                    ins.then_inc(fc_copied, 1)
                    act.wait_ge(lin_made, g + 1)
                    for k in range(2):
                        o = ps[2 + k][0:P, 0:2 * D].rearrange("p (t c) -> p t c", t=2)
                        t2 = slice(2 * k, 2 * k + 2)
                        nc.scalar.copy(hs[b][:, t2, :], o[:, :, 0:S0])
                        ins = nc.scalar.copy(hv[b][:, t2, 0:3, :], o[:, :, S0:D].rearrange("p t (i c) -> p t i c", i=3))
                    for k in range(2):
                        o = ps[2 + k][0:P, 0:2 * D].rearrange("p (t c) -> p t c", t=2)
                        ins = nc.scalar.copy(hv[b][:, 2 * k:2 * k + 2, 3:5, :],
                                             o[:, :, S0:S0 + 64].rearrange("p t (i c) -> p t i c", i=2))
                    ins.then_inc(ext_done, 1)

                def back(pair, b):
                    g = 2 * pair + b
                    act.wait_ge(mid_turned, g + 1)
                    act.wait_ge(out_made, g)
                    nc.scalar.copy(mT_s[:, :], ps[4][0:96, 0:TPG * P])
                    for i in range(3):
                        ins = nc.scalar.copy(mT_v[:, i, :], ps[5 + i][:, 0:TPG * P])
                    ins.then_inc(mid_copied, 1)
                    act.wait_ge(out_made, g + 1)
                    act.wait_ge(total_made, g)
                    for k in range(2):
                        ins = nc.scalar.copy(out[:, 2 * k:2 * k + 2, :],
                                             ps[4 + k][0:P, 0:2 * AGW].rearrange("p (t c) -> p t c", t=2))
                    ins.then_inc(out_copied, 1)
                    act.wait_ge(total_made, g + 1)
                    if reused(pair):
                        act.wait_ge(added, 16 * TPG * (g - 1))
                    for k in range(2):
                        ins = nc.scalar.copy(total[b][:, 2 * k:2 * k + 2, :],
                                             ps[6 + k][0:P, 0:2 * AGW].rearrange("p (t c) -> p t c", t=2))
                    ins.then_inc(total_copied, 1)

                by_two(act, NGR, front, back)

            @block.tensor
            def _(pe):
                eye = T["ident"][0:P, 0:P]

                def front(pair, b):
                    g = 2 * pair + b
                    pe.wait_ge(es_loaded[b], 16 * (pair + 1))
                    pe.wait_ge(fc_copied, g)
                    waits_alone(pe, T)
                    for j in range(TPG):
                        ins = nc.tensor.transpose(ps[0][0:64, j * P:(j + 1) * P], es[b][:, j, :], eye)
                    ins.then_inc(es_turned, 1)
                    pe.wait_ge(es_copied, g + 1)
                    pe.wait_ge(ext_done, g)
                    waits_alone(pe, T)
                    nc.tensor.matmul(ps[3][0:64, 0:TPG * P], T["w_fc1"][:, :], esT[:, :], start=True,
                                     stop=True).then_inc(hid_made, 1)
                    pe.wait_ge(h1_done, g + 1)
                    for j in range(TPG):
                        nc.tensor.transpose(ps[2][0:VD, j * P:(j + 1) * P], h1[:, j, S0:D], eye)
                        ins = nc.tensor.transpose(ps[1][0:S0, j * P:(j + 1) * P], h1[:, j, 0:S0], eye)
                    ins.then_inc(h1_turned, 1)
                    pe.wait_ge(silu_done, g + 1)
                    pe.wait_ge(h1_copied, g + 1)
                    for j in range(TPG):
                        ins = nc.tensor.matmul(ps[j // 2][0:P, j % 2 * 224:j % 2 * 224 + 224], hid[:, j * P:(j + 1) * P],
                                               T["w_fc2"][:, :], start=True, stop=True)
                    ins.then_inc(fc_made, 1)
                    for j in range(TPG):
                        o, at = ps[2 + j // 2], j % 2 * D
                        nc.tensor.matmul(o[0:P, at:at + S0], hT_s[:, j * P:(j + 1) * P], T["w_in_s"][:, :],
                                         start=True, stop=True)
                        ins = nc.tensor.matmul(o[0:P, at + S0:at + D], hT_v[:, j * P:(j + 1) * P], T["w_in_v"][:, :],
                                               start=True, stop=True)
                    ins.then_inc(lin_made, 1)

                def back(pair, b):
                    g = 2 * pair + b
                    pe.wait_ge(mid_done, g + 1)
                    pe.wait_ge(total_copied, g)
                    for j in range(TPG):
                        nc.tensor.transpose(ps[4][0:96, j * P:(j + 1) * P], mid_s[:, j, :], eye)
                        for i in range(3):
                            ins = nc.tensor.transpose(ps[5 + i][:, j * P:(j + 1) * P], mid_v[:, j, i, :], eye)
                    ins.then_inc(mid_turned, 1)
                    pe.wait_ge(mid_copied, g + 1)
                    for j in range(TPG):
                        o, at = ps[4 + j // 2], j % 2 * AGW
                        nc.tensor.matmul(o[0:P, at:at + 96], mT_s[:, j * P:(j + 1) * P], T["w_out_s"][:, :],
                                         start=True, stop=True)
                        for i in range(3):
                            ins = nc.tensor.matmul(o[0:P, at + 96 + 32 * i:at + 128 + 32 * i],
                                                   mT_v[:, i, j * P:(j + 1) * P], T["w_out_v"][:, :], start=True, stop=True)
                    ins.then_inc(out_made, 1)
                    pe.wait_ge(out_copied, g + 1)
                    pe.wait_ge(same_made, g + 1)
                    for j in range(TPG):
                        ins = nc.tensor.matmul(ps[6 + j // 2][0:P, j % 2 * AGW:(j % 2 + 1) * AGW], same[b][:, j, :],
                                               out[:, j, :], start=True, stop=True)
                    ins.then_inc(total_made, 1)

                by_two(pe, NGR, front, back)


def stage_nodes1(nc, T, W, sem, N, DR, out):
    NPP = N // P
    NCH = NPP // RPC
    x1_v = DR["x1"][0:N, :].rearrange("(p n) d -> p (n d)", p=P)
    ag_v = DR["agg"][0:N, :].rearrange("(p n) d -> p (n d)", p=P)
    out_v = out.rearrange("(p n) d -> p (n d)", p=P)

    with ExitStack() as ctx:
        def sb(name, shape, dt=F32):
            return ctx.enter_context(nc.sbuf_tensor(name, shape, dt))

        def pb(name):
            return ctx.enter_context(nc.psum_tensor(name, [128, 512], F32))

        xt = [sb(f"n1_x{b}", [P, RPC, X1W]) for b in range(2)]
        ag = [sb(f"n1_ag{b}", [P, RPC, AGW]) for b in range(2)]
        ht = sb("n1_h", [P, RPC, D])
        pre = [sb(f"n1_pre{b}", [P, RPC, AGW]) for b in range(2)]
        gate = sb("n1_gate", [P, RPC, 96])
        res = [sb(f"n1_res{b}", [P, RPC, D]) for b in range(2)]
        stat = sb("n1_stat", [P, RPC, 6])
        mv = sb("n1_mv", [P, RPC, 2])
        std = sb("n1_std", [P, RPC])
        rstd = sb("n1_rstd", [P, RPC])
        shift = sb("n1_shift", [P, RPC])
        hT_s = [sb(f"n1_hTs{h}", [S0, 4 * P]) for h in range(2)]
        hT_v = [sb(f"n1_hTv{h}", [VD, 4 * P]) for h in range(2)]
        ps_s = [pb(f"n1_ps_s{h}") for h in range(2)]
        ps_v = [pb(f"n1_ps_v{h}") for h in range(2)]
        ps_o = [pb(f"n1_ps_o{q}") for q in range(4)]

        x_loaded = [sem(f"n1_x_loaded{b}") for b in range(2)]
        stored = [sem(f"n1_stored{b}") for b in range(2)]
        (stats_done, var_done, std_done, rstd_done, shift_done, h_done, hT_made, hT_copied, sc_made, pre_added,
         pre_scaled, gate_done, gated, summed) = (sem("n1_" + n) for n in (
             "stats_done", "var_done", "std_done", "rstd_done", "shift_done", "h_done", "hT_made", "hT_copied",
             "sc_made", "pre_added", "pre_scaled", "gate_done", "gated", "summed"))

        with nc.Block() as block:
            @block.sync
            def _(sp):
                def load(pair, b):
                    c = 2 * pair + b
                    if reused(pair):
                        sp.wait_ge(summed, c - 1)
                    sp.dma_start(xt[b][:, :, :].rearrange("p r d -> p (r d)"),
                                 x1_v[:, bass.ds(c * (RPC * X1W), RPC * X1W)]).then_inc(x_loaded[b], 16)
                    sp.dma_start(ag[b][:, :, :].rearrange("p r d -> p (r d)"),
                                 ag_v[:, bass.ds(c * (RPC * AGW), RPC * AGW)]).then_inc(x_loaded[b], 16)

                def store(pair, b):
                    c = 2 * pair + b
                    sp.wait_ge(summed, c + 1)
                    sp.dma_start(out_v[:, bass.ds(c * (RPC * D), RPC * D)],
                                 res[b][:, :, :].rearrange("p r d -> p (r d)")).then_inc(stored[b], 16)

                by_two(sp, NCH, load, store)
                for b in range(2):
                    sp.wait_ge(stored[b], 16 * (NCH // 2))

            @block.vector
            def _(dve):
                def normalise(pair, b):
                    c = 2 * pair + b
                    dve.wait_ge(x_loaded[b], 32 * (pair + 1))
                    for r in range(RPC):
                        ins = nc.vector.bn_stats(stat[:, r, :], xt[b][:, r, 0:D])
                    ins.then_inc(stats_done, 1)
                    dve.wait_ge(stats_done, c + 1)
                    waits_alone(dve, T)
                    for r in range(RPC):
                        ins = nc.vector.bn_aggr(mv[:, r, :], stat[:, r, :])
                    ins.then_inc(var_done, 1)
                    dve.wait_ge(std_done, c + 1)
                    dve.wait_ge(h_done, c)
                    nc.vector.reciprocal(rstd[:, :], std[:, :]).then_inc(rstd_done, 1)
                    dve.wait_ge(rstd_done, c + 1)
                    nc.vector.scalar_tensor_tensor(shift[:, :], mv[:, :, 0], -1.0, rstd[:, :], ALU.mult,
                                                   ALU.mult).then_inc(shift_done, 1)

                def combine(pair, b):
                    c = 2 * pair + b
                    for q in range(4):
                        dve.wait_ge(sc_made, 4 * c + q + 1)
                        r = slice(2 * q, 2 * q + 2)
                        if q == 0:
                            dve.wait_ge(gated, 2 * pair)
                        nc.vector.tensor_tensor(pre[b][:, r, :], ag[b][:, r, :],
                                                ps_o[q][0:P, 0:2 * AGW].rearrange("p (r d) -> p r d", r=2),
                                                ALU.add).then_inc(pre_added, 1)
                    dve.wait_ge(gate_done, c + 1)
                    dve.wait_ge(stored[b], 16 * pair)
                    nc.vector.tensor_tensor(res[b][:, :, 0:64], pre[b][:, :, 0:64], gate[:, :, 0:64], ALU.mult)
                    nc.vector.tensor_tensor(res[b][:, :, 64:160].rearrange("p r (w i) -> p r w i", i=3),
                                            pre[b][:, :, 96:192].rearrange("p r (i w) -> p r w i", i=3),
                                            bcast(gate[:, :, 64:96], 3, 3), ALU.mult).then_inc(gated, 1)

                by_two(dve, NCH, normalise, combine)

            @block.gpsimd
            def _(pool):
                def finish(pair, b):
                    c = 2 * pair + b
                    pool.wait_ge(pre_added, 4 * (c + 1))
                    nc.gpsimd.tensor_tensor(pre[b][:, :, :], pre[b][:, :, :],
                                            xt[b][:, :, D:D + 1].broadcast_to([P, RPC, AGW]), ALU.mult).then_inc(pre_scaled, 1)
                    pool.wait_ge(gated, c + 1)
                    nc.gpsimd.tensor_tensor(res[b][:, :, :], res[b][:, :, :], xt[b][:, :, 0:D],
                                            ALU.add).then_inc(summed, 1)

                with pool.Fori(0, NCH // 2) as pair:
                    finish(pair, 0)
                    finish(pair, 1)

            @block.scalar
            def _(act):
                def relu(pair, b):
                    c = 2 * pair + b
                    act.wait_ge(var_done, c + 1)
                    act.wait_ge(rstd_done, c)
                    nc.scalar.activation(std[:, :], mv[:, :, 1], ACT.Sqrt, bias=T["eps"][:, 0:1]).then_inc(std_done, 1)
                    act.wait_ge(shift_done, c + 1)
                    act.wait_ge(hT_made, 2 * c)
                    for r in range(RPC):
                        ins = nc.scalar.activation(ht[:, r, :], xt[b][:, r, 0:D], ACT.Relu,
                                                   bias=shift[:, r:r + 1], scale=rstd[:, r:r + 1])
                    ins.then_inc(h_done, 1)
                    for h in range(2):
                        act.wait_ge(hT_made, 2 * c + h + 1)
                        act.wait_ge(sc_made, 4 * c)
                        nc.scalar.copy(hT_s[h][:, :], ps_s[h][0:S0, 0:4 * P])
                        nc.scalar.copy(hT_v[h][:, :], ps_v[h][0:VD, 0:4 * P]).then_inc(hT_copied, 1)

                def sigmoid(pair, b):
                    c = 2 * pair + b
                    act.wait_ge(pre_scaled, c + 1)
                    act.wait_ge(gated, c)
                    nc.scalar.activation(gate[:, :, :], pre[b][:, :, 0:96], ACT.Sigmoid).then_inc(gate_done, 1)

                by_two(act, NCH, relu, sigmoid)

            @block.tensor
            def _(pe):
                def both(pair, b):
                    c = 2 * pair + b
                    pe.wait_ge(h_done, c + 1)
                    for h in range(2):
                        pe.wait_ge(hT_copied, 2 * c)
                        for r in range(4):
                            nc.tensor.transpose(ps_v[h][0:VD, r * P:(r + 1) * P], ht[:, 4 * h + r, S0:D],
                                                T["ident"][0:P, 0:P])
                            ins = nc.tensor.transpose(ps_s[h][0:S0, r * P:(r + 1) * P], ht[:, 4 * h + r, 0:S0],
                                                      T["ident"][0:P, 0:P])
                        ins.then_inc(hT_made, 1)
                    for q in range(4):
                        pe.wait_ge(hT_copied, 2 * c + q // 2 + 1)
                        pe.wait_ge(pre_added, 4 * c)
                        for r in range(2):
                            m = (2 * q + r) % 4 * P
                            nc.tensor.matmul(ps_o[q][0:P, r * AGW:r * AGW + 96], hT_s[q // 2][:, m:m + P],
                                             T["w_sc_s"][:, :], start=True, stop=True)
                            ins = nc.tensor.matmul(ps_o[q][0:P, r * AGW + 96:(r + 1) * AGW], hT_v[q // 2][:, m:m + P],
                                                   T["w_sc_v"][:, :], start=True, stop=True)
                        ins.then_inc(sc_made, 1)

                both(0, 0)
                both(0, 1)
                with pe.Fori(1, NCH // 2) as pair:
                    both(pair, 0)
                    both(pair, 1)


def gnn_kernel(nc, W, out):
    N, E = W["x"].shape[0], W["src"].shape[0]
    NT = E // P
    DR = {"h0": nc.dram_tensor("h0", [N, D], F32).ap(),
          "x1": nc.dram_tensor("x1", [N + P, X1W], F32).ap(),
          "agg": nc.dram_tensor("agg", [N + P, AGW], F32).ap()}
    shapes = {
        "ident": [128, 128], "earlier": [P, P], "spare": [P, 1], "eps": [P, 1], "a_all": [P, N // P],
        "ea": [P, NT, 4], "w_pair": [128, 40, 64], "w_vec": [128, V0, 2 * V0], "w_msg_s": [S0, 160],
        "w_msg_v": [VD, 2 * VD + 3 * S0], "w_lin_s": [S0, S0], "w_lin_v": [VD, VD], "eye_v": [VD, VD],
        "w_in_s": [S0, S0], "w_in_v": [VD, VD], "w_fc1": [64, 64], "w_fc2": [64, 224], "w_sc_s": [S0, 96],
        "w_sc_v": [VD, VD], "w_out_s": [96, 96], "w_out_v": [128, 32],
    }
    with ExitStack() as ctx:
        def sem(name):
            return ctx.enter_context(nc.semaphore(name))

        T = {"passed": sem("passed")}
        T |= {n: ctx.enter_context(nc.sbuf_tensor("t_" + n, s, F32)) for n, s in shapes.items()}
        T["idx"] = ctx.enter_context(nc.sbuf_tensor("t_idx", [P, 2, NT], I32))
        T["put"] = ctx.enter_context(nc.sbuf_tensor("t_put", [P, 2, NT], I32))
        stage_weights(nc, T, W, sem)
        stage_nodes0(nc, T, W, sem, N, NT, DR)
        stage_edges0(nc, T, W, sem, NT, DR)
        stage_edges1(nc, T, W, sem, NT, DR)
        stage_nodes1(nc, T, W, sem, N, DR, out)


def kernel(**inputs):
    import numpy as np
    import concourse.bacc as bacc
    from concourse.bass_utils import run_bass_kernel_spmd

    nc = bacc.Bacc("TRN2", target_bir_lowering=False, num_devices=1)
    a = {n.removeprefix("L0_gnn_").removeprefix("L1_gnn_"): np.asarray(v) for n, v in inputs.items()}
    N, E = a["x"].shape[0], a["src"].shape[0]
    a["Wu_sv"] = a["Wu_sv"].transpose(0, 2, 1)
    a["Wu_vs"] = a["Wu_vs"].transpose(1, 2, 0)
    a["src_rows"] = a["src"].reshape(P, E // P).T.reshape(-1)
    a["dst_rows"] = a["dst"].reshape(P, E // P).T.reshape(-1)
    a["ident"] = np.eye(128, dtype=np.float32)
    a["earlier"] = np.tril(np.ones((P, P), np.float32), -1)
    a["spare_x"] = (N + np.arange(P, dtype=np.float32)).reshape(P, 1)
    arrays, W = {}, {}
    for name, v in a.items():
        v = np.ascontiguousarray(v)
        arrays[f"in_{name}"] = v
        W[name] = nc.dram_tensor(f"in_{name}", v.shape, mybir.dt.from_np(v.dtype), kind="ExternalInput").ap()
    out = nc.dram_tensor("out", (N, D), F32, kind="ExternalOutput").ap()
    gnn_kernel(nc, W, out)
    r = run_bass_kernel_spmd(nc, [arrays], core_ids=[0])
    return r.results[0]["out"]
```

```python
from contextlib import ExitStack

import concourse.bass as bass
from concourse import mybir
import math

P = 125
F32 = mybir.dt.float32
I32 = mybir.dt.int32
ALU = mybir.AluOpType
ACT = mybir.ActivationFunctionType
AX = mybir.AxisListType
S0, V0, D = 64, 32, 160
VD = 3 * V0
X1W = D + 1
AGW = 96 + VD
RPC = 8
TPG = 4
EPS = 1e-5


def waits_alone(eng, T):
    eng.sem_inc(T["passed"], 1)


def bcast(ap, axis, n):
    ap = ap.unsqueeze(axis)
    shape = list(ap.shape)
    shape[axis] = n
    return ap.broadcast_to(shape)


def reused(pair):
    return not (isinstance(pair, int) and pair == 0)


def by_two(eng, n, first, second):
    half = n // 2
    first(0, 0)

    def turn(pair):
        first(pair, 1)
        second(pair, 0)
        first(pair + 1, 0)
        second(pair, 1)

    if half > 1:
        turn(0)
    if half > 2:
        with eng.Fori(1, half - 1) as pair:
            turn(pair)
    first(half - 1, 1)
    second(half - 1, 0)
    second(half - 1, 1)


def stage_weights(nc, T, W, sem):
    names = sorted(W)

    with nc.Block() as block:
        loaded, cleared, scaled, eye_added = (sem(n) for n in ("w_loaded", "w_cleared", "w_scaled", "w_eye"))
        loads = []

        def load(dst, src):
            loads.append((dst, src))

        load(T["ident"][:, :], W["ident"])
        load(T["halves"][0:S0, :], W["ident"][0:S0, 0:S0])
        load(T["halves"][S0:2 * S0, :], W["ident"][0:S0, 0:S0])
        load(T["earlier"][:, :], W["earlier"])
        load(T["spare"][:, 0:1], W["spare_x"])
        load(T["a_all"][:, :], W["node_vec1"].rearrange("(p n) o -> p (n o)", p=P))
        load(T["ea"][:, :, :], W["edge_attr_4"].rearrange("(p t) c -> p t c", p=P))
        load(T["idx"][:, 0, :], W["src"].rearrange("(p t) -> p t", p=P))
        load(T["idx"][:, 1, :], W["dst"].rearrange("(p t) -> p t", p=P))
        load(T["w_pair"][:, 0:32, :], W["Wu_ss"].rearrange("(c a) v w -> (a v) c w", a=2))
        load(T["w_pair"][:, 32:40, :], W["Wu_vv"].rearrange("(c a) v w -> (a v) c w", a=4))
        load(T["w_vec"][S0:2 * S0, :, 0:V0], W["Wu_sv"])
        load(T["w_vec"][0:S0, :, V0:2 * V0], W["Wu_vs"])
        load(T["w_msg_s"][:, 0:64], W["Wm_ss"])
        load(T["w_msg_s"][:, 64:128], W["Lm_s"])
        load(T["w_msg_s"][:, 128:160], W["Wm_sv"])
        load(T["w_lin_s"][:, :], W["Lu_s"])
        load(T["w_in_s"][:, :], W["lin1_ws"])
        load(T["w_fc1"][:, :], W["fc_w1"])
        load(T["w_fc2"][:, :], W["fc_w2"])
        load(T["w_sc_s"][:, :], W["sc_ws"])
        load(T["w_out_s"][:, :], W["lin2_ws"])
        load(T["w_out_v"][:, :], W["lin2_wv"])
        for dst, src, n in (("w_msg_v", "Wm_vs", 32), ("w_lin_v", "Lu_v", 32), ("w_in_v", "lin1_wv", 32),
                            ("w_sc_v", "sc_wv", 32)):
            for i in range(3):
                load(T[dst][i:VD:3, i * n:(i + 1) * n], W[src])
        for i in range(3):
            load(T["w_msg_v"][i:VD:3, VD + i * 32:VD + (i + 1) * 32], W["Lm_v"])
            load(T["w_msg_v"][i:VD:3, 2 * VD + i * 64:2 * VD + (i + 1) * 64], W["Wm_vv"])
            load(T["eye_v"][i:VD:3, i * 32:(i + 1) * 32], W["ident"][0:32, 0:32])

        clears = [T[n] for n in ("w_msg_v", "w_lin_v", "w_in_v", "w_sc_v", "eye_v")]
        r32 = 1 / math.sqrt(32)
        scales = [
            (T["w_pair"][:, 0:32, :], 1 / 64),
            (T["w_pair"][:, 32:40, :], 1 / math.sqrt(3) / 32),
            (T["w_vec"][:, :, :], 1 / math.sqrt(2048)),
            (T["w_msg_s"][:, :], 1 / 8),
            (T["w_msg_v"][:, 0:2 * VD], r32),
            (T["w_msg_v"][:, 2 * VD:2 * VD + 192], r32 / math.sqrt(3)),
            (T["w_lin_s"][:, :], 1 / 8),
            (T["w_lin_v"][:, :], r32),
            (T["w_in_s"][:, :], 1 / 8),
            (T["w_in_v"][:, :], r32),
            (T["w_fc1"][:, :], 1 / 8),
            (T["w_fc2"][:, :], 1 / 8),
            (T["w_sc_s"][:, :], 1 / 8),
            (T["w_sc_v"][:, :], r32),
            (T["w_out_s"][0:64, :], 1 / 4 / math.sqrt(96)),
            (T["w_out_s"][64:96, :], 1 / 4 / math.sqrt(96) / math.sqrt(3)),
            (T["w_out_v"][0:96, :], 1 / 4 / math.sqrt(128)),
            (T["w_out_v"][96:128, :], 1 / 4 / math.sqrt(128) / math.sqrt(2)),
        ]

        @block.sync
        def _(sp):
            sp.wait_ge(cleared, len(clears) + 2)
            for dst, src in loads:
                sp.dma_start(dst, src, allow_slow_non_contiguous=True).then_inc(loaded, 16)
            sp.wait_ge(loaded, 16 * len(loads))

        @block.vector
        def _(dve):
            for t in clears:
                nc.vector.memset(t[:, :], 0.0).then_inc(cleared, 1)
            nc.vector.memset(T["w_vec"][:, :, :], 0.0).then_inc(cleared, 1)
            nc.vector.memset(T["eps"][:, :], EPS).then_inc(cleared, 1)
            dve.wait_ge(scaled, len(scales))
            nc.vector.tensor_tensor(T["w_lin_s"][:, :], T["w_lin_s"][:, :], T["ident"][0:S0, 0:S0],
                                    ALU.add).then_inc(eye_added, 1)
            nc.vector.tensor_tensor(T["w_lin_v"][:, :], T["w_lin_v"][:, :], T["eye_v"][:, :],
                                    ALU.add).then_inc(eye_added, 1)
            dve.wait_ge(eye_added, 2)

        @block.scalar
        def _(act):
            act.wait_ge(loaded, 16 * len(loads))
            for ap, c in scales:
                nc.scalar.mul(ap, ap, c).then_inc(scaled, 1)
            act.wait_ge(scaled, len(scales))


def stage_nodes0(nc, T, W, sem, N, NT, DR):
    NPP = N // P
    NCH = NPP // RPC
    TPC = NT // NCH
    x_v = W["x"].rearrange("(p n) d -> p (n d)", p=P)
    h_v = DR["h0"].rearrange("(p n) d -> p (n d)", p=P)
    x1_v = DR["x1"][0:N, :].rearrange("(p n) d -> p (n d)", p=P)
    ag_v = DR["agg"][0:N, :].rearrange("(p n) d -> p (n d)", p=P)

    with ExitStack() as ctx:
        def sb(name, shape, dt=F32):
            return ctx.enter_context(nc.sbuf_tensor(name, shape, dt))

        def pb(name):
            return ctx.enter_context(nc.psum_tensor(name, [128, 512], F32))

        xt = [sb(f"n0_x{b}", [P, RPC, D]) for b in range(2)]
        ht = [sb(f"n0_h{b}", [P, RPC, D]) for b in range(2)]
        base = [sb(f"n0_base{b}", [P, RPC, X1W]) for b in range(2)]
        stat = sb("n0_stat", [P, RPC, 6])
        mv = sb("n0_mv", [P, RPC, 2])
        std = sb("n0_std", [P, RPC])
        rstd = [sb(f"n0_rstd{b}", [P, RPC]) for b in range(2)]
        shift = [sb(f"n0_shift{b}", [P, RPC]) for b in range(2)]
        hT_s = [sb(f"n0_hTs{h}", [S0, 4 * P]) for h in range(2)]
        hT_v = [sb(f"n0_hTv{h}", [VD, 4 * P]) for h in range(2)]
        zero = sb("n0_zero", [P, RPC * AGW])
        rows = [sb(f"n0_rows{b}", [P, 2, TPC, P], I32) for b in range(2)]
        same = sb("n0_same", [P, 2 * TPC, P])
        hit = sb("n0_hit", [P, 2 * TPC, P])
        rep = sb("n0_rep", [P, 2, NT])
        target = sb("n0_target", [P, 2, NT])
        toward = sb("n0_toward", [P, 2, NT])
        ps_s = [pb(f"n0_ps_s{h}") for h in range(2)]
        ps_v = [pb(f"n0_ps_v{h}") for h in range(2)]
        ps_o = [pb(f"n0_ps_o{q}") for q in range(4)]

        x_loaded = [sem(f"n0_x_loaded{b}") for b in range(2)]
        rows_loaded = [sem(f"n0_rows_loaded{b}") for b in range(2)]
        rows_used = [sem(f"n0_rows_used{b}") for b in range(2)]
        zeroed = sem("n0_zeroed")
        spare_stored = sem("n0_spare_stored")
        agg_cleared = sem("n0_agg_cleared")
        stats_done = sem("n0_stats_done")
        var_done = sem("n0_var_done")
        std_done = sem("n0_std_done")
        rstd_done = sem("n0_rstd_done")
        shift_done = sem("n0_shift_done")
        h_done = [sem(f"n0_h_done{b}") for b in range(2)]
        hT_made = sem("n0_hT_made")
        hT_copied = sem("n0_hT_copied")
        lin_made = sem("n0_lin_made")
        base_added = sem("n0_base_added")
        base_done = [sem(f"n0_base_done{b}") for b in range(2)]
        h_stored = [sem(f"n0_h_stored{b}") for b in range(2)]
        x1_stored = [sem(f"n0_x1_stored{b}") for b in range(2)]
        compared = sem("n0_compared")
        masked = sem("n0_masked")
        rep_done = sem("n0_rep_done")
        target_done = sem("n0_target_done")

        with nc.Block() as block:
            @block.sync
            def _(sp):
                sp.wait_ge(zeroed, 1)
                sp.dma_start(DR["x1"][N:N + P, :], zero[:, 0:X1W]).then_inc(spare_stored, 16)
                sp.dma_start(DR["agg"][N:N + P, :], zero[:, 0:AGW]).then_inc(spare_stored, 16)

                def load(pair, b):
                    c = 2 * pair + b
                    sp.wait_ge(base_done[b], pair)
                    sp.wait_ge(h_done[b], pair)
                    sp.dma_start(xt[b][:, :, :].rearrange("p r d -> p (r d)"),
                                 x_v[:, bass.ds(c * (RPC * D), RPC * D)]).then_inc(x_loaded[b], 16)
                    sp.wait_ge(rows_used[b], pair)
                    for k, name in enumerate(("src_rows", "dst_rows")):
                        row = W[name][bass.ds(c * (TPC * P), TPC * P)].partition_broadcast(P)
                        sp.dma_start(rows[b][:, k, :, :].rearrange("p t q -> p (t q)"), row).then_inc(rows_loaded[b], 16)

                def store(pair, b):
                    c = 2 * pair + b
                    sp.dma_start(ag_v[:, bass.ds(c * (RPC * AGW), RPC * AGW)], zero[:, :]).then_inc(agg_cleared, 16)
                    sp.wait_ge(h_done[b], pair + 1)
                    sp.dma_start(h_v[:, bass.ds(c * (RPC * D), RPC * D)],
                                 ht[b][:, :, :].rearrange("p r d -> p (r d)")).then_inc(h_stored[b], 16)
                    sp.wait_ge(base_done[b], pair + 1)
                    sp.dma_start(x1_v[:, bass.ds(c * (RPC * X1W), RPC * X1W)],
                                 base[b][:, :, :].rearrange("p r d -> p (r d)")).then_inc(x1_stored[b], 16)

                by_two(sp, NCH, load, store)
                sp.wait_ge(spare_stored, 32)
                sp.wait_ge(agg_cleared, 16 * NCH)
                for b in range(2):
                    sp.wait_ge(h_stored[b], 16 * (NCH // 2))
                    sp.wait_ge(x1_stored[b], 16 * (NCH // 2))

            @block.vector
            def _(dve):
                nc.vector.memset(zero[:, :], 0.0).then_inc(zeroed, 1)

                def normalise(pair, b):
                    c = 2 * pair + b
                    dve.wait_ge(x_loaded[b], 16 * (pair + 1))
                    for r in range(RPC):
                        ins = nc.vector.bn_stats(stat[:, r, :], xt[b][:, r, :])
                    ins.then_inc(stats_done, 1)
                    dve.wait_ge(stats_done, c + 1)
                    dve.wait_ge(std_done, c)
                    waits_alone(dve, T)
                    for r in range(RPC):
                        ins = nc.vector.bn_aggr(mv[:, r, :], stat[:, r, :])
                    ins.then_inc(var_done, 1)
                    repeats(pair, b)
                    dve.wait_ge(std_done, c + 1)
                    dve.wait_ge(h_done[b], pair)
                    nc.vector.reciprocal(rstd[b][:, :], std[:, :]).then_inc(rstd_done, 1)
                    dve.wait_ge(rstd_done, c + 1)
                    nc.vector.scalar_tensor_tensor(shift[b][:, :], mv[:, :, 0], -1.0, rstd[b][:, :], ALU.mult,
                                                   ALU.mult).then_inc(shift_done, 1)

                def repeats(pair, b):
                    c = 2 * pair + b
                    dve.wait_ge(rows_loaded[b], 32 * (pair + 1))
                    for k in range(2):
                        mine = T["idx"][:, k, bass.ds(c * TPC, TPC)]
                        ins = nc.vector.tensor_tensor(same[:, k * TPC:(k + 1) * TPC, :], rows[b][:, k, :, :],
                                                      bcast(mine, 2, P), ALU.is_equal)
                        if k == 1:
                            ins.then_inc(compared, 1)
                    dve.wait_ge(compared, c + 1)
                    nc.vector.tensor_tensor(hit[:, :, :], same[:, :, :], bcast(T["earlier"][:, :], 1, 2 * TPC),
                                            ALU.mult).then_inc(masked, 1)
                    dve.wait_ge(masked, c + 1)
                    nc.vector.tensor_reduce(rep[:, :, bass.ds(c * TPC, TPC)],
                                            hit[:, :, :].rearrange("p (k t) q -> p k t q", k=2), AX.X,
                                            ALU.max).then_inc(rows_used[b], 1)

                def add(pair, b):
                    c = 2 * pair + b
                    dve.wait_ge(x1_stored[b], 16 * pair)
                    for q in range(4):
                        dve.wait_ge(lin_made, 4 * c + q + 1)
                        o = ps_o[q][0:P, 0:2 * D].rearrange("p (r d) -> p r d", r=2)
                        r = slice(2 * q, 2 * q + 2)
                        nc.vector.tensor_tensor(base[b][:, r, 0:S0], xt[b][:, r, 0:S0], o[:, :, 0:S0], ALU.add)
                        ins = nc.vector.tensor_tensor(
                            base[b][:, r, S0:D].rearrange("p r (w i) -> p r w i", i=3),
                            xt[b][:, r, S0:D].rearrange("p r (w i) -> p r w i", i=3),
                            o[:, :, S0:D].rearrange("p r (i w) -> p r w i", i=3), ALU.add)
                        ins.then_inc(base_added, 1)
                    nc.vector.tensor_copy(base[b][:, :, D], T["a_all"][:, bass.ds(c * RPC, RPC)]).then_inc(base_done[b], 1)

                by_two(dve, NCH, normalise, add)
                nc.vector.tensor_copy(target[:, :, :], T["idx"][:, :, 0:NT]).then_inc(target_done, 1)
                dve.wait_ge(target_done, 1)
                flat = "p k t -> p (k t)"
                nc.vector.tensor_scalar(toward[:, :, :].rearrange(flat), target[:, :, :].rearrange(flat), -1.0,
                                        T["spare"][:, 0:1], ALU.mult, ALU.add).then_inc(target_done, 1)
                for b in range(2):
                    dve.wait_ge(rows_used[b], NCH // 2)
                dve.wait_ge(target_done, 2)
                nc.vector.tensor_tensor(toward[:, :, :].rearrange(flat), toward[:, :, :].rearrange(flat),
                                        rep[:, :, :].rearrange(flat), ALU.mult).then_inc(target_done, 1)
                dve.wait_ge(target_done, 3)
                nc.vector.tensor_tensor(T["put"][:, :, :].rearrange(flat), toward[:, :, :].rearrange(flat),
                                        target[:, :, :].rearrange(flat), ALU.add).then_inc(target_done, 1)
                dve.wait_ge(target_done, 4)

            @block.scalar
            def _(act):
                def relu(pair, b):
                    c = 2 * pair + b
                    act.wait_ge(var_done, c + 1)
                    act.wait_ge(shift_done, c)
                    nc.scalar.activation(std[:, :], mv[:, :, 1], ACT.Sqrt, bias=T["eps"][:, 0:1]).then_inc(std_done, 1)
                    act.wait_ge(shift_done, c + 1)
                    act.wait_ge(h_stored[b], 16 * pair)
                    for r in range(RPC):
                        ins = nc.scalar.activation(ht[b][:, r, :], xt[b][:, r, :], ACT.Relu,
                                                   bias=shift[b][:, r:r + 1], scale=rstd[b][:, r:r + 1])
                    ins.then_inc(h_done[b], 1)

                def copy(pair, b):
                    c = 2 * pair + b
                    for h in range(2):
                        act.wait_ge(hT_made, 2 * c + h + 1)
                        act.wait_ge(lin_made, 4 * c)
                        nc.scalar.copy(hT_s[h][:, :], ps_s[h][0:S0, 0:4 * P])
                        nc.scalar.copy(hT_v[h][:, :], ps_v[h][0:VD, 0:4 * P]).then_inc(hT_copied, 1)

                by_two(act, NCH, relu, copy)

            @block.tensor
            def _(pe):
                def turn(pair, b):
                    c = 2 * pair + b
                    pe.wait_ge(h_done[b], pair + 1)
                    for h in range(2):
                        pe.wait_ge(hT_copied, 2 * c)
                        for r in range(4):
                            nc.tensor.transpose(ps_v[h][0:VD, r * P:(r + 1) * P], ht[b][:, 4 * h + r, S0:D],
                                                T["ident"][0:P, 0:P])
                            ins = nc.tensor.transpose(ps_s[h][0:S0, r * P:(r + 1) * P], ht[b][:, 4 * h + r, 0:S0],
                                                      T["ident"][0:P, 0:P])
                        ins.then_inc(hT_made, 1)

                def linear(pair, b):
                    c = 2 * pair + b
                    for q in range(4):
                        pe.wait_ge(hT_copied, 2 * c + q // 2 + 1)
                        pe.wait_ge(base_added, 4 * c)
                        for r in range(2):
                            m = (2 * q + r) % 4 * P
                            nc.tensor.matmul(ps_o[q][0:P, r * D:r * D + S0], hT_s[q // 2][:, m:m + P],
                                             T["w_lin_s"][:, :], start=True, stop=True)
                            ins = nc.tensor.matmul(ps_o[q][0:P, r * D + S0:(r + 1) * D], hT_v[q // 2][:, m:m + P],
                                                   T["w_lin_v"][:, :], start=True, stop=True)
                        ins.then_inc(lin_made, 1)

                by_two(pe, NCH, turn, linear)


def stage_edges0(nc, T, W, sem, NT, DR):
    G_AD, G_BE, G_C, G_F = 0, D, 2 * D, 2 * D + V0
    NG = 14
    DS = 1
    PP = 4 - DS + 3
    MSG = 8
    FOLD_AT, Y2_AT, TOTAL_AT, Y3_AT, TURN_AT, PRODUCTS_AT = 1, 2, 5, 5, 8, 10

    with ExitStack() as ctx:
        def sb(name, shape, dt=F32):
            return ctx.enter_context(nc.sbuf_tensor(name, shape, dt))

        def pb(name):
            return ctx.enter_context(nc.psum_tensor(name, [128, 512], F32))

        h_dst = [sb(f"e0_h_dst{b}", [P, D]) for b in range(2)]
        own = [sb(f"e0_own{b}", [P, S0 + D]) for b in range(2)]
        vec = [sb(f"e0_vec{b}", [P, 3, 2 * V0]) for b in range(2)]
        hd_s = sb("e0_hd_s", [S0, P])
        hd_v = sb("e0_hd_v", [VD, P])
        gm = sb("e0_gm", [P, 2 * D + V0 + 3 * S0])
        sm = [sb(f"e0_sm{b}", [128, P]) for b in range(2)]
        pair_s = [sb(f"e0_pair_s{b}", [P, 4, 16, S0]) for b in range(2)]
        pair_v = [sb(f"e0_pair_v{b}", [P, 3, V0, V0]) for b in range(2)]
        pairT = [sb(f"e0_pairT{k}", [128, 4 * P]) for k in range(3)]
        sums = sb("e0_sums", [128, P])
        prod = [sb(f"e0_prod{k}", [P, 3, 8, 2 * V0]) for k in range(2)]
        upd = [sb(f"e0_upd{b}", [P, X1W]) for b in range(2)]
        total = [sb(f"e0_total{b}", [P, X1W]) for b in range(2)]
        rows = [sb(f"e0_rows{b}", [P, P], I32) for b in range(2)]
        same = [sb(f"e0_same{b}", [P, P]) for b in range(2)]
        ends = [sb(f"e0_ends{b}", [P, 2], I32) for b in range(2)]
        put = sb("e0_put", [P, 1], I32)
        ps_y = [pb(f"e0_ps_y{k}") for k in range(2)]
        ps_t = [pb(f"e0_ps_t{k}") for k in range(2)]
        ps_m, ps_u, ps_g, ps_f = pb("e0_ps_m"), pb("e0_ps_u"), pb("e0_ps_g"), pb("e0_ps_f")

        gathered = [sem(f"e0_gathered{b}") for b in range(2)]
        rows_loaded = [sem(f"e0_rows_loaded{b}") for b in range(2)]
        (same_made, hd_turned, hd_copied, gm_made, gm_copied, msg_step, vec_copied, sm_turned, sm_copied, dve_paired,
         pool_paired, pairs_turned, pairs_copied, pairs_summed, y_made, y_used, vec_summed, upd_cleared, upd_s_copied,
         total_made, total_copied, added, ends_copied, put_copied, sums_copied, folded) = (sem("e0_" + n) for n in (
             "same_made", "hd_turned", "hd_copied", "gm_made", "gm_copied", "msg_step", "vec_copied", "sm_turned",
             "sm_copied", "dve_paired", "pool_paired", "pairs_turned", "pairs_copied", "pairs_summed", "y_made",
             "y_used", "vec_summed", "upd_cleared", "upd_s_copied", "total_made", "total_copied", "added",
             "ends_copied", "put_copied", "sums_copied", "folded"))

        def pipeline(eng, step):
            step(None, None, None, (0, 0))
            step(None, None, (0, 0), (0, 1))
            step(None, (0, 0), (0, 1), (1, 0))
            step((0, 0), (0, 1), (1, 0), (1, 1))
            with eng.Fori(1, NT // 2 - 1) as pair:
                step((pair - 1, 1), (pair, 0), (pair, 1), (pair + 1, 0))
                step((pair, 0), (pair, 1), (pair + 1, 0), (pair + 1, 1))
            last = NT // 2 - 1
            step((last - 1, 1), (last, 0), (last, 1), None)
            step((last, 0), (last, 1), None, None)
            step((last, 1), None, None, None)

        with nc.Block() as block:
            @block.sync
            def _(sp):
                def rows_of(pair, b):
                    t = 2 * pair + b
                    sp.dma_start(rows[b][:, :],
                                 W["src_rows"][bass.ds(t * P, P)].partition_broadcast(P)).then_inc(rows_loaded[b], 16)

                rows_of(0, 0)
                rows_of(0, 1)
                with sp.Fori(0, NT // 2 - 1) as pair:
                    for b in range(2):
                        sp.wait_ge(same_made, 2 * pair + b + 1)
                        rows_of(pair + 1, b)

            @block.gpsimd
            def _(pool):
                def gather(pair, b):
                    t = 2 * pair + b
                    if reused(pair):
                        pool.wait_ge(hd_turned, t - 1)
                        pool.wait_ge(sm_turned, t - 1)
                        pool.wait_ge(dve_paired, DS * (t - 1))
                        pool.wait_ge(pool_paired, PP * (t - 1))
                        pool.wait_ge(vec_copied, t - 1)
                    waits_alone(pool, T)
                    nc.gpsimd.tensor_copy(ends[b][:, :], T["idx"][:, :, bass.ds(t, 1)].squeeze(2)).then_inc(ends_copied, 1)
                    pool.wait_ge(ends_copied, t + 1)
                    waits_alone(pool, T)
                    pool.indirect_dma_start(h_dst[b][:, :], None, DR["h0"],
                                            bass.IndirectOffsetOnAxis(ends[b][:, 1:2], 0)).then_inc(gathered[b], 16)
                    pool.indirect_dma_start(own[b][:, S0:S0 + D], None, DR["h0"],
                                            bass.IndirectOffsetOnAxis(ends[b][:, 0:1], 0)).then_inc(gathered[b], 16)

                def copy_vec(pair, b):
                    t = 2 * pair + b
                    pool.wait_ge(gathered[b], 32 * (pair + 1))
                    if reused(pair):
                        pool.wait_ge(vec_summed, 4 * (t - 1))
                    waits_alone(pool, T)
                    nc.gpsimd.tensor_copy(vec[b][:, :, V0:2 * V0],
                                          own[b][:, 2 * S0:S0 + D].rearrange("p (u i) -> p i u", i=3)).then_inc(vec_copied, 1)

                def pairs_scalar(pair, b):
                    t = 2 * pair + b
                    pool.wait_ge(msg_step, MSG * (t + 1))
                    if reused(pair):
                        pool.wait_ge(pairs_turned, NG * (t - 1))
                    for k in range(DS, 4):
                        nc.gpsimd.tensor_tensor(pair_s[b][:, k, :, :], bcast(own[b][:, S0 + 16 * k:S0 + 16 * (k + 1)], 2, S0),
                                                bcast(own[b][:, 0:S0], 1, 16), ALU.mult).then_inc(pool_paired, 1)

                def pairs_vector(pair, b):
                    pool.wait_ge(vec_copied, 2 * pair + b + 1)
                    for i in range(3):
                        nc.gpsimd.tensor_tensor(pair_v[b][:, i, :, :], bcast(vec[b][:, i, V0:2 * V0], 2, V0),
                                                bcast(vec[b][:, i, 0:V0], 1, V0), ALU.mult).then_inc(pool_paired, 1)

                def scatter(pair, b):
                    t = 2 * pair + b
                    pool.wait_ge(added, 16 * t)
                    waits_alone(pool, T)
                    nc.gpsimd.tensor_copy(put[:, :], T["put"][:, 0, bass.ds(t, 1)]).then_inc(put_copied, 1)
                    pool.wait_ge(put_copied, t + 1)
                    pool.wait_ge(total_copied, t + 1)
                    waits_alone(pool, T)
                    pool.indirect_dma_start(DR["x1"], bass.IndirectOffsetOnAxis(put[:, 0:1], 0),
                                            total[b][:, :], None, compute_op=ALU.add).then_inc(added, 16)

                def step(before, this, after, after2):
                    if after:
                        copy_vec(*after)
                        pairs_scalar(*after)
                    if after2:
                        gather(*after2)
                    if after:
                        pairs_vector(*after)
                    if before:
                        scatter(*before)

                pipeline(pool, step)
                pool.wait_ge(added, 16 * NT)

            @block.vector
            def _(dve):
                for b in range(2):
                    nc.vector.memset(upd[b][:, :], 0.0).then_inc(upd_cleared, 1)

                def message(pair, b):
                    t = 2 * pair + b
                    dve.wait_ge(gm_copied, t + 1)
                    dve.wait_ge(vec_copied, t + 1)
                    m0 = own[b][:, 0:S0]
                    m1 = vec[b][:, :, 0:V0]
                    dist = T["ea"][:, bass.ds(t, 1), 3]
                    nc.vector.scalar_tensor_tensor(m0, gm[:, G_AD:G_AD + S0], dist, gm[:, G_BE:G_BE + S0], ALU.mult,
                                                   ALU.add).then_inc(msg_step, 1)
                    nc.vector.scalar_tensor_tensor(
                        m1, gm[:, G_AD + S0:G_AD + D].rearrange("p (i w) -> p i w", i=3), dist,
                        gm[:, G_BE + S0:G_BE + D].rearrange("p (i w) -> p i w", i=3), ALU.mult,
                        ALU.add).then_inc(msg_step, 1)
                    for i in range(3):
                        r = T["ea"][:, bass.ds(t, 1), i]
                        dve.wait_ge(msg_step, MSG * t + 2 * i + 1)
                        nc.vector.scalar_tensor_tensor(m0, gm[:, G_F + i * S0:G_F + (i + 1) * S0], r, m0, ALU.mult,
                                                       ALU.add).then_inc(msg_step, 1)
                        dve.wait_ge(msg_step, MSG * t + 2)
                        nc.vector.scalar_tensor_tensor(m1[:, i, :], gm[:, G_C:G_C + V0], r, m1[:, i, :], ALU.mult,
                                                       ALU.add).then_inc(msg_step, 1)

                def pairs_scalar(pair, b):
                    t = 2 * pair + b
                    dve.wait_ge(msg_step, MSG * (t + 1))
                    if reused(pair):
                        dve.wait_ge(pairs_turned, NG * (t - 1))
                    for k in range(DS):
                        nc.vector.tensor_tensor(pair_s[b][:, k, :, :], bcast(own[b][:, S0 + 16 * k:S0 + 16 * (k + 1)], 2, S0),
                                                bcast(own[b][:, 0:S0], 1, 16), ALU.mult).then_inc(dve_paired, 1)

                def update_vector(pair, b):
                    t = 2 * pair + b
                    if reused(pair):
                        dve.wait_ge(total_made, t - 1)
                    dve.wait_ge(rows_loaded[b], 16 * (pair + 1))
                    nc.vector.tensor_tensor(same[b][:, :], rows[b][:, :],
                                            T["idx"][:, 0, bass.ds(t, 1)].broadcast_to([P, P]),
                                            ALU.is_equal).then_inc(same_made, 1)

                    def multiply(q):
                        dve.wait_ge(y_made, 4 * t + q + 1)
                        if q >= 2:
                            dve.wait_ge(vec_summed, 4 * t + q - 1)
                        y = ps_y[q % 2][0:P, :].rearrange("p (w c) -> p w c", c=2 * V0)
                        nc.vector.tensor_tensor(prod[q % 2][:, :, :, :], bcast(y, 1, 3), bcast(vec[b][:, :, :], 2, 8),
                                                ALU.mult).then_inc(y_used, 1)

                    def reduce(q):
                        dve.wait_ge(y_used, 4 * t + q + 1)
                        out = upd[b][:, S0 + 24 * q:S0 + 24 * (q + 1)].rearrange("p (w i) -> p i w", i=3)
                        nc.vector.tensor_reduce(out, prod[q % 2][:, :, :, :], AX.X, ALU.add).then_inc(vec_summed, 1)

                    dve.wait_ge(vec_summed, 4 * t)
                    multiply(0)
                    multiply(1)
                    reduce(0)
                    multiply(2)
                    reduce(1)
                    multiply(3)
                    reduce(2)
                    reduce(3)

                def step(before, this, after, after2):
                    if after:
                        message(*after)
                        pairs_scalar(*after)
                    if this:
                        update_vector(*this)

                dve.wait_ge(upd_cleared, 2)
                pipeline(dve, step)

            @block.scalar
            def _(act):
                def copy_sm(pair, b):
                    t = 2 * pair + b
                    act.wait_ge(sm_turned, t + 1)
                    if reused(pair):
                        act.wait_ge(y_made, 4 * (t - 1))
                    nc.scalar.copy(sm[b][:, :], ps_m[:, 0:P]).then_inc(sm_copied, 1)

                def copy_hd(pair, b):
                    t = 2 * pair + b
                    act.wait_ge(hd_turned, t + 1)
                    act.wait_ge(gm_made, t)
                    nc.scalar.copy(hd_s[:, :], ps_f[0:S0, 2 * P:3 * P])
                    nc.scalar.copy(hd_v[:, :], ps_f[0:VD, 3 * P:4 * P]).then_inc(hd_copied, 1)

                def copy_gm(pair, b):
                    t = 2 * pair + b
                    act.wait_ge(gm_made, t + 1)
                    act.wait_ge(msg_step, MSG * t)
                    nc.scalar.copy(gm[:, 0:2 * D], ps_g[0:P, 0:2 * D])
                    nc.scalar.copy(gm[:, 2 * D:], ps_f[0:P, 0:V0 + 3 * S0]).then_inc(gm_copied, 1)

                def copy_pairs(pair, b, g):
                    t = 2 * pair + b
                    act.wait_ge(pairs_turned, NG * t + g + 1)
                    act.wait_ge(pairs_summed, NG * t + (g - 2 if g >= 3 else 0))
                    nc.scalar.copy(pairT[g % 3][:, :], ps_t[g % 2][:, 0:4 * P]).then_inc(pairs_copied, 1)

                def copy_update(pair, b):
                    t = 2 * pair + b
                    act.wait_ge(folded, t + 1)
                    if reused(pair):
                        act.wait_ge(total_made, t - 1)
                    nc.scalar.copy(upd[b][:, 0:S0], ps_m[0:P, 2 * P:2 * P + S0]).then_inc(upd_s_copied, 1)

                def copy_sums(pair, b):
                    t = 2 * pair + b
                    act.wait_ge(pairs_summed, NG * (t + 1))
                    act.wait_ge(folded, t)
                    nc.scalar.copy(sums[:, :], ps_u[:, 0:P]).then_inc(sums_copied, 1)

                def copy_total(pair, b):
                    t = 2 * pair + b
                    act.wait_ge(total_made, t + 1)
                    if reused(pair):
                        act.wait_ge(added, 16 * (t - 1))
                    nc.scalar.copy(total[b][:, :], ps_g[0:P, 0:X1W]).then_inc(total_copied, 1)

                def step(before, this, after, after2):
                    if after:
                        copy_sm(*after)
                    for g in range(NG):
                        if after:
                            copy_pairs(*after, g)
                        if g == FOLD_AT and this:
                            copy_update(*this)
                        if g == TOTAL_AT and before:
                            copy_total(*before)
                        if g == TURN_AT and after2:
                            copy_hd(*after2)
                        if g == PRODUCTS_AT and after2:
                            copy_gm(*after2)
                    if after:
                        copy_sums(*after)

                act.wait_ge(upd_cleared, 2)
                pipeline(act, step)

            @block.tensor
            def _(pe):
                eye = T["ident"][0:P, 0:P]

                def turn_sm(pair, b):
                    t = 2 * pair + b
                    pe.wait_ge(msg_step, MSG * (t + 1))
                    if reused(pair):
                        pe.wait_ge(upd_s_copied, t - 1)
                    pe.wait_ge(sm_copied, t)
                    nc.tensor.transpose(ps_m[:, 0:P], own[b][:, 0:2 * S0], eye).then_inc(sm_turned, 1)

                def turn_hd(pair, b):
                    t = 2 * pair + b
                    pe.wait_ge(gathered[b], 32 * (pair + 1))
                    pe.wait_ge(gm_copied, t)
                    nc.tensor.transpose(ps_f[0:VD, 3 * P:4 * P], h_dst[b][:, S0:D], eye)
                    nc.tensor.transpose(ps_f[0:S0, 2 * P:3 * P], h_dst[b][:, 0:S0], eye).then_inc(hd_turned, 1)

                def message_products(pair, b):
                    t = 2 * pair + b
                    pe.wait_ge(hd_copied, t + 1)
                    mv = T["w_msg_v"]
                    for out, x, w in ((ps_g[0:P, 0:S0], hd_s, T["w_msg_s"][:, 0:S0]),
                                      (ps_g[0:P, S0:D], hd_v, mv[:, 0:VD]),
                                      (ps_g[0:P, D:D + S0], hd_s, T["w_msg_s"][:, S0:2 * S0]),
                                      (ps_g[0:P, D + S0:2 * D], hd_v, mv[:, VD:2 * VD]),
                                      (ps_f[0:P, 0:V0], hd_s, T["w_msg_s"][:, 2 * S0:2 * S0 + V0]),
                                      (ps_f[0:P, V0:V0 + 3 * S0], hd_v, mv[:, 2 * VD:])):
                        ins = nc.tensor.matmul(out, x[:, :], w, start=True, stop=True)
                    ins.then_inc(gm_made, 1)

                def vector_weights(pair, b, q):
                    t = 2 * pair + b
                    pe.wait_ge(sm_copied, t + 1)
                    pe.wait_ge(y_used, 4 * t + (q - 1 if q >= 2 else 0))
                    nc.tensor.matmul(ps_y[q % 2][0:P, :], sm[b][:, 0:P],
                                     T["w_vec"][:, 8 * q:8 * (q + 1), :].rearrange("p w c -> p (w c)"),
                                     start=True, stop=True).then_inc(y_made, 1)

                def turn_pairs(pair, b, g):
                    t = 2 * pair + b
                    if g % 2 == 0:
                        if g < 2 * DS:
                            pe.wait_ge(dve_paired, DS * t + g // 2 + 1)
                        else:
                            pe.wait_ge(pool_paired, PP * t + g // 2 - DS + 1)
                    if g >= 2:
                        pe.wait_ge(pairs_copied, NG * t + g - 1)
                    for n in range(4):
                        c = 4 * g + n
                        if c < 32:
                            x = pair_s[b][:, c // 8, 2 * (c % 8):2 * (c % 8) + 2, :].rearrange("p u v -> p (u v)")
                        else:
                            i, c8 = divmod(c - 32, 8)
                            x = pair_v[b][:, i, 4 * c8:4 * c8 + 4, :].rearrange("p u v -> p (u v)")
                        ins = nc.tensor.transpose(ps_t[g % 2][:, n * P:(n + 1) * P], x, eye)
                    ins.then_inc(pairs_turned, 1)

                def sum_pairs(pair, b, g):
                    t = 2 * pair + b
                    pe.wait_ge(pairs_copied, NG * t + g + 1)
                    if g == 0:
                        pe.wait_ge(sums_copied, t)
                    for n in range(4):
                        c, half = 4 * g + n, n % 2 * S0
                        w = T["w_pair"][:, c if c < 32 else 32 + (c - 32) % 8, :]
                        ins = nc.tensor.matmul(ps_u[half:half + S0, 0:P], w, pairT[g % 3][:, n * P:(n + 1) * P],
                                               start=(c < 2), stop=(c >= 4 * NG - 2))
                    ins.then_inc(pairs_summed, 1)

                def fold(pair, b):
                    t = 2 * pair + b
                    pe.wait_ge(sums_copied, t + 1)
                    nc.tensor.matmul(ps_m[0:P, 2 * P:2 * P + S0], sums[:, :], T["halves"][:, :], start=True,
                                     stop=True).then_inc(folded, 1)

                def sum_tile(pair, b):
                    t = 2 * pair + b
                    pe.wait_ge(total_copied, t)
                    pe.wait_ge(upd_s_copied, t + 1)
                    pe.wait_ge(vec_summed, 4 * (t + 1))
                    pe.wait_ge(same_made, t + 1)
                    nc.tensor.matmul(ps_g[0:P, 0:X1W], same[b][:, :], upd[b][:, :], start=True, stop=True).then_inc(total_made, 1)

                def step(before, this, after, after2):
                    if this:
                        vector_weights(*this, 0)
                        vector_weights(*this, 1)
                    if after:
                        turn_sm(*after)
                    for g in range(NG + 2):
                        if after:
                            if g < NG:
                                turn_pairs(*after, g)
                            if g >= 2:
                                sum_pairs(*after, g - 2)
                        if g == FOLD_AT and this:
                            if after:
                                pe.wait_ge(sm_copied, 2 * after[0] + after[1] + 1)
                            fold(*this)
                        if g == Y2_AT and this:
                            vector_weights(*this, 2)
                        if g == TOTAL_AT and before:
                            pe.wait_ge(gm_copied, 2 * after[0] + after[1] + 1 if after else NT)
                            sum_tile(*before)
                        if g == Y3_AT and this:
                            vector_weights(*this, 3)
                        if g == TURN_AT and after2:
                            turn_hd(*after2)
                        if g == PRODUCTS_AT and after2:
                            if before:
                                pe.wait_ge(total_copied, 2 * before[0] + before[1] + 1)
                            message_products(*after2)

                pipeline(pe, step)


def stage_edges1(nc, T, W, sem, NT, DR):
    NGR = NT // TPG
    es_v = W["edge_attr_64"].rearrange("(p t) c -> p (t c)", p=P)

    with ExitStack() as ctx:
        def sb(name, shape, dt=F32):
            return ctx.enter_context(nc.sbuf_tensor(name, shape, dt))

        ps = [ctx.enter_context(nc.psum_tensor(f"e1_ps{k}", [128, 512], F32)) for k in range(8)]
        es = [sb(f"e1_es{b}", [P, TPG, 64]) for b in range(2)]
        rows = [sb(f"e1_rows{b}", [P, TPG, P], I32) for b in range(2)]
        x1r = [sb(f"e1_x1r{b}", [P, TPG, X1W]) for b in range(2)]
        stat = sb("e1_stat", [P, TPG, 6])
        mv = sb("e1_mv", [P, TPG, 2])
        std = sb("e1_std", [P, TPG])
        rstd = sb("e1_rstd", [P, TPG])
        shift = sb("e1_shift", [P, TPG])
        h1 = sb("e1_h1", [P, TPG, D])
        esT = sb("e1_esT", [64, TPG * P])
        sig = sb("e1_sig", [64, TPG * P])
        hid = sb("e1_hid", [64, TPG * P])
        hT_s = sb("e1_hT_s", [S0, TPG * P])
        hT_v = sb("e1_hT_v", [VD, TPG * P])
        fc = [sb(f"e1_fc{b}", [P, TPG, 224]) for b in range(2)]
        hs = [sb(f"e1_hs{b}", [P, TPG, S0]) for b in range(2)]
        hv = [sb(f"e1_hv{b}", [P, TPG, 5, V0]) for b in range(2)]
        ea = [sb(f"e1_ea{b}", [P, TPG, 6]) for b in range(2)]
        ws = sb("e1_ws", [P, TPG, 2, 64])
        w3e = sb("e1_w3e", [P, TPG, V0])
        dots = sb("e1_dots", [P, TPG, 3, V0])
        dot = sb("e1_dot", [P, TPG, V0])
        cr1 = sb("e1_cr1", [P, TPG, 3, V0])
        cr2 = sb("e1_cr2", [P, TPG, 3, V0])
        mid_s = sb("e1_mid_s", [P, TPG, 96])
        mid_v = sb("e1_mid_v", [P, TPG, 3, 128])
        mT_s = sb("e1_mT_s", [96, TPG * P])
        mT_v = sb("e1_mT_v", [128, 3, TPG * P])
        out = sb("e1_out", [P, TPG, AGW])
        total = [sb(f"e1_total{b}", [P, TPG, AGW]) for b in range(2)]
        same = [sb(f"e1_same{b}", [P, TPG, P]) for b in range(2)]

        starts = [sb(f"e1_starts{b}", [P, TPG], I32) for b in range(2)]
        put = sb("e1_put", [P, TPG], I32)
        starts_copied, put_copied = sem("e1_starts_copied"), sem("e1_put_copied")
        es_loaded = [sem(f"e1_es_loaded{b}") for b in range(2)]
        rows_loaded = [sem(f"e1_rows_loaded{b}") for b in range(2)]
        gathered = [sem(f"e1_gathered{b}") for b in range(2)]
        (stats_done, var_done, std_done, rstd_done, shift_done, h1_done, ea_done, same_made, es_turned, es_copied,
         h1_turned, h1_copied, hid_made, sig_done, silu_done, fc_made, fc_copied, lin_made, lin_copied, ext_done,
         mid_step, mid_done, mid_turned, mid_copied, out_made, out_copied, total_made, total_copied, added) = (
            sem("e1_" + n) for n in (
                "stats_done", "var_done", "std_done", "rstd_done", "shift_done", "h1_done", "ea_done", "same_made",
                "es_turned", "es_copied", "h1_turned", "h1_copied", "hid_made", "sig_done", "silu_done", "fc_made",
                "fc_copied", "lin_made", "lin_copied", "ext_done", "mid_step", "mid_done", "mid_turned", "mid_copied",
                "out_made", "out_copied", "total_made", "total_copied", "added"))
        MID = 12

        with nc.Block() as block:
            @block.sync
            def _(sp):
                def load(pair, b):
                    g = 2 * pair + b
                    sp.dma_start(es[b][:, :, :].rearrange("p t c -> p (t c)"),
                                 es_v[:, bass.ds(g * (TPG * 64), TPG * 64)]).then_inc(es_loaded[b], 16)
                    sp.dma_start(rows[b][:, :, :].rearrange("p t q -> p (t q)"),
                                 W["dst_rows"][bass.ds(g * (TPG * P), TPG * P)].partition_broadcast(P)).then_inc(rows_loaded[b], 16)

                def freed(pair, b):
                    g = 2 * pair + b
                    sp.wait_ge(es_turned, g + 1)
                    sp.wait_ge(same_made, g + 1)

                load(0, 0)
                load(0, 1)
                with sp.Fori(0, NGR // 2 - 1) as pair:
                    for b in range(2):
                        freed(pair, b)
                        load(pair + 1, b)

            @block.gpsimd
            def _(pool):
                def gather(pair, b):
                    g = 2 * pair + b
                    waits_alone(pool, T)
                    nc.gpsimd.tensor_copy(starts[b][:, :], T["idx"][:, 0, bass.ds(g * TPG, TPG)]).then_inc(starts_copied, 1)
                    pool.wait_ge(starts_copied, g + 1)
                    for j in range(TPG):
                        waits_alone(pool, T)
                        pool.indirect_dma_start(x1r[b][:, j, :], None, DR["x1"],
                                                bass.IndirectOffsetOnAxis(starts[b][:, j:j + 1], 0)).then_inc(gathered[b], 16)

                def scatter(pair, b):
                    g = 2 * pair + b
                    pool.wait_ge(added, 16 * TPG * g)
                    waits_alone(pool, T)
                    nc.gpsimd.tensor_copy(put[:, :], T["put"][:, 1, bass.ds(g * TPG, TPG)]).then_inc(put_copied, 1)
                    pool.wait_ge(put_copied, g + 1)
                    pool.wait_ge(total_copied, g + 1)
                    for j in range(TPG):
                        pool.wait_ge(added, 16 * (g * TPG + j))
                        waits_alone(pool, T)
                        pool.indirect_dma_start(DR["agg"],
                                                bass.IndirectOffsetOnAxis(put[:, j:j + 1], 0),
                                                total[b][:, j, :], None, compute_op=ALU.add).then_inc(added, 16)

                gather(0, 0)
                gather(0, 1)

                def turn(pair):
                    for b in range(2):
                        g = 2 * pair + b
                        pool.wait_ge(h1_done, g + 1)
                        pool.wait_ge(ea_done, g + 1)
                        gather(pair + 1, b)
                        scatter(pair, b)

                turn(0)
                with pool.Fori(1, NGR // 2 - 1) as pair:
                    turn(pair)
                scatter(NGR // 2 - 1, 0)
                scatter(NGR // 2 - 1, 1)
                pool.wait_ge(added, 16 * NT)

            @block.vector
            def _(dve):
                def front(pair, b):
                    g = 2 * pair + b
                    dve.wait_ge(gathered[b], 16 * TPG * (pair + 1))
                    for j in range(TPG):
                        ins = nc.vector.bn_stats(stat[:, j, :], x1r[b][:, j, 0:D])
                    ins.then_inc(stats_done, 1)
                    dve.wait_ge(stats_done, g + 1)
                    waits_alone(dve, T)
                    for j in range(TPG):
                        ins = nc.vector.bn_aggr(mv[:, j, :], stat[:, j, :])
                    ins.then_inc(var_done, 1)
                    att = T["ea"][:, bass.ds(g * TPG, TPG), :]
                    a = x1r[b][:, :, D:D + 1]
                    nc.vector.tensor_tensor(ea[b][:, :, 0:4], att, a.broadcast_to([P, TPG, 4]), ALU.mult)
                    nc.vector.tensor_tensor(ea[b][:, :, 4:6], att[:, :, 1:3], a.broadcast_to([P, TPG, 2]),
                                            ALU.mult).then_inc(ea_done, 1)
                    dve.wait_ge(rows_loaded[b], 16 * (pair + 1))
                    if reused(pair):
                        dve.wait_ge(total_made, g - 1)
                    nc.vector.tensor_tensor(same[b][:, :, :], rows[b][:, :, :],
                                            bcast(T["idx"][:, 1, bass.ds(g * TPG, TPG)], 2, P),
                                            ALU.is_equal).then_inc(same_made, 1)
                    dve.wait_ge(std_done, g + 1)
                    dve.wait_ge(h1_done, g)
                    nc.vector.reciprocal(rstd[:, :], std[:, :]).then_inc(rstd_done, 1)
                    dve.wait_ge(rstd_done, g + 1)
                    nc.vector.scalar_tensor_tensor(shift[:, :], mv[:, :, 0], -1.0, rstd[:, :], ALU.mult,
                                                   ALU.mult).then_inc(shift_done, 1)
                    dve.wait_ge(sig_done, g + 1)
                    dve.wait_ge(fc_made, g)
                    nc.vector.tensor_tensor(hid[:, :], ps[3][0:64, 0:TPG * P], sig[:, :], ALU.mult).then_inc(silu_done, 1)

                def back(pair, b):
                    g = 2 * pair + b
                    e0 = ea[b][:, :, 0:1]
                    e1 = ea[b][:, :, 1:4]
                    f = fc[b]
                    v = hv[b]
                    comp = [P, TPG, 3, V0]
                    dve.wait_ge(fc_copied, g + 1)
                    dve.wait_ge(ext_done, g + 1)
                    dve.wait_ge(ea_done, g + 1)
                    dve.wait_ge(mid_turned, g)
                    tt = nc.vector.tensor_tensor
                    tt(ws[:, :, :, :], f[:, :, 0:128].rearrange("p t (k c) -> p t k c", k=2),
                       bcast(hs[b][:, :, :], 2, 2), ALU.mult).then_inc(mid_step, 1)
                    tt(w3e[:, :, :], f[:, :, 128:160], e0.broadcast_to([P, TPG, V0]), ALU.mult).then_inc(mid_step, 1)
                    tt(dots[:, :, :, :], v[:, :, 0:3, :], bcast(e1, 3, V0), ALU.mult).then_inc(mid_step, 1)
                    tt(cr1[:, :, :, :], v[:, :, 1:4, :], bcast(ea[b][:, :, 3:6], 3, V0), ALU.mult).then_inc(mid_step, 1)
                    tt(cr2[:, :, :, :], v[:, :, 2:5, :], bcast(ea[b][:, :, 2:5], 3, V0), ALU.mult).then_inc(mid_step, 1)
                    dve.wait_ge(mid_step, MID * g + 1)
                    tt(mid_s[:, :, 0:64], ws[:, :, 0, :], e0.broadcast_to([P, TPG, 64]), ALU.mult).then_inc(mid_step, 1)
                    tt(mid_v[:, :, :, 0:64], bcast(ws[:, :, 1, :], 2, 3), bcast(e1, 3, 64), ALU.mult).then_inc(mid_step, 1)
                    dve.wait_ge(mid_step, MID * g + 5)
                    tt(mid_v[:, :, :, 64:96], v[:, :, 0:3, :], bcast(w3e[:, :, :], 2, 3), ALU.mult).then_inc(mid_step, 1)
                    tt(dot[:, :, :], dots[:, :, 0, :], dots[:, :, 1, :], ALU.add).then_inc(mid_step, 1)
                    tt(cr1[:, :, :, :], cr1[:, :, :, :], cr2[:, :, :, :], ALU.subtract).then_inc(mid_step, 1)
                    dve.wait_ge(mid_step, MID * g + 9)
                    tt(dot[:, :, :], dot[:, :, :], dots[:, :, 2, :], ALU.add).then_inc(mid_step, 1)
                    dve.wait_ge(mid_step, MID * g + 11)
                    tt(mid_v[:, :, :, 96:128], cr1[:, :, :, :], bcast(f[:, :, 192:224], 2, 3), ALU.mult).then_inc(mid_step, 1)
                    tt(mid_s[:, :, 64:96], dot[:, :, :], f[:, :, 160:192], ALU.mult).then_inc(mid_done, 1)

                by_two(dve, NGR, front, back)

            @block.scalar
            def _(act):
                def front(pair, b):
                    g = 2 * pair + b
                    act.wait_ge(es_turned, g + 1)
                    act.wait_ge(hid_made, g)
                    nc.scalar.copy(esT[:, :], ps[0][0:64, 0:TPG * P]).then_inc(es_copied, 1)
                    act.wait_ge(var_done, g + 1)
                    act.wait_ge(rstd_done, g)
                    nc.scalar.activation(std[:, :], mv[:, :, 1], ACT.Sqrt, bias=T["eps"][:, 0:1]).then_inc(std_done, 1)
                    act.wait_ge(shift_done, g + 1)
                    act.wait_ge(h1_turned, g)
                    for j in range(TPG):
                        ins = nc.scalar.activation(h1[:, j, :], x1r[b][:, j, 0:D], ACT.Relu,
                                                   bias=shift[:, j:j + 1], scale=rstd[:, j:j + 1])
                    ins.then_inc(h1_done, 1)
                    act.wait_ge(hid_made, g + 1)
                    act.wait_ge(silu_done, g)
                    nc.scalar.activation(sig[:, :], ps[3][0:64, 0:TPG * P], ACT.Sigmoid).then_inc(sig_done, 1)
                    act.wait_ge(h1_turned, g + 1)
                    act.wait_ge(lin_made, g)
                    nc.scalar.copy(hT_s[:, :], ps[1][0:S0, 0:TPG * P])
                    nc.scalar.copy(hT_v[:, :], ps[2][0:VD, 0:TPG * P]).then_inc(h1_copied, 1)
                    if reused(pair):
                        act.wait_ge(mid_done, g - 1)
                    act.wait_ge(fc_made, g + 1)
                    for k in range(2):
                        ins = nc.scalar.copy(fc[b][:, 2 * k:2 * k + 2, :],
                                             ps[k][0:P, 0:448].rearrange("p (t c) -> p t c", t=2))
                    ins.then_inc(fc_copied, 1)
                    act.wait_ge(lin_made, g + 1)
                    for k in range(2):
                        o = ps[2 + k][0:P, 0:2 * D].rearrange("p (t c) -> p t c", t=2)
                        t2 = slice(2 * k, 2 * k + 2)
                        nc.scalar.copy(hs[b][:, t2, :], o[:, :, 0:S0])
                        ins = nc.scalar.copy(hv[b][:, t2, 0:3, :], o[:, :, S0:D].rearrange("p t (i c) -> p t i c", i=3))
                    for k in range(2):
                        o = ps[2 + k][0:P, 0:2 * D].rearrange("p (t c) -> p t c", t=2)
                        ins = nc.scalar.copy(hv[b][:, 2 * k:2 * k + 2, 3:5, :],
                                             o[:, :, S0:S0 + 64].rearrange("p t (i c) -> p t i c", i=2))
                    ins.then_inc(ext_done, 1)

                def back(pair, b):
                    g = 2 * pair + b
                    act.wait_ge(mid_turned, g + 1)
                    act.wait_ge(out_made, g)
                    nc.scalar.copy(mT_s[:, :], ps[4][0:96, 0:TPG * P])
                    for i in range(3):
                        ins = nc.scalar.copy(mT_v[:, i, :], ps[5 + i][:, 0:TPG * P])
                    ins.then_inc(mid_copied, 1)
                    act.wait_ge(out_made, g + 1)
                    act.wait_ge(total_made, g)
                    for k in range(2):
                        ins = nc.scalar.copy(out[:, 2 * k:2 * k + 2, :],
                                             ps[4 + k][0:P, 0:2 * AGW].rearrange("p (t c) -> p t c", t=2))
                    ins.then_inc(out_copied, 1)
                    act.wait_ge(total_made, g + 1)
                    if reused(pair):
                        act.wait_ge(added, 16 * TPG * (g - 1))
                    for k in range(2):
                        ins = nc.scalar.copy(total[b][:, 2 * k:2 * k + 2, :],
                                             ps[6 + k][0:P, 0:2 * AGW].rearrange("p (t c) -> p t c", t=2))
                    ins.then_inc(total_copied, 1)

                by_two(act, NGR, front, back)

            @block.tensor
            def _(pe):
                eye = T["ident"][0:P, 0:P]

                def front(pair, b):
                    g = 2 * pair + b
                    pe.wait_ge(es_loaded[b], 16 * (pair + 1))
                    pe.wait_ge(fc_copied, g)
                    waits_alone(pe, T)
                    for j in range(TPG):
                        ins = nc.tensor.transpose(ps[0][0:64, j * P:(j + 1) * P], es[b][:, j, :], eye)
                    ins.then_inc(es_turned, 1)
                    pe.wait_ge(es_copied, g + 1)
                    pe.wait_ge(ext_done, g)
                    waits_alone(pe, T)
                    nc.tensor.matmul(ps[3][0:64, 0:TPG * P], T["w_fc1"][:, :], esT[:, :], start=True,
                                     stop=True).then_inc(hid_made, 1)
                    pe.wait_ge(h1_done, g + 1)
                    for j in range(TPG):
                        nc.tensor.transpose(ps[2][0:VD, j * P:(j + 1) * P], h1[:, j, S0:D], eye)
                        ins = nc.tensor.transpose(ps[1][0:S0, j * P:(j + 1) * P], h1[:, j, 0:S0], eye)
                    ins.then_inc(h1_turned, 1)
                    pe.wait_ge(silu_done, g + 1)
                    pe.wait_ge(h1_copied, g + 1)
                    for j in range(TPG):
                        ins = nc.tensor.matmul(ps[j // 2][0:P, j % 2 * 224:j % 2 * 224 + 224], hid[:, j * P:(j + 1) * P],
                                               T["w_fc2"][:, :], start=True, stop=True)
                    ins.then_inc(fc_made, 1)
                    for j in range(TPG):
                        o, at = ps[2 + j // 2], j % 2 * D
                        nc.tensor.matmul(o[0:P, at:at + S0], hT_s[:, j * P:(j + 1) * P], T["w_in_s"][:, :],
                                         start=True, stop=True)
                        ins = nc.tensor.matmul(o[0:P, at + S0:at + D], hT_v[:, j * P:(j + 1) * P], T["w_in_v"][:, :],
                                               start=True, stop=True)
                    ins.then_inc(lin_made, 1)

                def back(pair, b):
                    g = 2 * pair + b
                    pe.wait_ge(mid_done, g + 1)
                    pe.wait_ge(total_copied, g)
                    for j in range(TPG):
                        nc.tensor.transpose(ps[4][0:96, j * P:(j + 1) * P], mid_s[:, j, :], eye)
                        for i in range(3):
                            ins = nc.tensor.transpose(ps[5 + i][:, j * P:(j + 1) * P], mid_v[:, j, i, :], eye)
                    ins.then_inc(mid_turned, 1)
                    pe.wait_ge(mid_copied, g + 1)
                    for j in range(TPG):
                        o, at = ps[4 + j // 2], j % 2 * AGW
                        nc.tensor.matmul(o[0:P, at:at + 96], mT_s[:, j * P:(j + 1) * P], T["w_out_s"][:, :],
                                         start=True, stop=True)
                        for i in range(3):
                            ins = nc.tensor.matmul(o[0:P, at + 96 + 32 * i:at + 128 + 32 * i],
                                                   mT_v[:, i, j * P:(j + 1) * P], T["w_out_v"][:, :], start=True, stop=True)
                    ins.then_inc(out_made, 1)
                    pe.wait_ge(out_copied, g + 1)
                    pe.wait_ge(same_made, g + 1)
                    for j in range(TPG):
                        ins = nc.tensor.matmul(ps[6 + j // 2][0:P, j % 2 * AGW:(j % 2 + 1) * AGW], same[b][:, j, :],
                                               out[:, j, :], start=True, stop=True)
                    ins.then_inc(total_made, 1)

                by_two(pe, NGR, front, back)


def stage_nodes1(nc, T, W, sem, N, DR, out):
    NPP = N // P
    NCH = NPP // RPC
    x1_v = DR["x1"][0:N, :].rearrange("(p n) d -> p (n d)", p=P)
    ag_v = DR["agg"][0:N, :].rearrange("(p n) d -> p (n d)", p=P)
    out_v = out.rearrange("(p n) d -> p (n d)", p=P)

    with ExitStack() as ctx:
        def sb(name, shape, dt=F32):
            return ctx.enter_context(nc.sbuf_tensor(name, shape, dt))

        def pb(name):
            return ctx.enter_context(nc.psum_tensor(name, [128, 512], F32))

        xt = [sb(f"n1_x{b}", [P, RPC, X1W]) for b in range(2)]
        ag = [sb(f"n1_ag{b}", [P, RPC, AGW]) for b in range(2)]
        ht = sb("n1_h", [P, RPC, D])
        pre = [sb(f"n1_pre{b}", [P, RPC, AGW]) for b in range(2)]
        gate = sb("n1_gate", [P, RPC, 96])
        res = [sb(f"n1_res{b}", [P, RPC, D]) for b in range(2)]
        stat = sb("n1_stat", [P, RPC, 6])
        mv = sb("n1_mv", [P, RPC, 2])
        std = sb("n1_std", [P, RPC])
        rstd = sb("n1_rstd", [P, RPC])
        shift = sb("n1_shift", [P, RPC])
        hT_s = [sb(f"n1_hTs{h}", [S0, 4 * P]) for h in range(2)]
        hT_v = [sb(f"n1_hTv{h}", [VD, 4 * P]) for h in range(2)]
        ps_s = [pb(f"n1_ps_s{h}") for h in range(2)]
        ps_v = [pb(f"n1_ps_v{h}") for h in range(2)]
        ps_o = [pb(f"n1_ps_o{q}") for q in range(4)]

        x_loaded = [sem(f"n1_x_loaded{b}") for b in range(2)]
        stored = [sem(f"n1_stored{b}") for b in range(2)]
        (stats_done, var_done, std_done, rstd_done, shift_done, h_done, hT_made, hT_copied, sc_made, pre_added,
         pre_scaled, gate_done, gated, summed) = (sem("n1_" + n) for n in (
             "stats_done", "var_done", "std_done", "rstd_done", "shift_done", "h_done", "hT_made", "hT_copied",
             "sc_made", "pre_added", "pre_scaled", "gate_done", "gated", "summed"))

        with nc.Block() as block:
            @block.sync
            def _(sp):
                def load(pair, b):
                    c = 2 * pair + b
                    if reused(pair):
                        sp.wait_ge(summed, c - 1)
                    sp.dma_start(xt[b][:, :, :].rearrange("p r d -> p (r d)"),
                                 x1_v[:, bass.ds(c * (RPC * X1W), RPC * X1W)]).then_inc(x_loaded[b], 16)
                    sp.dma_start(ag[b][:, :, :].rearrange("p r d -> p (r d)"),
                                 ag_v[:, bass.ds(c * (RPC * AGW), RPC * AGW)]).then_inc(x_loaded[b], 16)

                def store(pair, b):
                    c = 2 * pair + b
                    sp.wait_ge(summed, c + 1)
                    sp.dma_start(out_v[:, bass.ds(c * (RPC * D), RPC * D)],
                                 res[b][:, :, :].rearrange("p r d -> p (r d)")).then_inc(stored[b], 16)

                by_two(sp, NCH, load, store)
                for b in range(2):
                    sp.wait_ge(stored[b], 16 * (NCH // 2))

            @block.vector
            def _(dve):
                def normalise(pair, b):
                    c = 2 * pair + b
                    dve.wait_ge(x_loaded[b], 32 * (pair + 1))
                    for r in range(RPC):
                        ins = nc.vector.bn_stats(stat[:, r, :], xt[b][:, r, 0:D])
                    ins.then_inc(stats_done, 1)
                    dve.wait_ge(stats_done, c + 1)
                    waits_alone(dve, T)
                    for r in range(RPC):
                        ins = nc.vector.bn_aggr(mv[:, r, :], stat[:, r, :])
                    ins.then_inc(var_done, 1)
                    dve.wait_ge(std_done, c + 1)
                    dve.wait_ge(h_done, c)
                    nc.vector.reciprocal(rstd[:, :], std[:, :]).then_inc(rstd_done, 1)
                    dve.wait_ge(rstd_done, c + 1)
                    nc.vector.scalar_tensor_tensor(shift[:, :], mv[:, :, 0], -1.0, rstd[:, :], ALU.mult,
                                                   ALU.mult).then_inc(shift_done, 1)

                def combine(pair, b):
                    c = 2 * pair + b
                    for q in range(4):
                        dve.wait_ge(sc_made, 4 * c + q + 1)
                        r = slice(2 * q, 2 * q + 2)
                        if q == 0:
                            dve.wait_ge(gated, 2 * pair)
                        nc.vector.tensor_tensor(pre[b][:, r, :], ag[b][:, r, :],
                                                ps_o[q][0:P, 0:2 * AGW].rearrange("p (r d) -> p r d", r=2),
                                                ALU.add).then_inc(pre_added, 1)
                    dve.wait_ge(gate_done, c + 1)
                    dve.wait_ge(stored[b], 16 * pair)
                    nc.vector.tensor_tensor(res[b][:, :, 0:64], pre[b][:, :, 0:64], gate[:, :, 0:64], ALU.mult)
                    nc.vector.tensor_tensor(res[b][:, :, 64:160].rearrange("p r (w i) -> p r w i", i=3),
                                            pre[b][:, :, 96:192].rearrange("p r (i w) -> p r w i", i=3),
                                            bcast(gate[:, :, 64:96], 3, 3), ALU.mult).then_inc(gated, 1)

                by_two(dve, NCH, normalise, combine)

            @block.gpsimd
            def _(pool):
                def finish(pair, b):
                    c = 2 * pair + b
                    pool.wait_ge(pre_added, 4 * (c + 1))
                    nc.gpsimd.tensor_tensor(pre[b][:, :, :], pre[b][:, :, :],
                                            xt[b][:, :, D:D + 1].broadcast_to([P, RPC, AGW]), ALU.mult).then_inc(pre_scaled, 1)
                    pool.wait_ge(gated, c + 1)
                    nc.gpsimd.tensor_tensor(res[b][:, :, :], res[b][:, :, :], xt[b][:, :, 0:D],
                                            ALU.add).then_inc(summed, 1)

                with pool.Fori(0, NCH // 2) as pair:
                    finish(pair, 0)
                    finish(pair, 1)

            @block.scalar
            def _(act):
                def relu(pair, b):
                    c = 2 * pair + b
                    act.wait_ge(var_done, c + 1)
                    act.wait_ge(rstd_done, c)
                    nc.scalar.activation(std[:, :], mv[:, :, 1], ACT.Sqrt, bias=T["eps"][:, 0:1]).then_inc(std_done, 1)
                    act.wait_ge(shift_done, c + 1)
                    act.wait_ge(hT_made, 2 * c)
                    for r in range(RPC):
                        ins = nc.scalar.activation(ht[:, r, :], xt[b][:, r, 0:D], ACT.Relu,
                                                   bias=shift[:, r:r + 1], scale=rstd[:, r:r + 1])
                    ins.then_inc(h_done, 1)
                    for h in range(2):
                        act.wait_ge(hT_made, 2 * c + h + 1)
                        act.wait_ge(sc_made, 4 * c)
                        nc.scalar.copy(hT_s[h][:, :], ps_s[h][0:S0, 0:4 * P])
                        nc.scalar.copy(hT_v[h][:, :], ps_v[h][0:VD, 0:4 * P]).then_inc(hT_copied, 1)

                def sigmoid(pair, b):
                    c = 2 * pair + b
                    act.wait_ge(pre_scaled, c + 1)
                    act.wait_ge(gated, c)
                    nc.scalar.activation(gate[:, :, :], pre[b][:, :, 0:96], ACT.Sigmoid).then_inc(gate_done, 1)

                by_two(act, NCH, relu, sigmoid)

            @block.tensor
            def _(pe):
                def both(pair, b):
                    c = 2 * pair + b
                    pe.wait_ge(h_done, c + 1)
                    for h in range(2):
                        pe.wait_ge(hT_copied, 2 * c)
                        for r in range(4):
                            nc.tensor.transpose(ps_v[h][0:VD, r * P:(r + 1) * P], ht[:, 4 * h + r, S0:D],
                                                T["ident"][0:P, 0:P])
                            ins = nc.tensor.transpose(ps_s[h][0:S0, r * P:(r + 1) * P], ht[:, 4 * h + r, 0:S0],
                                                      T["ident"][0:P, 0:P])
                        ins.then_inc(hT_made, 1)
                    for q in range(4):
                        pe.wait_ge(hT_copied, 2 * c + q // 2 + 1)
                        pe.wait_ge(pre_added, 4 * c)
                        for r in range(2):
                            m = (2 * q + r) % 4 * P
                            nc.tensor.matmul(ps_o[q][0:P, r * AGW:r * AGW + 96], hT_s[q // 2][:, m:m + P],
                                             T["w_sc_s"][:, :], start=True, stop=True)
                            ins = nc.tensor.matmul(ps_o[q][0:P, r * AGW + 96:(r + 1) * AGW], hT_v[q // 2][:, m:m + P],
                                                   T["w_sc_v"][:, :], start=True, stop=True)
                        ins.then_inc(sc_made, 1)

                both(0, 0)
                both(0, 1)
                with pe.Fori(1, NCH // 2) as pair:
                    both(pair, 0)
                    both(pair, 1)


def gnn_kernel(nc, W, out):
    N, E = W["x"].shape[0], W["src"].shape[0]
    NT = E // P
    DR = {"h0": nc.dram_tensor("h0", [N, D], F32).ap(),
          "x1": nc.dram_tensor("x1", [N + P, X1W], F32).ap(),
          "agg": nc.dram_tensor("agg", [N + P, AGW], F32).ap()}
    shapes = {
        "ident": [128, 128], "halves": [128, S0], "earlier": [P, P], "spare": [P, 1], "eps": [P, 1], "a_all": [P, N // P],
        "ea": [P, NT, 4], "w_pair": [128, 40, 64], "w_vec": [128, V0, 2 * V0], "w_msg_s": [S0, 160],
        "w_msg_v": [VD, 2 * VD + 3 * S0], "w_lin_s": [S0, S0], "w_lin_v": [VD, VD], "eye_v": [VD, VD],
        "w_in_s": [S0, S0], "w_in_v": [VD, VD], "w_fc1": [64, 64], "w_fc2": [64, 224], "w_sc_s": [S0, 96],
        "w_sc_v": [VD, VD], "w_out_s": [96, 96], "w_out_v": [128, 32],
    }
    with ExitStack() as ctx:
        def sem(name):
            return ctx.enter_context(nc.semaphore(name))

        T = {"passed": sem("passed")}
        T |= {n: ctx.enter_context(nc.sbuf_tensor("t_" + n, s, F32)) for n, s in shapes.items()}
        T["idx"] = ctx.enter_context(nc.sbuf_tensor("t_idx", [P, 2, NT], I32))
        T["put"] = ctx.enter_context(nc.sbuf_tensor("t_put", [P, 2, NT], I32))
        stage_weights(nc, T, W, sem)
        stage_nodes0(nc, T, W, sem, N, NT, DR)
        stage_edges0(nc, T, W, sem, NT, DR)
        stage_edges1(nc, T, W, sem, NT, DR)
        stage_nodes1(nc, T, W, sem, N, DR, out)


def kernel(**inputs):
    import numpy as np
    import concourse.bacc as bacc
    from concourse.bass_utils import run_bass_kernel_spmd

    nc = bacc.Bacc("TRN2", target_bir_lowering=False, num_devices=1)
    a = {n.removeprefix("L0_gnn_").removeprefix("L1_gnn_"): np.asarray(v) for n, v in inputs.items()}
    N, E = a["x"].shape[0], a["src"].shape[0]
    a["Wu_sv"] = a["Wu_sv"].transpose(0, 2, 1)
    a["Wu_vs"] = a["Wu_vs"].transpose(1, 2, 0)
    a["src_rows"] = a["src"].reshape(P, E // P).T.reshape(-1)
    a["dst_rows"] = a["dst"].reshape(P, E // P).T.reshape(-1)
    a["ident"] = np.eye(128, dtype=np.float32)
    a["earlier"] = np.tril(np.ones((P, P), np.float32), -1)
    a["spare_x"] = (N + np.arange(P, dtype=np.float32)).reshape(P, 1)
    arrays, W = {}, {}
    for name, v in a.items():
        v = np.ascontiguousarray(v)
        arrays[f"in_{name}"] = v
        W[name] = nc.dram_tensor(f"in_{name}", v.shape, mybir.dt.from_np(v.dtype), kind="ExternalInput").ap()
    out = nc.dram_tensor("out", (N, D), F32, kind="ExternalOutput").ap()
    gnn_kernel(nc, W, out)
    r = run_bass_kernel_spmd(nc, [arrays], core_ids=[0])
    return r.results[0]["out"]
```

```python
from contextlib import ExitStack

import concourse.bass as bass
from concourse import mybir
import math

P = 125
F32 = mybir.dt.float32
I32 = mybir.dt.int32
ALU = mybir.AluOpType
ACT = mybir.ActivationFunctionType
AX = mybir.AxisListType
S0, V0, D = 64, 32, 160
VD = 3 * V0
X1W = D + 1
AGW = 96 + VD
RPC = 8
TPG = 4
CB = 6
GB = 4
EPS = 1e-5


def waits_alone(eng, T):
    eng.sem_inc(T["passed"], 1)


def bcast(ap, axis, n):
    ap = ap.unsqueeze(axis)
    shape = list(ap.shape)
    shape[axis] = n
    return ap.broadcast_to(shape)


def reused(turn):
    return not (isinstance(turn, int) and turn == 0)


def in_turns(eng, n, U, *parts):
    ahead, behind = max(lead for _, lead in parts), max(-lead for _, lead in parts)

    def steps(first, last):
        for s in range(first, last):
            for do, lead in parts:
                if 0 <= s + lead < n:
                    do((s + lead) // U, (s + lead) % U)

    begin = U + behind
    turns = max(0, (n - ahead - begin) // U)
    if turns < 2:
        steps(-ahead, n + behind)
        return
    steps(-ahead, begin)
    with eng.Fori(0, turns) as turn:
        for s in range(begin, begin + U):
            for do, lead in parts:
                do(turn + (s + lead) // U, (s + lead) % U)
    steps(begin + U * turns, n + behind)


def wait_for(eng, sem, count, most):
    if not isinstance(count, int):
        eng.wait_ge(sem, count)
    elif count > 0:
        eng.wait_ge(sem, min(count, most))


def chunks_in(b, n):
    return (n - b + CB - 1) // CB


def stage_weights(nc, T, W, sem):
    with nc.Block() as block:
        loaded, cleared, scaled, eye_added = (sem(n) for n in ("w_loaded", "w_cleared", "w_scaled", "w_eye"))
        loads = []

        def load(dst, src):
            loads.append((dst, src))

        load(T["ident"][:, :], W["ident"])
        load(T["halves"][0:S0, :], W["ident"][0:S0, 0:S0])
        load(T["halves"][S0:2 * S0, :], W["ident"][0:S0, 0:S0])
        load(T["earlier"][:, :], W["earlier"])
        load(T["spare"][:, 0:1], W["spare_x"])
        load(T["a_all"][:, :], W["node_vec1"].rearrange("(p n) o -> p (n o)", p=P))
        load(T["ea"][:, :, :], W["edge_attr_4"].rearrange("(p t) c -> p t c", p=P))
        load(T["idx"][:, 0, :], W["src"].rearrange("(p t) -> p t", p=P))
        load(T["idx"][:, 1, :], W["dst"].rearrange("(p t) -> p t", p=P))
        load(T["w_pair"][:, 0:32, :], W["Wu_ss"].rearrange("(c a) v w -> (a v) c w", a=2))
        load(T["w_pair"][:, 32:40, :], W["Wu_vv"].rearrange("(c a) v w -> (a v) c w", a=4))
        load(T["w_vec"][S0:2 * S0, :, :], W["Wu_sv"])
        load(T["w_vec"][0:S0, :, :], W["Wu_vs"])
        load(T["w_msg_s"][:, 0:64], W["Wm_ss"])
        load(T["w_msg_s"][:, 64:128], W["Lm_s"])
        load(T["w_msg_s"][:, 128:160], W["Wm_sv"])
        load(T["w_lin_s"][:, :], W["Lu_s"])
        load(T["w_in_s"][:, :], W["lin1_ws"])
        load(T["w_fc1"][:, :], W["fc_w1"])
        load(T["w_fc2"][:, :], W["fc_w2"])
        load(T["w_sc_s"][:, :], W["sc_ws"])
        load(T["w_out_s"][:, :], W["lin2_ws"])
        load(T["w_out_v"][:, :], W["lin2_wv"])
        for dst, src, n in (("w_msg_v", "Wm_vs", 32), ("w_lin_v", "Lu_v", 32), ("w_in_v", "lin1_wv", 32),
                            ("w_sc_v", "sc_wv", 32)):
            for i in range(3):
                load(T[dst][i:VD:3, i * n:(i + 1) * n], W[src])
        for i in range(3):
            load(T["w_msg_v"][i:VD:3, VD + i * 32:VD + (i + 1) * 32], W["Lm_v"])
            load(T["w_msg_v"][i:VD:3, 2 * VD + i * 64:2 * VD + (i + 1) * 64], W["Wm_vv"])
            load(T["eye_v"][i:VD:3, i * 32:(i + 1) * 32], W["ident"][0:32, 0:32])

        clears = [T[n] for n in ("w_msg_v", "w_lin_v", "w_in_v", "w_sc_v", "eye_v")]
        r32 = 1 / math.sqrt(32)
        scales = [
            (T["w_pair"][:, 0:32, :], 1 / 64),
            (T["w_pair"][:, 32:40, :], 1 / math.sqrt(3) / 32),
            (T["w_vec"][:, :, :], 1 / math.sqrt(2048)),
            (T["w_msg_s"][:, :], 1 / 8),
            (T["w_msg_v"][:, 0:2 * VD], r32),
            (T["w_msg_v"][:, 2 * VD:2 * VD + 192], r32 / math.sqrt(3)),
            (T["w_lin_s"][:, :], 1 / 8),
            (T["w_lin_v"][:, :], r32),
            (T["w_in_s"][:, :], 1 / 8),
            (T["w_in_v"][:, :], r32),
            (T["w_fc1"][:, :], 1 / 8),
            (T["w_fc2"][:, :], 1 / 8),
            (T["w_sc_s"][:, :], 1 / 8),
            (T["w_sc_v"][:, :], r32),
            (T["w_out_s"][0:64, :], 1 / 4 / math.sqrt(96)),
            (T["w_out_s"][64:96, :], 1 / 4 / math.sqrt(96) / math.sqrt(3)),
            (T["w_out_v"][0:96, :], 1 / 4 / math.sqrt(128)),
            (T["w_out_v"][96:128, :], 1 / 4 / math.sqrt(128) / math.sqrt(2)),
        ]

        @block.sync
        def _(sp):
            sp.wait_ge(cleared, len(clears) + 1)
            for dst, src in loads:
                sp.dma_start(dst, src, allow_slow_non_contiguous=True).then_inc(loaded, 16)
            sp.wait_ge(loaded, 16 * len(loads))

        @block.vector
        def _(dve):
            for t in clears:
                nc.vector.memset(t[:, :], 0.0).then_inc(cleared, 1)
            nc.vector.memset(T["eps"][:, :], EPS).then_inc(cleared, 1)
            dve.wait_ge(scaled, len(scales))
            nc.vector.tensor_tensor(T["w_lin_s"][:, :], T["w_lin_s"][:, :], T["ident"][0:S0, 0:S0],
                                    ALU.add).then_inc(eye_added, 1)
            nc.vector.tensor_tensor(T["w_lin_v"][:, :], T["w_lin_v"][:, :], T["eye_v"][:, :],
                                    ALU.add).then_inc(eye_added, 1)
            dve.wait_ge(eye_added, 2)

        @block.scalar
        def _(act):
            act.wait_ge(loaded, 16 * len(loads))
            for ap, c in scales:
                nc.scalar.mul(ap, ap, c).then_inc(scaled, 1)
            act.wait_ge(scaled, len(scales))


def stage_nodes0(nc, T, W, sem, N, NT, DR):
    NPP = N // P
    NCH = NPP // RPC
    TPC = NT // NCH
    x_v = W["x"].rearrange("(p n) d -> p (n d)", p=P)
    h_v = DR["h0"].rearrange("(p n) d -> p (n d)", p=P)
    x1_v = DR["x1"][0:N, :].rearrange("(p n) d -> p (n d)", p=P)

    with ExitStack() as ctx:
        def sb(name, shape, dt=F32):
            return ctx.enter_context(nc.sbuf_tensor(name, shape, dt))

        def pb(name):
            return ctx.enter_context(nc.psum_tensor(name, [128, 512], F32))

        xt = [sb(f"n0_x{b}", [P, RPC, D]) for b in range(CB)]
        ht = [sb(f"n0_h{b}", [P, RPC, D]) for b in range(CB)]
        base = [sb(f"n0_base{b}", [P, RPC, X1W]) for b in range(CB)]
        rows = [sb(f"n0_rows{b}", [P, 2, TPC, P], I32) for b in range(CB)]
        stat = sb("n0_stat", [P, RPC, 6])
        mv = [sb(f"n0_mv{b}", [P, RPC, 2]) for b in range(CB)]
        std = [sb(f"n0_std{b}", [P, RPC]) for b in range(CB)]
        rstd = [sb(f"n0_rstd{b}", [P, RPC]) for b in range(CB)]
        shift = [sb(f"n0_shift{b}", [P, RPC]) for b in range(CB)]
        hT_s = [sb(f"n0_hTs{h}", [S0, 4 * P]) for h in range(2)]
        hT_v = [sb(f"n0_hTv{h}", [VD, 4 * P]) for h in range(2)]
        zero = sb("n0_zero", [P, AGW])
        same = [sb(f"n0_same{b}", [P, 2 * TPC, P]) for b in range(CB)]
        hit = [sb(f"n0_hit{b}", [P, 2 * TPC, P]) for b in range(CB)]
        rep = sb("n0_rep", [P, 2, NT])
        ps_s = [pb(f"n0_ps_s{h}") for h in range(2)]
        ps_v = [pb(f"n0_ps_v{h}") for h in range(2)]
        ps_o = [pb(f"n0_ps_o{q}") for q in range(4)]

        x_loaded = [sem(f"n0_x_loaded{b}") for b in range(CB)]
        rows_loaded = [sem(f"n0_rows_loaded{b}") for b in range(CB)]
        h_stored = [sem(f"n0_h_stored{b}") for b in range(CB)]
        x1_stored = [sem(f"n0_x1_stored{b}") for b in range(CB)]
        (zeroed, spare_stored, stats_done, var_done, std_done, rstd_done, shift_done, h_done, hT_made,
         hT_copied, lin_made, base_added, base_done, compared, masked, rep_done, target_done) = (
            sem("n0_" + n) for n in (
                "zeroed", "spare_stored", "stats_done", "var_done", "std_done", "rstd_done",
                "shift_done", "h_done", "hT_made", "hT_copied", "lin_made", "base_added", "base_done", "compared",
                "masked", "rep_done", "target_done"))

        with nc.Block() as block:
            @block.sync
            def _(sp):
                sp.wait_ge(zeroed, 1)
                sp.dma_start(DR["x1"][N:N + P, :], zero[:, 0:X1W]).then_inc(spare_stored, 16)
                sp.dma_start(DR["agg"][N:N + P, :], zero[:, 0:AGW]).then_inc(spare_stored, 16)

                def load(turn, b):
                    c = CB * turn + b
                    if reused(turn):
                        sp.wait_ge(base_done, c - CB + 1)
                        sp.wait_ge(compared, c - CB + 1)
                    sp.dma_start(xt[b][:, :, :].rearrange("p r d -> p (r d)"),
                                 x_v[:, bass.ds(c * (RPC * D), RPC * D)]).then_inc(x_loaded[b], 16)
                    for k, name in enumerate(("src_rows", "dst_rows")):
                        row = W[name][bass.ds(c * (TPC * P), TPC * P)].partition_broadcast(P)
                        sp.dma_start(rows[b][:, k, :, :].rearrange("p t q -> p (t q)"), row).then_inc(rows_loaded[b], 16)

                def store_h(turn, b):
                    c = CB * turn + b
                    sp.wait_ge(h_done, c + 1)
                    sp.dma_start(h_v[:, bass.ds(c * (RPC * D), RPC * D)],
                                 ht[b][:, :, :].rearrange("p r d -> p (r d)")).then_inc(h_stored[b], 16)

                def store_x1(turn, b):
                    c = CB * turn + b
                    sp.wait_ge(base_done, c + 1)
                    sp.dma_start(x1_v[:, bass.ds(c * (RPC * X1W), RPC * X1W)],
                                 base[b][:, :, :].rearrange("p r d -> p (r d)")).then_inc(x1_stored[b], 16)

                in_turns(sp, NCH, CB, (load, 5), (store_h, 1), (store_x1, 0))
                sp.wait_ge(spare_stored, 32)
                for b in range(CB):
                    sp.wait_ge(h_stored[b], 16 * chunks_in(b, NCH))
                    sp.wait_ge(x1_stored[b], 16 * chunks_in(b, NCH))

            @block.vector
            def _(dve):
                nc.vector.memset(zero[:, :], 0.0).then_inc(zeroed, 1)

                def stats(turn, b):
                    c = CB * turn + b
                    dve.wait_ge(x_loaded[b], 16 * (turn + 1))
                    for r in range(RPC):
                        ins = nc.vector.bn_stats(stat[:, r, :], xt[b][:, r, :])
                    ins.then_inc(stats_done, 1)
                    dve.wait_ge(stats_done, c + 1)
                    waits_alone(dve, T)
                    for r in range(RPC):
                        ins = nc.vector.bn_aggr(mv[b][:, r, :], stat[:, r, :])
                    ins.then_inc(var_done, 1)

                def scales(turn, b):
                    c = CB * turn + b
                    dve.wait_ge(std_done, c + 1)
                    nc.vector.reciprocal(rstd[b][:, :], std[b][:, :]).then_inc(rstd_done, 1)
                    dve.wait_ge(rstd_done, c + 1)
                    nc.vector.scalar_tensor_tensor(shift[b][:, :], mv[b][:, :, 0], -1.0, rstd[b][:, :], ALU.mult,
                                                   ALU.mult).then_inc(shift_done, 1)

                def compare(turn, b):
                    c = CB * turn + b
                    dve.wait_ge(rows_loaded[b], 32 * (turn + 1))
                    if reused(turn):
                        dve.wait_ge(masked, c - CB + 1)
                    for k in range(2):
                        mine = T["idx"][:, k, bass.ds(c * TPC, TPC)]
                        ins = nc.vector.tensor_tensor(same[b][:, k * TPC:(k + 1) * TPC, :], rows[b][:, k, :, :],
                                                      bcast(mine, 2, P), ALU.is_equal)
                    ins.then_inc(compared, 1)

                def repeats(turn, b):
                    c = CB * turn + b
                    dve.wait_ge(masked, c + 1)
                    nc.vector.tensor_reduce(rep[:, :, bass.ds(c * TPC, TPC)],
                                            hit[b][:, :, :].rearrange("p (k t) q -> p k t q", k=2), AX.X,
                                            ALU.max).then_inc(rep_done, 1)

                def add(turn, b):
                    c = CB * turn + b
                    dve.wait_ge(x1_stored[b], 16 * turn)
                    for q in range(4):
                        dve.wait_ge(lin_made, 4 * c + q + 1)
                        o = ps_o[q][0:P, 0:2 * D].rearrange("p (r d) -> p r d", r=2)
                        r = slice(2 * q, 2 * q + 2)
                        nc.vector.tensor_tensor(base[b][:, r, 0:S0], xt[b][:, r, 0:S0], o[:, :, 0:S0], ALU.add)
                        ins = nc.vector.tensor_tensor(
                            base[b][:, r, S0:D].rearrange("p r (w i) -> p r w i", i=3),
                            xt[b][:, r, S0:D].rearrange("p r (w i) -> p r w i", i=3),
                            o[:, :, S0:D].rearrange("p r (i w) -> p r w i", i=3), ALU.add)
                        ins.then_inc(base_added, 1)
                    nc.vector.tensor_copy(base[b][:, :, D], T["a_all"][:, bass.ds(c * RPC, RPC)]).then_inc(base_done, 1)

                in_turns(dve, NCH, CB, (scales, 2), (stats, 3), (compare, 0), (add, 0), (repeats, -1))
                dve.wait_ge(rep_done, NCH)
                target = same[0][:, :, :].rearrange("p k q -> p (k q)")[:, 0:2 * NT]
                toward = hit[0][:, :, :].rearrange("p k q -> p (k q)")[:, 0:2 * NT]
                flat = "p k t -> p (k t)"
                nc.vector.tensor_copy(target, T["idx"][:, :, :].rearrange(flat)).then_inc(target_done, 1)
                dve.wait_ge(target_done, 1)
                nc.vector.tensor_scalar(toward, target, -1.0, T["spare"][:, 0:1], ALU.mult, ALU.add).then_inc(target_done, 1)
                dve.wait_ge(target_done, 2)
                nc.vector.tensor_tensor(toward, toward, rep[:, :, :].rearrange(flat), ALU.mult).then_inc(target_done, 1)
                dve.wait_ge(target_done, 3)
                nc.vector.tensor_tensor(T["put"][:, :, :].rearrange(flat), toward, target, ALU.add).then_inc(target_done, 1)
                dve.wait_ge(target_done, 4)

            @block.gpsimd
            def _(pool):
                def mask(turn, b):
                    c = CB * turn + b
                    pool.wait_ge(compared, c + 1)
                    if reused(turn):
                        pool.wait_ge(rep_done, c - CB + 1)
                    nc.gpsimd.tensor_tensor(hit[b][:, :, :], same[b][:, :, :], bcast(T["earlier"][:, :], 1, 2 * TPC),
                                            ALU.mult).then_inc(masked, 1)

                in_turns(pool, NCH, CB, (mask, 0))

            @block.scalar
            def _(act):
                def root(turn, b):
                    c = CB * turn + b
                    act.wait_ge(var_done, c + 1)
                    if reused(turn):
                        act.wait_ge(rstd_done, c - CB + 1)
                    nc.scalar.activation(std[b][:, :], mv[b][:, :, 1], ACT.Sqrt, bias=T["eps"][:, 0:1]).then_inc(std_done, 1)

                def relu(turn, b):
                    c = CB * turn + b
                    act.wait_ge(shift_done, c + 1)
                    act.wait_ge(h_stored[b], 16 * turn)
                    for r in range(RPC):
                        ins = nc.scalar.activation(ht[b][:, r, :], xt[b][:, r, :], ACT.Relu,
                                                   bias=shift[b][:, r:r + 1], scale=rstd[b][:, r:r + 1])
                    ins.then_inc(h_done, 1)

                def copy(turn, b):
                    c = CB * turn + b
                    for h in range(2):
                        act.wait_ge(hT_made, 2 * c + h + 1)
                        act.wait_ge(lin_made, 4 * c)
                        nc.scalar.copy(hT_s[h][:, :], ps_s[h][0:S0, 0:4 * P])
                        nc.scalar.copy(hT_v[h][:, :], ps_v[h][0:VD, 0:4 * P]).then_inc(hT_copied, 1)

                in_turns(act, NCH, CB, (copy, 0), (relu, 2), (root, 3))

            @block.tensor
            def _(pe):
                def turn_h(turn, b):
                    c = CB * turn + b
                    pe.wait_ge(h_done, c + 1)
                    for h in range(2):
                        pe.wait_ge(hT_copied, 2 * c)
                        for r in range(4):
                            nc.tensor.transpose(ps_v[h][0:VD, r * P:(r + 1) * P], ht[b][:, 4 * h + r, S0:D],
                                                T["ident"][0:P, 0:P])
                            ins = nc.tensor.transpose(ps_s[h][0:S0, r * P:(r + 1) * P], ht[b][:, 4 * h + r, 0:S0],
                                                      T["ident"][0:P, 0:P])
                        ins.then_inc(hT_made, 1)

                def linear(turn, b):
                    c = CB * turn + b
                    for q in range(4):
                        pe.wait_ge(hT_copied, 2 * c + q // 2 + 1)
                        pe.wait_ge(base_added, 4 * c)
                        for r in range(2):
                            m = (2 * q + r) % 4 * P
                            nc.tensor.matmul(ps_o[q][0:P, r * D:r * D + S0], hT_s[q // 2][:, m:m + P],
                                             T["w_lin_s"][:, :], start=True, stop=True)
                            ins = nc.tensor.matmul(ps_o[q][0:P, r * D + S0:(r + 1) * D], hT_v[q // 2][:, m:m + P],
                                                   T["w_lin_v"][:, :], start=True, stop=True)
                        ins.then_inc(lin_made, 1)

                in_turns(pe, NCH, CB, (linear, 0), (turn_h, 1))


def stage_edges0(nc, T, W, sem, N, NT, DR):
    RPT = N // P // NT
    NG = 10
    DVE_ROWS = 26
    ACT_ROWS = (5, 2, 3, 3, 5)
    ACT_FROM = S0 - sum(ACT_ROWS)
    PP = 6
    MSG = 2
    TERMS = 5
    FOLD_AT, Y1_AT, TOTAL_AT, TURN_AT, PRODUCTS_AT = 1, 3, 2, 1, 3

    ag_v = DR["agg"][0:N, :].rearrange("(p n) d -> p (n d)", p=P)

    with ExitStack() as ctx:
        def sb(name, shape, dt=F32):
            return ctx.enter_context(nc.sbuf_tensor(name, shape, dt))

        def pb(name):
            return ctx.enter_context(nc.psum_tensor(name, [128, 512], F32))

        h_dst = [sb(f"e0_h_dst{b}", [P, D]) for b in range(2)]
        own = [sb(f"e0_own{b}", [P, S0 + D]) for b in range(2)]
        vec = [sb(f"e0_vec{b}", [P, 3, 2 * V0]) for b in range(2)]
        hd_s = sb("e0_hd_s", [S0, P])
        hd_v = sb("e0_hd_v", [VD, P])
        gm = sb("e0_gm", [P, TERMS, D])
        sm = [sb(f"e0_sm{b}", [128, P]) for b in range(2)]
        pair_s = [sb(f"e0_pair_s{b}", [P, S0, S0]) for b in range(2)]
        pair_v = [sb(f"e0_pair_v{b}", [P, 3, V0, V0]) for b in range(2)]
        pairT = [sb(f"e0_pairT{k}", [128, 4 * P]) for k in range(3)]
        sums = sb("e0_sums", [128, P])
        prod = [sb(f"e0_prod{h}", [P, 3, V0 // 2, 2 * V0]) for h in range(2)]
        upd = [sb(f"e0_upd{b}", [P, X1W]) for b in range(2)]
        total = [sb(f"e0_total{b}", [P, X1W]) for b in range(2)]
        rows = [sb(f"e0_rows{b}", [P, P], I32) for b in range(2)]
        same = [sb(f"e0_same{b}", [P, P]) for b in range(2)]
        ends = [sb(f"e0_ends{b}", [P, 2], I32) for b in range(2)]
        put = sb("e0_put", [P, 1], I32)
        zero = sb("e0_zero", [P, RPT * AGW])
        ps_y = [pb(f"e0_ps_y{k}") for k in range(2)]
        ps_t = [pb(f"e0_ps_t{k}") for k in range(2)]
        ps_m, ps_u, ps_g, ps_f = pb("e0_ps_m"), pb("e0_ps_u"), pb("e0_ps_g"), pb("e0_ps_f")

        gathered = [sem(f"e0_gathered{b}") for b in range(2)]
        rows_loaded = [sem(f"e0_rows_loaded{b}") for b in range(2)]
        (same_made, hd_turned, hd_copied, gm_made, gm_copied, msg_step, vec_copied, sm_turned, sm_copied, dve_paired,
         pool_paired, act_paired, pairs_turned, pairs_copied, pairs_summed, y_made, y_used, vec_summed, upd_cleared, upd_s_copied,
         total_made, total_copied, added, ends_copied, put_copied, sums_copied, folded, zeroed, agg_cleared) = (sem("e0_" + n) for n in (
             "same_made", "hd_turned", "hd_copied", "gm_made", "gm_copied", "msg_step", "vec_copied", "sm_turned",
             "sm_copied", "dve_paired", "pool_paired", "act_paired", "pairs_turned", "pairs_copied", "pairs_summed", "y_made",
             "y_used", "vec_summed", "upd_cleared", "upd_s_copied", "total_made", "total_copied", "added",
             "ends_copied", "put_copied", "sums_copied", "folded", "zeroed",
             "agg_cleared"))

        def pipeline(eng, step):
            step(None, None, None, (0, 0))
            step(None, None, (0, 0), (0, 1))
            step(None, (0, 0), (0, 1), (1, 0))
            step((0, 0), (0, 1), (1, 0), (1, 1))
            with eng.Fori(1, NT // 2 - 1) as pair:
                step((pair - 1, 1), (pair, 0), (pair, 1), (pair + 1, 0))
                step((pair, 0), (pair, 1), (pair + 1, 0), (pair + 1, 1))
            last = NT // 2 - 1
            step((last - 1, 1), (last, 0), (last, 1), None)
            step((last, 0), (last, 1), None, None)
            step((last, 1), None, None, None)

        with nc.Block() as block:
            @block.sync
            def _(sp):
                def rows_of(pair, b):
                    t = 2 * pair + b
                    sp.dma_start(rows[b][:, :],
                                 W["src_rows"][bass.ds(t * P, P)].partition_broadcast(P)).then_inc(rows_loaded[b], 16)

                def clear(t):
                    sp.dma_start(ag_v[:, bass.ds(t * (RPT * AGW), RPT * AGW)], zero[:, :]).then_inc(agg_cleared, 16)

                rows_of(0, 0)
                rows_of(0, 1)
                sp.wait_ge(zeroed, 1)
                clear(0)
                clear(1)
                with sp.Fori(0, NT // 2 - 1) as pair:
                    for b in range(2):
                        clear(2 * pair + b + 2)
                        sp.wait_ge(same_made, 2 * pair + b + 1)
                        rows_of(pair + 1, b)
                sp.wait_ge(agg_cleared, 16 * NT)

            @block.gpsimd
            def _(pool):
                def gather(pair, b):
                    t = 2 * pair + b
                    if reused(pair):
                        pool.wait_ge(hd_turned, t - 1)
                        pool.wait_ge(sm_turned, t - 1)
                        pool.wait_ge(dve_paired, t - 1)
                        pool.wait_ge(pool_paired, PP * (t - 1))
                        pool.wait_ge(act_paired, t - 1)
                        pool.wait_ge(vec_copied, t - 1)
                    waits_alone(pool, T)
                    nc.gpsimd.tensor_copy(ends[b][:, :], T["idx"][:, :, bass.ds(t, 1)].squeeze(2)).then_inc(ends_copied, 1)
                    pool.wait_ge(ends_copied, t + 1)
                    waits_alone(pool, T)
                    pool.indirect_dma_start(h_dst[b][:, :], None, DR["h0"],
                                            bass.IndirectOffsetOnAxis(ends[b][:, 1:2], 0)).then_inc(gathered[b], 16)
                    pool.indirect_dma_start(own[b][:, S0:S0 + D], None, DR["h0"],
                                            bass.IndirectOffsetOnAxis(ends[b][:, 0:1], 0)).then_inc(gathered[b], 16)

                def pairs_scalar(pair, b):
                    t = 2 * pair + b
                    pool.wait_ge(msg_step, MSG * (t + 1))
                    if reused(pair):
                        pool.wait_ge(pairs_turned, NG * (t - 1))
                    nc.gpsimd.tensor_tensor(pair_s[b][:, DVE_ROWS:ACT_FROM, :],
                                            bcast(own[b][:, S0 + DVE_ROWS:S0 + ACT_FROM], 2, S0),
                                            bcast(own[b][:, 0:S0], 1, ACT_FROM - DVE_ROWS),
                                            ALU.mult).then_inc(pool_paired, 1)

                def pairs_vector(pair, b):
                    pool.wait_ge(vec_copied, 2 * pair + b + 1)
                    for i in range(3):
                        nc.gpsimd.tensor_tensor(pair_v[b][:, i, :, :], bcast(vec[b][:, i, V0:2 * V0], 2, V0),
                                                bcast(vec[b][:, i, 0:V0], 1, V0), ALU.mult).then_inc(pool_paired, 1)
                    for i in range(1, 3):
                        pool.wait_ge(pool_paired, PP * (2 * pair + b) + (3 if i == 1 else 5))
                        nc.gpsimd.tensor_tensor(pair_v[b][:, 0, :, :], pair_v[b][:, 0, :, :], pair_v[b][:, i, :, :],
                                                ALU.add).then_inc(pool_paired, 1)

                def scatter(pair, b):
                    t = 2 * pair + b
                    pool.wait_ge(added, 16 * t)
                    waits_alone(pool, T)
                    nc.gpsimd.tensor_copy(put[:, :], T["put"][:, 0, bass.ds(t, 1)]).then_inc(put_copied, 1)
                    pool.wait_ge(put_copied, t + 1)
                    pool.wait_ge(total_copied, t + 1)
                    waits_alone(pool, T)
                    pool.indirect_dma_start(DR["x1"], bass.IndirectOffsetOnAxis(put[:, 0:1], 0),
                                            total[b][:, :], None, compute_op=ALU.add).then_inc(added, 16)

                def step(before, this, after, after2):
                    if after2:
                        gather(*after2)
                    if after:
                        pairs_scalar(*after)
                        pairs_vector(*after)
                    if before:
                        scatter(*before)

                pipeline(pool, step)
                pool.wait_ge(added, 16 * NT)

            @block.vector
            def _(dve):
                nc.vector.memset(zero[:, :], 0.0).then_inc(zeroed, 1)
                for b in range(2):
                    nc.vector.memset(upd[b][:, :], 0.0).then_inc(upd_cleared, 1)

                def message(pair, b):
                    t = 2 * pair + b
                    dve.wait_ge(gm_copied, t + 1)
                    if reused(pair):
                        dve.wait_ge(pool_paired, PP * (t - 1))
                        dve.wait_ge(act_paired, t - 1)
                        dve.wait_ge(sm_turned, t - 1)
                        dve.wait_ge(y_used, 4 * (t - 1))
                        dve.wait_ge(dve_paired, t - 1)
                    nc.vector.tensor_reduce(own[b][:, 0:S0], gm[:, :, 0:S0].rearrange("p k c -> p c k"), AX.X,
                                            ALU.add).then_inc(msg_step, 1)
                    nc.vector.tensor_reduce(vec[b][:, :, 0:V0],
                                            gm[:, 0:3, S0:D].rearrange("p k (i w) -> p i w k", i=3), AX.X,
                                            ALU.add).then_inc(msg_step, 1)

                def pairs_scalar(pair, b):
                    t = 2 * pair + b
                    dve.wait_ge(msg_step, MSG * (t + 1))
                    if reused(pair):
                        dve.wait_ge(pairs_turned, NG * (t - 1))
                    nc.vector.tensor_tensor(pair_s[b][:, 0:DVE_ROWS, :], bcast(own[b][:, S0:S0 + DVE_ROWS], 2, S0),
                                            bcast(own[b][:, 0:S0], 1, DVE_ROWS), ALU.mult).then_inc(dve_paired, 1)

                def update_vector(pair, b, after2):
                    t = 2 * pair + b
                    if reused(pair):
                        dve.wait_ge(total_made, t - 1)
                    dve.wait_ge(rows_loaded[b], 16 * (pair + 1))
                    nc.vector.tensor_tensor(same[b][:, :], rows[b][:, :],
                                            T["idx"][:, 0, bass.ds(t, 1)].broadcast_to([P, P]),
                                            ALU.is_equal).then_inc(same_made, 1)

                    def multiply(h, k):
                        dve.wait_ge(y_made, 4 * t + 2 * h + k + 1)
                        y = ps_y[k][0:P, :].rearrange("p (w c) -> p w c", c=V0)
                        nc.vector.tensor_tensor(prod[h][:, :, :, k * V0:(k + 1) * V0], bcast(y, 1, 3),
                                                bcast(vec[b][:, :, k * V0:(k + 1) * V0], 2, V0 // 2),
                                                ALU.mult).then_inc(y_used, 1)

                    def reduce(h):
                        dve.wait_ge(y_used, 4 * t + 2 * h + 2)
                        out = upd[b][:, S0 + 48 * h:S0 + 48 * (h + 1)].rearrange("p (w i) -> p i w", i=3)
                        nc.vector.tensor_reduce(out, prod[h][:, :, :, :], AX.X, ALU.add).then_inc(vec_summed, 1)

                    dve.wait_ge(vec_summed, 2 * t)
                    for h in range(2):
                        multiply(h, 0)
                        multiply(h, 1)
                        if h == 1 and after2:
                            message(*after2)
                        reduce(h)

                def step(before, this, after, after2):
                    if after:
                        pairs_scalar(*after)
                    if this:
                        update_vector(*this, after2)
                    elif after2:
                        message(*after2)

                dve.wait_ge(upd_cleared, 2)
                pipeline(dve, step)

            @block.scalar
            def _(act):
                def copy_vec(pair, b):
                    t = 2 * pair + b
                    act.wait_ge(gathered[b], 32 * (pair + 1))
                    if reused(pair):
                        act.wait_ge(y_used, 4 * (t - 1))
                    nc.scalar.copy(vec[b][:, :, V0:2 * V0],
                                          own[b][:, 2 * S0:S0 + D].rearrange("p (u i) -> p i u", i=3)).then_inc(vec_copied, 1)

                def copy_sm(pair, b):
                    t = 2 * pair + b
                    act.wait_ge(sm_turned, t + 1)
                    if reused(pair):
                        act.wait_ge(y_made, 4 * (t - 1))
                    nc.scalar.copy(sm[b][:, :], ps_m[:, 0:P]).then_inc(sm_copied, 1)

                def copy_hd(pair, b):
                    t = 2 * pair + b
                    act.wait_ge(hd_turned, t + 1)
                    act.wait_ge(gm_made, t)
                    nc.scalar.copy(hd_s[:, :], ps_f[0:S0, 2 * P:3 * P])
                    nc.scalar.copy(hd_v[:, :], ps_f[0:VD, 3 * P:4 * P]).then_inc(hd_copied, 1)

                def copy_gm(pair, b):
                    t = 2 * pair + b
                    act.wait_ge(gm_made, t + 1)
                    act.wait_ge(msg_step, MSG * t)
                    nc.scalar.mul(gm[:, 0, :], ps_g[0:P, 0:D], T["ea"][:, bass.ds(t, 1), 3])
                    nc.scalar.copy(gm[:, 1, :], ps_g[0:P, D:2 * D])

                def copy_gm_rest(pair, b):
                    t = 2 * pair + b
                    for i in range(3):
                        r = T["ea"][:, bass.ds(t, 1), i]
                        nc.scalar.mul(gm[:, 2 + i, 0:S0], ps_f[0:P, V0 + i * S0:V0 + (i + 1) * S0], r)
                        ins = nc.scalar.mul(gm[:, 2, S0 + i * V0:S0 + (i + 1) * V0], ps_f[0:P, 0:V0], r)
                    ins.then_inc(gm_copied, 1)

                def copy_pairs(pair, b, g):
                    t = 2 * pair + b
                    act.wait_ge(pairs_turned, NG * t + g + 1)
                    act.wait_ge(pairs_summed, NG * t + (g - 2 if g >= 3 else 0))
                    nc.scalar.copy(pairT[g % 3][:, :], ps_t[g % 2][:, 0:4 * P]).then_inc(pairs_copied, 1)

                def copy_update(pair, b):
                    t = 2 * pair + b
                    act.wait_ge(folded, t + 1)
                    if reused(pair):
                        act.wait_ge(total_made, t - 1)
                    nc.scalar.copy(upd[b][:, 0:S0], ps_m[0:P, 2 * P:2 * P + S0]).then_inc(upd_s_copied, 1)

                def copy_sums(pair, b):
                    t = 2 * pair + b
                    act.wait_ge(pairs_summed, NG * (t + 1))
                    act.wait_ge(folded, t)
                    nc.scalar.copy(sums[:, :], ps_u[:, 0:P]).then_inc(sums_copied, 1)

                def copy_total(pair, b):
                    t = 2 * pair + b
                    act.wait_ge(total_made, t + 1)
                    if reused(pair):
                        act.wait_ge(added, 16 * (t - 1))
                    nc.scalar.copy(total[b][:, :], ps_g[0:P, 0:X1W]).then_inc(total_copied, 1)

                def pairs_scalar(pair, b, n):
                    t = 2 * pair + b
                    if n == 0:
                        act.wait_ge(gathered[b], 32 * (pair + 1))
                        act.wait_ge(msg_step, MSG * (t + 1))
                        if reused(pair):
                            act.wait_ge(pairs_turned, NG * (t - 1))
                    first = ACT_FROM + sum(ACT_ROWS[:n])
                    for u in range(first, first + ACT_ROWS[n]):
                        ins = nc.scalar.mul(pair_s[b][:, u, :], own[b][:, 0:S0], own[b][:, S0 + u:S0 + u + 1])
                    if n == len(ACT_ROWS) - 1:
                        ins.then_inc(act_paired, 1)

                def step(before, this, after, after2):
                    if after:
                        copy_vec(*after)
                        pairs_scalar(*after, 0)
                        copy_sm(*after)
                    for g in range(NG):
                        if after:
                            copy_pairs(*after, g)
                            if g + 1 < len(ACT_ROWS):
                                pairs_scalar(*after, g + 1)
                        if g == FOLD_AT and this:
                            copy_update(*this)
                        if g == TOTAL_AT and before:
                            copy_total(*before)
                        if g == TURN_AT and after2:
                            copy_hd(*after2)
                        if g == PRODUCTS_AT and after2:
                            copy_gm(*after2)
                        if g == PRODUCTS_AT + 1 and after2:
                            copy_gm_rest(*after2)
                    if after:
                        copy_sums(*after)

                act.wait_ge(upd_cleared, 2)
                pipeline(act, step)

            @block.tensor
            def _(pe):
                eye = T["ident"][0:P, 0:P]

                def turn_sm(pair, b):
                    t = 2 * pair + b
                    pe.wait_ge(msg_step, MSG * (t + 1))
                    if reused(pair):
                        pe.wait_ge(upd_s_copied, t - 1)
                    pe.wait_ge(sm_copied, t)
                    nc.tensor.transpose(ps_m[:, 0:P], own[b][:, 0:2 * S0], eye).then_inc(sm_turned, 1)

                def turn_hd(pair, b):
                    t = 2 * pair + b
                    pe.wait_ge(gathered[b], 32 * (pair + 1))
                    pe.wait_ge(gm_copied, t)
                    nc.tensor.transpose(ps_f[0:VD, 3 * P:4 * P], h_dst[b][:, S0:D], eye)
                    nc.tensor.transpose(ps_f[0:S0, 2 * P:3 * P], h_dst[b][:, 0:S0], eye).then_inc(hd_turned, 1)

                def message_products(pair, b):
                    t = 2 * pair + b
                    pe.wait_ge(hd_copied, t + 1)
                    mv = T["w_msg_v"]
                    for out, x, w in ((ps_g[0:P, 0:S0], hd_s, T["w_msg_s"][:, 0:S0]),
                                      (ps_g[0:P, S0:D], hd_v, mv[:, 0:VD]),
                                      (ps_g[0:P, D:D + S0], hd_s, T["w_msg_s"][:, S0:2 * S0]),
                                      (ps_g[0:P, D + S0:2 * D], hd_v, mv[:, VD:2 * VD]),
                                      (ps_f[0:P, 0:V0], hd_s, T["w_msg_s"][:, 2 * S0:2 * S0 + V0]),
                                      (ps_f[0:P, V0:V0 + 3 * S0], hd_v, mv[:, 2 * VD:])):
                        ins = nc.tensor.matmul(out, x[:, :], w, start=True, stop=True)
                    ins.then_inc(gm_made, 1)

                def vector_weights(pair, b, h):
                    t = 2 * pair + b
                    pe.wait_ge(sm_copied, t + 1)
                    pe.wait_ge(y_used, 4 * t + 2 * h)
                    for k, half in enumerate((slice(S0, 2 * S0), slice(0, S0))):
                        nc.tensor.matmul(ps_y[k][0:P, :], sm[b][half, 0:P],
                                         T["w_vec"][half, 16 * h:16 * (h + 1), :].rearrange("p w c -> p (w c)"),
                                         start=True, stop=True).then_inc(y_made, 1)

                def turn_pairs(pair, b, g):
                    t = 2 * pair + b
                    if g == 0:
                        pe.wait_ge(dve_paired, t + 1)
                    if g == DVE_ROWS // 8:
                        pe.wait_ge(pool_paired, PP * t + 1)
                    if g == ACT_FROM // 8:
                        pe.wait_ge(act_paired, t + 1)
                    if g == 8:
                        pe.wait_ge(pool_paired, PP * (t + 1))
                    if g >= 2:
                        pe.wait_ge(pairs_copied, NG * t + g - 1)
                    for n in range(4):
                        c = 4 * g + n
                        if c < 32:
                            x = pair_s[b][:, 2 * c:2 * c + 2, :].rearrange("p u v -> p (u v)")
                        else:
                            x = pair_v[b][:, 0, 4 * (c - 32):4 * (c - 32) + 4, :].rearrange("p u v -> p (u v)")
                        ins = nc.tensor.transpose(ps_t[g % 2][:, n * P:(n + 1) * P], x, eye)
                    ins.then_inc(pairs_turned, 1)

                def sum_pairs(pair, b, g):
                    t = 2 * pair + b
                    pe.wait_ge(pairs_copied, NG * t + g + 1)
                    if g == 0:
                        pe.wait_ge(sums_copied, t)
                    for n in range(4):
                        c, half = 4 * g + n, n % 2 * S0
                        w = T["w_pair"][:, c, :]
                        ins = nc.tensor.matmul(ps_u[half:half + S0, 0:P], w, pairT[g % 3][:, n * P:(n + 1) * P],
                                               start=(c < 2), stop=(c >= 4 * NG - 2))
                    ins.then_inc(pairs_summed, 1)

                def fold(pair, b):
                    t = 2 * pair + b
                    pe.wait_ge(sums_copied, t + 1)
                    nc.tensor.matmul(ps_m[0:P, 2 * P:2 * P + S0], sums[:, :], T["halves"][:, :], start=True,
                                     stop=True).then_inc(folded, 1)

                def sum_tile(pair, b):
                    t = 2 * pair + b
                    pe.wait_ge(total_copied, t)
                    pe.wait_ge(upd_s_copied, t + 1)
                    pe.wait_ge(vec_summed, 2 * (t + 1))
                    pe.wait_ge(same_made, t + 1)
                    nc.tensor.matmul(ps_g[0:P, 0:X1W], same[b][:, :], upd[b][:, :], start=True, stop=True).then_inc(total_made, 1)

                def step(before, this, after, after2):
                    if this:
                        vector_weights(*this, 0)
                    if after:
                        turn_sm(*after)
                    for g in range(NG + 2):
                        if after:
                            if g < NG:
                                turn_pairs(*after, g)
                            if g >= 2:
                                sum_pairs(*after, g - 2)
                        if g == FOLD_AT and this:
                            if after:
                                pe.wait_ge(sm_copied, 2 * after[0] + after[1] + 1)
                            fold(*this)
                        if g == Y1_AT and this:
                            vector_weights(*this, 1)
                        if g == TOTAL_AT and before:
                            pe.wait_ge(gm_copied, 2 * after[0] + after[1] + 1 if after else NT)
                            sum_tile(*before)
                        if g == TURN_AT and after2:
                            turn_hd(*after2)
                        if g == PRODUCTS_AT and after2:
                            if before:
                                pe.wait_ge(total_copied, 2 * before[0] + before[1] + 1)
                            message_products(*after2)

                pipeline(pe, step)


def stage_edges1(nc, T, W, sem, NT, DR):
    NGR = NT // TPG
    es_v = W["edge_attr_64"].rearrange("(p t) c -> p (t c)", p=P)

    with ExitStack() as ctx:
        def sb(name, shape, dt=F32):
            return ctx.enter_context(nc.sbuf_tensor(name, shape, dt))

        ps = [ctx.enter_context(nc.psum_tensor(f"e1_ps{k}", [128, 512], F32)) for k in range(8)]
        ps_mid_s, ps_mid_v = ps[0], ps[1:4]
        ps_esT, ps_hid, ps_hT_s, ps_hT_v = ps[0:4]
        ps_fc, ps_lin = ps[4:6], ps[6:8]
        ps_out = ps[4:6]
        es = [sb(f"e1_es{b}", [P, TPG, 64]) for b in range(GB)]
        rows = [sb(f"e1_rows{b}", [P, TPG, P], I32) for b in range(GB)]
        x1r = [sb(f"e1_x1r{b}", [P, TPG, X1W]) for b in range(GB)]
        stat = sb("e1_stat", [P, TPG, 6])
        mv = [sb(f"e1_mv{b}", [P, TPG, 2]) for b in range(GB)]
        std = [sb(f"e1_std{b}", [P, TPG]) for b in range(GB)]
        rstd = [sb(f"e1_rstd{b}", [P, TPG]) for b in range(GB)]
        shift = [sb(f"e1_shift{b}", [P, TPG]) for b in range(GB)]
        h1 = [sb(f"e1_h1{b}", [P, TPG, D]) for b in range(GB)]
        esT = sb("e1_esT", [64, TPG * P])
        sig = sb("e1_sig", [64, TPG * P])
        hid = sb("e1_hid", [64, TPG * P])
        hT_s = sb("e1_hT_s", [S0, TPG * P])
        hT_v = sb("e1_hT_v", [VD, TPG * P])
        fc = [sb(f"e1_fc{b}", [P, TPG, 224]) for b in range(GB)]
        hs = [sb(f"e1_hs{b}", [P, TPG, S0]) for b in range(GB)]
        hv = [sb(f"e1_hv{b}", [P, TPG, 5, V0]) for b in range(GB)]
        ea = [sb(f"e1_ea{b}", [P, TPG, 6]) for b in range(GB)]
        ws = sb("e1_ws", [P, TPG, 2, 64])
        w3e = sb("e1_w3e", [P, TPG, V0])
        dots = sb("e1_dots", [P, TPG, 3, V0])
        dot = sb("e1_dot", [P, TPG, V0])
        cr1 = sb("e1_cr1", [P, TPG, 3, V0])
        cr2 = sb("e1_cr2", [P, TPG, 3, V0])
        mid_s = sb("e1_mid_s", [P, TPG, 96])
        mid_v = sb("e1_mid_v", [P, TPG, 3, 128])
        same = [sb(f"e1_same{b}", [P, TPG, P]) for b in range(GB)]
        mT_s = sb("e1_mT_s", [96, TPG * P])
        mT_v = sb("e1_mT_v", [128, 3, TPG * P])
        total = [sb(f"e1_total{b}", [P, TPG, AGW]) for b in range(GB)]

        starts = [sb(f"e1_starts{b}", [P, TPG], I32) for b in range(GB)]
        put = [sb(f"e1_put{b}", [P, TPG], I32) for b in range(GB)]
        es_loaded = [sem(f"e1_es_loaded{b}") for b in range(GB)]
        rows_loaded = [sem(f"e1_rows_loaded{b}") for b in range(GB)]
        gathered = [sem(f"e1_gathered{b}") for b in range(GB)]
        (starts_copied, put_copied, stats_done, var_done, std_done, rstd_done, shift_done, h1_done, ea_done, same_made,
         es_turned, es_copied, h1_turned, h1_copied, hid_made, sig_done, silu_done, fc_made, fc_copied, lin_made,
         lin_copied, mid_step, mid_done, sums_turned, sums_copied, out_made, total_copied, added) = (
            sem("e1_" + n) for n in (
                "starts_copied", "put_copied", "stats_done", "var_done", "std_done", "rstd_done", "shift_done",
                "h1_done", "ea_done", "same_made", "es_turned", "es_copied", "h1_turned", "h1_copied", "hid_made",
                "sig_done", "silu_done", "fc_made", "fc_copied", "lin_made", "lin_copied", "mid_step", "mid_done",
                "sums_turned", "sums_copied", "out_made", "total_copied", "added"))
        MID = 12

        with nc.Block() as block:
            @block.sync
            def _(sp):
                def load(turn, b):
                    g = GB * turn + b
                    if reused(turn):
                        sp.wait_ge(es_turned, g - GB + 1)
                        sp.wait_ge(same_made, g - GB + 1)
                    sp.dma_start(es[b][:, :, :].rearrange("p t c -> p (t c)"),
                                 es_v[:, bass.ds(g * (TPG * 64), TPG * 64)]).then_inc(es_loaded[b], 16)
                    sp.dma_start(rows[b][:, :, :].rearrange("p t q -> p (t q)"),
                                 W["dst_rows"][bass.ds(g * (TPG * P), TPG * P)].partition_broadcast(P)).then_inc(rows_loaded[b], 16)

                in_turns(sp, NGR, GB, (load, 5))

            @block.gpsimd
            def _(pool):
                def gather(turn, b, j):
                    g = GB * turn + b
                    if j == 0:
                        if reused(turn):
                            pool.wait_ge(h1_done, g - GB + 1)
                            pool.wait_ge(ea_done, g - GB + 1)
                        waits_alone(pool, T)
                        nc.gpsimd.tensor_copy(starts[b][:, :], T["idx"][:, 0, bass.ds(g * TPG, TPG)]).then_inc(starts_copied, 1)
                        pool.wait_ge(starts_copied, g + 1)
                        waits_alone(pool, T)
                    pool.indirect_dma_start(x1r[b][:, j, :], None, DR["x1"],
                                            bass.IndirectOffsetOnAxis(starts[b][:, j:j + 1], 0)).then_inc(gathered[b], 16)

                def scatter(turn, b, j):
                    g = GB * turn + b
                    if j == 0:
                        nc.gpsimd.tensor_copy(put[b][:, :], T["put"][:, 1, bass.ds(g * TPG, TPG)]).then_inc(put_copied, 1)
                        pool.wait_ge(put_copied, g + 1)
                        pool.wait_ge(total_copied, g + 1)
                    pool.wait_ge(added, 16 * (g * TPG + j))
                    waits_alone(pool, T)
                    pool.indirect_dma_start(DR["agg"],
                                            bass.IndirectOffsetOnAxis(put[b][:, j:j + 1], 0),
                                            total[b][:, j, :], None, compute_op=ALU.add).then_inc(added, 16)

                in_turns(pool, NGR, GB, *(part for j in range(TPG) for part in (
                    (lambda turn, b, j=j: scatter(turn, b, j), -2),
                    (lambda turn, b, j=j: gather(turn, b, j), 5))))
                pool.wait_ge(added, 16 * NT)

            @block.vector
            def _(dve):
                def stats(turn, b):
                    g = GB * turn + b
                    dve.wait_ge(gathered[b], 16 * TPG * (turn + 1))
                    for j in range(TPG):
                        ins = nc.vector.bn_stats(stat[:, j, :], x1r[b][:, j, 0:D])
                    ins.then_inc(stats_done, 1)
                    dve.wait_ge(stats_done, g + 1)
                    waits_alone(dve, T)
                    for j in range(TPG):
                        ins = nc.vector.bn_aggr(mv[b][:, j, :], stat[:, j, :])
                    ins.then_inc(var_done, 1)

                def scales(turn, b):
                    g = GB * turn + b
                    dve.wait_ge(std_done, g + 1)
                    nc.vector.reciprocal(rstd[b][:, :], std[b][:, :]).then_inc(rstd_done, 1)
                    dve.wait_ge(rstd_done, g + 1)
                    nc.vector.scalar_tensor_tensor(shift[b][:, :], mv[b][:, :, 0], -1.0, rstd[b][:, :], ALU.mult,
                                                   ALU.mult).then_inc(shift_done, 1)

                def attributes(turn, b):
                    g = GB * turn + b
                    att = T["ea"][:, bass.ds(g * TPG, TPG), :]
                    a = x1r[b][:, :, D:D + 1]
                    nc.vector.tensor_tensor(ea[b][:, :, 0:4], att, a.broadcast_to([P, TPG, 4]), ALU.mult)
                    nc.vector.tensor_tensor(ea[b][:, :, 4:6], att[:, :, 1:3], a.broadcast_to([P, TPG, 2]),
                                            ALU.mult).then_inc(ea_done, 1)

                def compare(turn, b):
                    g = GB * turn + b
                    dve.wait_ge(rows_loaded[b], 16 * (turn + 1))
                    if reused(turn):
                        dve.wait_ge(sums_turned, g - GB + 1)
                    mine = T["idx"][:, 1, bass.ds(g * TPG, TPG)]
                    nc.vector.tensor_tensor(same[b][:, :, :], rows[b][:, :, :], bcast(mine, 2, P),
                                            ALU.is_equal).then_inc(same_made, 1)

                def silu(turn, b):
                    g = GB * turn + b
                    dve.wait_ge(sig_done, g + 1)
                    dve.wait_ge(fc_made, g)
                    nc.vector.tensor_tensor(hid[:, :], ps_hid[0:64, 0:TPG * P], sig[:, :], ALU.mult).then_inc(silu_done, 1)

                def messages(turn, b):
                    g = GB * turn + b
                    e0 = ea[b][:, :, 0:1]
                    e1 = ea[b][:, :, 1:4]
                    f = fc[b]
                    v = hv[b]
                    dve.wait_ge(fc_copied, g + 1)
                    dve.wait_ge(lin_copied, g + 1)
                    dve.wait_ge(ea_done, g + 1)
                    dve.wait_ge(sums_turned, g)
                    tt = nc.vector.tensor_tensor
                    tt(ws[:, :, :, :], f[:, :, 0:128].rearrange("p t (k c) -> p t k c", k=2),
                       bcast(hs[b][:, :, :], 2, 2), ALU.mult).then_inc(mid_step, 1)
                    tt(w3e[:, :, :], f[:, :, 128:160], e0.broadcast_to([P, TPG, V0]), ALU.mult).then_inc(mid_step, 1)
                    tt(dots[:, :, :, :], v[:, :, 0:3, :], bcast(e1, 3, V0), ALU.mult).then_inc(mid_step, 1)
                    tt(cr1[:, :, :, :], v[:, :, 1:4, :], bcast(ea[b][:, :, 3:6], 3, V0), ALU.mult).then_inc(mid_step, 1)
                    tt(cr2[:, :, :, :], v[:, :, 2:5, :], bcast(ea[b][:, :, 2:5], 3, V0), ALU.mult).then_inc(mid_step, 1)
                    dve.wait_ge(mid_step, MID * g + 1)
                    tt(mid_s[:, :, 0:64], ws[:, :, 0, :], e0.broadcast_to([P, TPG, 64]), ALU.mult).then_inc(mid_step, 1)
                    tt(mid_v[:, :, :, 0:64], bcast(ws[:, :, 1, :], 2, 3), bcast(e1, 3, 64), ALU.mult).then_inc(mid_step, 1)
                    dve.wait_ge(mid_step, MID * g + 5)
                    tt(mid_v[:, :, :, 64:96], v[:, :, 0:3, :], bcast(w3e[:, :, :], 2, 3), ALU.mult).then_inc(mid_step, 1)
                    tt(dot[:, :, :], dots[:, :, 0, :], dots[:, :, 1, :], ALU.add).then_inc(mid_step, 1)
                    tt(cr1[:, :, :, :], cr1[:, :, :, :], cr2[:, :, :, :], ALU.subtract).then_inc(mid_step, 1)
                    dve.wait_ge(mid_step, MID * g + 9)
                    tt(dot[:, :, :], dot[:, :, :], dots[:, :, 2, :], ALU.add).then_inc(mid_step, 1)
                    dve.wait_ge(mid_step, MID * g + 11)
                    tt(mid_v[:, :, :, 96:128], cr1[:, :, :, :], bcast(f[:, :, 192:224], 2, 3), ALU.mult).then_inc(mid_step, 1)
                    tt(mid_s[:, :, 64:96], dot[:, :, :], f[:, :, 160:192], ALU.mult).then_inc(mid_done, 1)

                in_turns(dve, NGR, GB, (scales, 3), (attributes, 3), (stats, 4), (compare, 1), (messages, 0), (silu, 2))

            @block.scalar
            def _(act):
                def root(turn, b):
                    g = GB * turn + b
                    act.wait_ge(var_done, g + 1)
                    if reused(turn):
                        act.wait_ge(rstd_done, g - GB + 1)
                    nc.scalar.activation(std[b][:, :], mv[b][:, :, 1], ACT.Sqrt, bias=T["eps"][:, 0:1]).then_inc(std_done, 1)

                def relu(turn, b):
                    g = GB * turn + b
                    act.wait_ge(shift_done, g + 1)
                    if reused(turn):
                        act.wait_ge(h1_turned, g - GB + 1)
                    for j in range(TPG):
                        ins = nc.scalar.activation(h1[b][:, j, :], x1r[b][:, j, 0:D], ACT.Relu,
                                                   bias=shift[b][:, j:j + 1], scale=rstd[b][:, j:j + 1])
                    ins.then_inc(h1_done, 1)

                def copy_es(turn, b):
                    g = GB * turn + b
                    act.wait_ge(es_turned, g + 1)
                    act.wait_ge(hid_made, g)
                    nc.scalar.copy(esT[:, :], ps_esT[0:64, 0:TPG * P]).then_inc(es_copied, 1)

                def sigmoid(turn, b):
                    g = GB * turn + b
                    act.wait_ge(hid_made, g + 1)
                    act.wait_ge(silu_done, g)
                    nc.scalar.activation(sig[:, :], ps_hid[0:64, 0:TPG * P], ACT.Sigmoid).then_inc(sig_done, 1)

                def copy_h1(turn, b):
                    g = GB * turn + b
                    act.wait_ge(h1_turned, g + 1)
                    act.wait_ge(lin_made, g)
                    nc.scalar.copy(hT_s[:, :], ps_hT_s[0:S0, 0:TPG * P])
                    nc.scalar.copy(hT_v[:, :], ps_hT_v[0:VD, 0:TPG * P]).then_inc(h1_copied, 1)

                def copy_products(turn, b):
                    g = GB * turn + b
                    if reused(turn):
                        act.wait_ge(mid_done, g - GB + 1)
                    act.wait_ge(fc_made, g + 1)
                    for k in range(2):
                        ins = nc.scalar.copy(fc[b][:, 2 * k:2 * k + 2, :],
                                             ps_fc[k][0:P, 0:448].rearrange("p (t c) -> p t c", t=2))
                    ins.then_inc(fc_copied, 1)
                    act.wait_ge(lin_made, g + 1)
                    for k in range(2):
                        o = ps_lin[k][0:P, 0:2 * D].rearrange("p (t c) -> p t c", t=2)
                        t2 = slice(2 * k, 2 * k + 2)
                        nc.scalar.copy(hs[b][:, t2, :], o[:, :, 0:S0])
                        nc.scalar.copy(hv[b][:, t2, 0:3, :], o[:, :, S0:D].rearrange("p t (i c) -> p t i c", i=3))
                        ins = nc.scalar.copy(hv[b][:, t2, 3:5, :],
                                             o[:, :, S0:S0 + 64].rearrange("p t (i c) -> p t i c", i=2))
                    ins.then_inc(lin_copied, 1)

                def copy_sums(turn, b):
                    g = GB * turn + b
                    act.wait_ge(sums_turned, g + 1)
                    act.wait_ge(out_made, g)
                    nc.scalar.copy(mT_s[:, :], ps_mid_s[0:96, 0:TPG * P])
                    for i in range(3):
                        ins = nc.scalar.copy(mT_v[:, i, :], ps_mid_v[i][:, 0:TPG * P])
                    ins.then_inc(sums_copied, 1)

                def copy_total(turn, b):
                    g = GB * turn + b
                    act.wait_ge(out_made, g + 1)
                    if reused(turn):
                        act.wait_ge(added, 16 * TPG * (g - GB + 1))
                    for k in range(2):
                        ins = nc.scalar.copy(total[b][:, 2 * k:2 * k + 2, :],
                                             ps_out[k][0:P, 0:2 * AGW].rearrange("p (t c) -> p t c", t=2))
                    ins.then_inc(total_copied, 1)

                in_turns(act, NGR, GB, (copy_sums, -1), (copy_products, 1), (copy_es, 3), (sigmoid, 2), (copy_h1, 2),
                         (copy_total, -1), (relu, 3), (root, 4))

            @block.tensor
            def _(pe):
                eye = T["ident"][0:P, 0:P]

                def turn_es(turn, b):
                    g = GB * turn + b
                    pe.wait_ge(es_loaded[b], 16 * (turn + 1))
                    wait_for(pe, sums_copied, g - 3, NGR)
                    pe.wait_ge(es_copied, g)
                    waits_alone(pe, T)
                    for j in range(TPG):
                        ins = nc.tensor.transpose(ps_esT[0:64, j * P:(j + 1) * P], es[b][:, j, :], eye)
                    ins.then_inc(es_turned, 1)

                def hidden(turn, b):
                    g = GB * turn + b
                    pe.wait_ge(es_copied, g + 1)
                    wait_for(pe, sums_copied, g - 2, NGR)
                    pe.wait_ge(silu_done, g)
                    waits_alone(pe, T)
                    nc.tensor.matmul(ps_hid[0:64, 0:TPG * P], T["w_fc1"][:, :], esT[:, :], start=True,
                                     stop=True).then_inc(hid_made, 1)

                def turn_h1(turn, b):
                    g = GB * turn + b
                    pe.wait_ge(h1_done, g + 1)
                    wait_for(pe, sums_copied, g - 2, NGR)
                    pe.wait_ge(h1_copied, g)
                    for j in range(TPG):
                        nc.tensor.transpose(ps_hT_v[0:VD, j * P:(j + 1) * P], h1[b][:, j, S0:D], eye)
                        ins = nc.tensor.transpose(ps_hT_s[0:S0, j * P:(j + 1) * P], h1[b][:, j, 0:S0], eye)
                    ins.then_inc(h1_turned, 1)

                def products(turn, b):
                    g = GB * turn + b
                    pe.wait_ge(silu_done, g + 1)
                    wait_for(pe, total_copied, g - 2, NGR)
                    for j in range(TPG):
                        ins = nc.tensor.matmul(ps_fc[j // 2][0:P, j % 2 * 224:j % 2 * 224 + 224], hid[:, j * P:(j + 1) * P],
                                               T["w_fc2"][:, :], start=True, stop=True)
                    ins.then_inc(fc_made, 1)
                    pe.wait_ge(h1_copied, g + 1)
                    pe.wait_ge(lin_copied, g)
                    for j in range(TPG):
                        o, at = ps_lin[j // 2], j % 2 * D
                        nc.tensor.matmul(o[0:P, at:at + S0], hT_s[:, j * P:(j + 1) * P], T["w_in_s"][:, :],
                                         start=True, stop=True)
                        ins = nc.tensor.matmul(o[0:P, at + S0:at + D], hT_v[:, j * P:(j + 1) * P], T["w_in_v"][:, :],
                                               start=True, stop=True)
                    ins.then_inc(lin_made, 1)

                def turn_sums(turn, b):
                    g = GB * turn + b
                    pe.wait_ge(mid_done, g + 1)
                    pe.wait_ge(same_made, g + 1)
                    wait_for(pe, es_copied, g + 4, NGR)
                    wait_for(pe, silu_done, g + 3, NGR)
                    wait_for(pe, h1_copied, g + 3, NGR)
                    pe.wait_ge(sums_copied, g)
                    for j in range(TPG):
                        nc.tensor.matmul(ps_mid_s[0:96, j * P:(j + 1) * P], mid_s[:, j, :], same[b][:, j, :],
                                         start=True, stop=True)
                        for i in range(3):
                            ins = nc.tensor.matmul(ps_mid_v[i][:, j * P:(j + 1) * P], mid_v[:, j, i, :],
                                                   same[b][:, j, :], start=True, stop=True)
                    ins.then_inc(sums_turned, 1)

                def lin2(turn, b):
                    g = GB * turn + b
                    pe.wait_ge(sums_copied, g + 1)
                    wait_for(pe, fc_copied, g + 3, NGR)
                    pe.wait_ge(total_copied, g)
                    for j in range(TPG):
                        o, at = ps_out[j // 2], j % 2 * AGW
                        nc.tensor.matmul(o[0:P, at:at + 96], mT_s[:, j * P:(j + 1) * P], T["w_out_s"][:, :],
                                         start=True, stop=True)
                        for i in range(3):
                            ins = nc.tensor.matmul(o[0:P, at + 96 + 32 * i:at + 128 + 32 * i],
                                                   mT_v[:, i, j * P:(j + 1) * P], T["w_out_v"][:, :], start=True, stop=True)
                    ins.then_inc(out_made, 1)

                in_turns(pe, NGR, GB, (turn_sums, -1), (products, 1), (turn_es, 3), (hidden, 2), (turn_h1, 2), (lin2, -1))


def stage_nodes1(nc, T, W, sem, N, DR, out):
    NPP = N // P
    NCH = NPP // RPC
    DVE_ROWS = 4
    x1_v = DR["x1"][0:N, :].rearrange("(p n) d -> p (n d)", p=P)
    ag_v = DR["agg"][0:N, :].rearrange("(p n) d -> p (n d)", p=P)
    out_v = out.rearrange("(p n) d -> p (n d)", p=P)

    with ExitStack() as ctx:
        def sb(name, shape, dt=F32):
            return ctx.enter_context(nc.sbuf_tensor(name, shape, dt))

        def pb(name):
            return ctx.enter_context(nc.psum_tensor(name, [128, 512], F32))

        xt = [sb(f"n1_x{b}", [P, RPC, X1W]) for b in range(CB)]
        pre = [sb(f"n1_pre{b}", [P, RPC, AGW]) for b in range(CB)]
        ht = [sb(f"n1_h{b}", [P, RPC, D]) for b in range(CB)]
        gate = sb("n1_gate", [P, RPC, 96])
        stat = sb("n1_stat", [P, RPC, 6])
        mv = [sb(f"n1_mv{b}", [P, RPC, 2]) for b in range(CB)]
        std = [sb(f"n1_std{b}", [P, RPC]) for b in range(CB)]
        rstd = [sb(f"n1_rstd{b}", [P, RPC]) for b in range(CB)]
        shift = [sb(f"n1_shift{b}", [P, RPC]) for b in range(CB)]
        hT_s = [sb(f"n1_hTs{h}", [S0, 4 * P]) for h in range(2)]
        hT_v = [sb(f"n1_hTv{h}", [VD, 4 * P]) for h in range(2)]
        ps_s = [pb(f"n1_ps_s{h}") for h in range(2)]
        ps_v = [pb(f"n1_ps_v{h}") for h in range(2)]
        ps_o = [pb(f"n1_ps_o{q}") for q in range(4)]

        x_loaded = [sem(f"n1_x_loaded{b}") for b in range(CB)]
        agg_loaded = [sem(f"n1_agg_loaded{b}") for b in range(CB)]
        stored = [sem(f"n1_stored{b}") for b in range(CB)]
        (stats_done, var_done, std_done, rstd_done, shift_done, h_done, hT_made, hT_copied, sc_made, pre_added,
         pre_scaled, gate_done, gated, summed, normalised) = (sem("n1_" + n) for n in (
             "stats_done", "var_done", "std_done", "rstd_done", "shift_done", "h_done", "hT_made", "hT_copied",
             "sc_made", "pre_added", "pre_scaled", "gate_done", "gated", "summed", "normalised"))

        with nc.Block() as block:
            @block.sync
            def _(sp):
                def load(turn, b):
                    c = CB * turn + b
                    if reused(turn):
                        sp.wait_ge(summed, c - CB + 1)
                    sp.dma_start(xt[b][:, :, :].rearrange("p r d -> p (r d)"),
                                 x1_v[:, bass.ds(c * (RPC * X1W), RPC * X1W)]).then_inc(x_loaded[b], 16)
                    sp.dma_start(pre[b][:, :, :].rearrange("p r d -> p (r d)"),
                                 ag_v[:, bass.ds(c * (RPC * AGW), RPC * AGW)]).then_inc(agg_loaded[b], 16)

                def store(turn, b):
                    c = CB * turn + b
                    sp.wait_ge(summed, c + 1)
                    sp.dma_start(out_v[:, bass.ds(c * (RPC * D), RPC * D)],
                                 ht[b][:, :, :].rearrange("p r d -> p (r d)")).then_inc(stored[b], 16)

                in_turns(sp, NCH, CB, (store, -1), (load, 5))
                for b in range(CB):
                    sp.wait_ge(stored[b], 16 * chunks_in(b, NCH))

            @block.vector
            def _(dve):
                def stats(turn, b):
                    c = CB * turn + b
                    dve.wait_ge(x_loaded[b], 16 * (turn + 1))
                    for r in range(RPC):
                        ins = nc.vector.bn_stats(stat[:, r, :], xt[b][:, r, 0:D])
                    ins.then_inc(stats_done, 1)
                    dve.wait_ge(stats_done, c + 1)
                    waits_alone(dve, T)
                    for r in range(RPC):
                        ins = nc.vector.bn_aggr(mv[b][:, r, :], stat[:, r, :])
                    ins.then_inc(var_done, 1)

                def scales(turn, b):
                    c = CB * turn + b
                    dve.wait_ge(std_done, c + 1)
                    nc.vector.reciprocal(rstd[b][:, :], std[b][:, :]).then_inc(rstd_done, 1)
                    dve.wait_ge(rstd_done, c + 1)
                    nc.vector.scalar_tensor_tensor(shift[b][:, :], mv[b][:, :, 0], -1.0, rstd[b][:, :], ALU.mult,
                                                   ALU.mult).then_inc(shift_done, 1)

                def normalise(turn, b):
                    c = CB * turn + b
                    dve.wait_ge(shift_done, c + 1)
                    dve.wait_ge(stored[b], 16 * turn)
                    for r in range(DVE_ROWS):
                        ins = nc.vector.tensor_scalar(ht[b][:, r, :], xt[b][:, r, 0:D], rstd[b][:, r:r + 1],
                                                      shift[b][:, r:r + 1], ALU.mult, ALU.add)
                    ins.then_inc(normalised, 1)

                def add(turn, b):
                    c = CB * turn + b
                    dve.wait_ge(agg_loaded[b], 16 * (turn + 1))
                    for q in range(4):
                        dve.wait_ge(sc_made, 4 * c + q + 1)
                        r = slice(2 * q, 2 * q + 2)
                        nc.vector.tensor_tensor(pre[b][:, r, :], pre[b][:, r, :],
                                                ps_o[q][0:P, 0:2 * AGW].rearrange("p (r d) -> p r d", r=2),
                                                ALU.add).then_inc(pre_added, 1)

                def apply_gate(turn, b):
                    c = CB * turn + b
                    dve.wait_ge(gate_done, c + 1)
                    nc.vector.tensor_tensor(ht[b][:, :, 0:64], pre[b][:, :, 0:64], gate[:, :, 0:64], ALU.mult)
                    nc.vector.tensor_tensor(ht[b][:, :, 64:160].rearrange("p r (w i) -> p r w i", i=3),
                                            pre[b][:, :, 96:192].rearrange("p r (i w) -> p r w i", i=3),
                                            bcast(gate[:, :, 64:96], 3, 3), ALU.mult).then_inc(gated, 1)

                in_turns(dve, NCH, CB, (scales, 2), (normalise, 2), (stats, 3), (apply_gate, -1),
                         (add, 0))

            @block.gpsimd
            def _(pool):
                def scale(turn, b):
                    c = CB * turn + b
                    pool.wait_ge(pre_added, 4 * (c + 1))
                    nc.gpsimd.tensor_tensor(pre[b][:, :, :], pre[b][:, :, :],
                                            xt[b][:, :, D:D + 1].broadcast_to([P, RPC, AGW]), ALU.mult).then_inc(pre_scaled, 1)

                def residual(turn, b):
                    c = CB * turn + b
                    pool.wait_ge(gated, c + 1)
                    nc.gpsimd.tensor_tensor(ht[b][:, :, :], ht[b][:, :, :], xt[b][:, :, 0:D],
                                            ALU.add).then_inc(summed, 1)

                in_turns(pool, NCH, CB, (residual, -1), (scale, 0))

            @block.scalar
            def _(act):
                def root(turn, b):
                    c = CB * turn + b
                    act.wait_ge(var_done, c + 1)
                    if reused(turn):
                        act.wait_ge(rstd_done, c - CB + 1)
                    nc.scalar.activation(std[b][:, :], mv[b][:, :, 1], ACT.Sqrt, bias=T["eps"][:, 0:1]).then_inc(std_done, 1)

                def relu(turn, b):
                    c = CB * turn + b
                    act.wait_ge(shift_done, c + 1)
                    act.wait_ge(stored[b], 16 * turn)
                    for r in range(DVE_ROWS, RPC):
                        ins = nc.scalar.activation(ht[b][:, r, :], xt[b][:, r, 0:D], ACT.Relu,
                                                   bias=shift[b][:, r:r + 1], scale=rstd[b][:, r:r + 1])
                    ins.then_inc(h_done, 1)

                def copy(turn, b):
                    c = CB * turn + b
                    for h in range(2):
                        act.wait_ge(hT_made, 2 * c + h + 1)
                        act.wait_ge(sc_made, 4 * c)
                        nc.scalar.activation(hT_s[h][:, :], ps_s[h][0:S0, 0:4 * P], ACT.Relu)
                        nc.scalar.activation(hT_v[h][:, :], ps_v[h][0:VD, 0:4 * P], ACT.Relu).then_inc(hT_copied, 1)

                def sigmoid(turn, b):
                    c = CB * turn + b
                    act.wait_ge(pre_scaled, c + 1)
                    act.wait_ge(gated, c)
                    nc.scalar.activation(gate[:, :, :], pre[b][:, :, 0:96], ACT.Sigmoid).then_inc(gate_done, 1)

                in_turns(act, NCH, CB, (copy, 0), (sigmoid, -1), (relu, 2), (root, 3))

            @block.tensor
            def _(pe):
                def turn_h(turn, b):
                    c = CB * turn + b
                    pe.wait_ge(h_done, c + 1)
                    pe.wait_ge(normalised, c + 1)
                    for h in range(2):
                        pe.wait_ge(hT_copied, 2 * c)
                        for r in range(4):
                            nc.tensor.transpose(ps_v[h][0:VD, r * P:(r + 1) * P], ht[b][:, 4 * h + r, S0:D],
                                                T["ident"][0:P, 0:P])
                            ins = nc.tensor.transpose(ps_s[h][0:S0, r * P:(r + 1) * P], ht[b][:, 4 * h + r, 0:S0],
                                                      T["ident"][0:P, 0:P])
                        ins.then_inc(hT_made, 1)

                def contract(turn, b):
                    c = CB * turn + b
                    for q in range(4):
                        pe.wait_ge(hT_copied, 2 * c + q // 2 + 1)
                        pe.wait_ge(pre_added, 4 * c)
                        for r in range(2):
                            m = (2 * q + r) % 4 * P
                            nc.tensor.matmul(ps_o[q][0:P, r * AGW:r * AGW + 96], hT_s[q // 2][:, m:m + P],
                                             T["w_sc_s"][:, :], start=True, stop=True)
                            ins = nc.tensor.matmul(ps_o[q][0:P, r * AGW + 96:(r + 1) * AGW], hT_v[q // 2][:, m:m + P],
                                                   T["w_sc_v"][:, :], start=True, stop=True)
                        ins.then_inc(sc_made, 1)

                in_turns(pe, NCH, CB, (contract, 0), (turn_h, 1))


def gnn_kernel(nc, W, out):
    N, E = W["x"].shape[0], W["src"].shape[0]
    NT = E // P
    DR = {"h0": nc.dram_tensor("h0", [N, D], F32).ap(),
          "x1": nc.dram_tensor("x1", [N + P, X1W], F32).ap(),
          "agg": nc.dram_tensor("agg", [N + P, AGW], F32).ap()}
    shapes = {
        "ident": [128, 128], "halves": [128, S0], "earlier": [P, P], "spare": [P, 1], "eps": [P, 1], "a_all": [P, N // P],
        "ea": [P, NT, 4], "w_pair": [128, 40, 64], "w_vec": [128, V0, V0], "w_msg_s": [S0, 160],
        "w_msg_v": [VD, 2 * VD + 3 * S0], "w_lin_s": [S0, S0], "w_lin_v": [VD, VD], "eye_v": [VD, VD],
        "w_in_s": [S0, S0], "w_in_v": [VD, VD], "w_fc1": [64, 64], "w_fc2": [64, 224], "w_sc_s": [S0, 96],
        "w_sc_v": [VD, VD], "w_out_s": [96, 96], "w_out_v": [128, 32],
    }
    with ExitStack() as ctx:
        def sem(name):
            return ctx.enter_context(nc.semaphore(name))

        T = {"passed": sem("passed")}
        T |= {n: ctx.enter_context(nc.sbuf_tensor("t_" + n, s, F32)) for n, s in shapes.items()}
        T["idx"] = ctx.enter_context(nc.sbuf_tensor("t_idx", [P, 2, NT], I32))
        T["put"] = ctx.enter_context(nc.sbuf_tensor("t_put", [P, 2, NT], I32))
        stage_weights(nc, T, W, sem)
        stage_nodes0(nc, T, W, sem, N, NT, DR)
        stage_edges0(nc, T, W, sem, N, NT, DR)
        stage_edges1(nc, T, W, sem, NT, DR)
        stage_nodes1(nc, T, W, sem, N, DR, out)


def kernel(**inputs):
    import numpy as np
    import concourse.bacc as bacc
    from concourse.bass_utils import run_bass_kernel_spmd

    nc = bacc.Bacc("TRN2", target_bir_lowering=False, num_devices=1)
    a = {n.removeprefix("L0_gnn_").removeprefix("L1_gnn_"): np.asarray(v) for n, v in inputs.items()}
    N, E = a["x"].shape[0], a["src"].shape[0]
    a["Wu_sv"] = a["Wu_sv"].transpose(0, 2, 1)
    a["Wu_vs"] = a["Wu_vs"].transpose(1, 2, 0)
    a["src_rows"] = a["src"].reshape(P, E // P).T.reshape(-1)
    a["dst_rows"] = a["dst"].reshape(P, E // P).T.reshape(-1)
    a["ident"] = np.eye(128, dtype=np.float32)
    a["earlier"] = np.tril(np.ones((P, P), np.float32), -1)
    a["spare_x"] = (N + np.arange(P, dtype=np.float32)).reshape(P, 1)
    arrays, W = {}, {}
    for name, v in a.items():
        v = np.ascontiguousarray(v)
        arrays[f"in_{name}"] = v
        W[name] = nc.dram_tensor(f"in_{name}", v.shape, mybir.dt.from_np(v.dtype), kind="ExternalInput").ap()
    out = nc.dram_tensor("out", (N, D), F32, kind="ExternalOutput").ap()
    gnn_kernel(nc, W, out)
    r = run_bass_kernel_spmd(nc, [arrays], core_ids=[0])
    return r.results[0]["out"]
```
